# Optimizing a Trainium2 kernel written in Bass

```python
import numpy as np
import jax
import jax.numpy as jnp

def _softmax(x, axis=-1):
    return jax.nn.softmax(x, axis=axis)

def _gelu(x):
    return jax.nn.gelu(x, approximate=True)

def _silu(x):
    return jax.nn.silu(x)

def _sigmoid(x):
    return jax.nn.sigmoid(x)

def _layernorm(x, axis=-1, eps=1e-05):
    m = jnp.mean(x, axis=axis, keepdims=True)
    v = jnp.var(x, axis=axis, keepdims=True)
    return (x - m) / jnp.sqrt(v + eps)

def _scatter_add(tgt, idx, src, axis=0):
    return tgt.at[idx].add(src)

def _segment_sum(src, seg, n):
    return jax.ops.segment_sum(src, seg, n)
kernel_name = 'mk_audio_tower_d1_tok_aud1d768_r4_af593a'

def setup_inputs(seed: int=0):
    np.random.seed(seed)
    _w = jnp.asarray

    def _rec_inputs():
        import jax
        import jax.numpy as jnp
        _rk = jax.random.key(seed)
        x = 8.9527e-05 + 1.00009 * jax.random.normal(jax.random.fold_in(_rk, 1), (4, 120000), jnp.float32)
        return x
    x = _rec_inputs()

    def _L0_tok_setup():
        import jax, jax.numpy as jnp
        import numpy as np
        from jax import lax
        CONV_LAYERS = [(128, 10, 5), (128, 3, 2), (128, 3, 2), (128, 3, 2), (128, 3, 2), (128, 2, 2)]
        NUM_GROUPS = 32
        EPS = 1e-05
        EMBED_DIM = 192

        def _block(x, cw, cb, gw, gb, stride):
            y = lax.conv_general_dilated(x, cw, (stride,), 'VALID', dimension_numbers=('NCH', 'OIH', 'NCH'))
            y = y + cb[None, :, None]
            B, C, T = y.shape
            yg = y.reshape(B, NUM_GROUPS, C // NUM_GROUPS * T)
            mu = yg.mean(axis=-1, keepdims=True)
            var = yg.var(axis=-1, keepdims=True)
            yn = ((yg - mu) * lax.rsqrt(var + EPS)).reshape(B, C, T)
            yn = yn * gw[None, :, None] + gb[None, :, None]
            return jax.nn.gelu(yn)

        def _forward(x, conv_params, pw, pb):
            h = x[:, None, :]
            for (cw, cb, gw, gb), (_, _, s) in zip(conv_params, CONV_LAYERS):
                h = _block(h, cw, cb, gw, gb, s)
            h = jnp.transpose(h, (0, 2, 1))
            return jnp.einsum('bfc,ec->bfe', h, pw) + pb
        key = jax.random.key(seed)
        ks = jax.random.split(key, 16)
        inp = {'x': jax.random.normal(ks[0], (2, 80000), dtype=jnp.float32)}
        in_c = 1
        for li, (oc, k, s) in enumerate(CONV_LAYERS):
            lim = 1.0 / np.sqrt(in_c * k)
            inp[f'cw{li}'] = jax.random.uniform(jax.random.fold_in(ks[1], li), (oc, in_c, k), jnp.float32, -lim, lim)
            inp[f'cb{li}'] = jax.random.uniform(jax.random.fold_in(ks[2], li), (oc,), jnp.float32, -lim, lim)
            inp[f'gw{li}'] = jnp.ones((oc,), jnp.float32)
            inp[f'gb{li}'] = jnp.zeros((oc,), jnp.float32)
            in_c = oc
        lim = 1.0 / np.sqrt(128)
        inp['pw'] = jax.random.uniform(ks[3], (EMBED_DIM, 128), jnp.float32, -lim, lim)
        inp['pb'] = jax.random.uniform(ks[4], (EMBED_DIM,), jnp.float32, -lim, lim)
        return inp
    _L0_tok_all = _L0_tok_setup()
    _L0_tok_in = {k: v for k, v in _L0_tok_all.items() if k in ('cw0', 'cb0', 'gw0', 'gb0', 'cw1', 'cb1', 'gw1', 'gb1', 'cw2', 'cb2', 'gw2', 'gb2', 'cw3', 'cb3', 'gw3', 'gb3', 'cw4', 'cb4', 'gw4', 'gb4', 'cw5', 'cb5', 'gw5', 'gb5', 'pw', 'pb')}
    del _L0_tok_all

    def _L0_attn_setup():
        import jax, jax.numpy as jnp
        import numpy as np
        D_HEAD = 64
        IGNORE = -100000.0
        key = jax.random.key(seed)
        ks = jax.random.split(key, 5)
        B, S, D, H, M = (2, 512, 192, 12, D_HEAD)
        scale = 0.05
        return {'x': jax.random.normal(ks[0], (B, S, D), jnp.float32), 'W_Q': jax.random.normal(ks[1], (H, D, M), jnp.float32) * scale, 'b_Q': jnp.zeros((H, M), jnp.float32), 'W_K': jax.random.normal(ks[2], (H, D, M), jnp.float32) * scale, 'b_K': jnp.zeros((H, M), jnp.float32), 'W_V': jax.random.normal(ks[3], (H, D, M), jnp.float32) * scale, 'b_V': jnp.zeros((H, M), jnp.float32), 'W_O': jax.random.normal(ks[4], (H, M, D), jnp.float32) * scale, 'b_O': jnp.zeros((D,), jnp.float32)}
    _L0_attn_all = _L0_attn_setup()
    _L0_attn_in = {k: v for k, v in _L0_attn_all.items() if k in ('W_Q', 'b_Q', 'W_K', 'b_K', 'W_V', 'b_V', 'W_O', 'b_O')}
    del _L0_attn_all

    def _L0_ffn_setup():
        import jax, jax.numpy as jnp
        import numpy as np
        B, S, D, E = (8, 256, 192, 8)
        F = 4 * D
        key = jax.random.key(seed)
        ks = jax.random.split(key, 5)
        scale = 0.02
        x = jax.random.normal(ks[0], (B, S, D), jnp.float32)
        gate_w = jax.random.normal(ks[1], (D, E), jnp.float32) * scale
        gate_b = jnp.zeros((E,), jnp.float32)
        w1 = jax.random.normal(ks[2], (E, D, F), jnp.float32) * scale
        b1 = jnp.zeros((E, F), jnp.float32)
        w2 = jax.random.normal(ks[3], (E, F, D), jnp.float32) * scale
        b2 = jnp.zeros((E, D), jnp.float32)
        return {'x': x, 'gate_w': gate_w, 'gate_b': gate_b, 'w1': w1, 'b1': b1, 'w2': w2, 'b2': b2}
    _L0_ffn_all = _L0_ffn_setup()
    _L0_ffn_in = {k: v for k, v in _L0_ffn_all.items() if k in ('gate_w', 'gate_b', 'w1', 'b1', 'w2', 'b2')}
    del _L0_ffn_all
    return {'x': x, 'L0_tok_cw0': _L0_tok_in['cw0'], 'L0_tok_cb0': _L0_tok_in['cb0'], 'L0_tok_gw0': _L0_tok_in['gw0'], 'L0_tok_gb0': _L0_tok_in['gb0'], 'L0_tok_cw1': _L0_tok_in['cw1'], 'L0_tok_cb1': _L0_tok_in['cb1'], 'L0_tok_gw1': _L0_tok_in['gw1'], 'L0_tok_gb1': _L0_tok_in['gb1'], 'L0_tok_cw2': _L0_tok_in['cw2'], 'L0_tok_cb2': _L0_tok_in['cb2'], 'L0_tok_gw2': _L0_tok_in['gw2'], 'L0_tok_gb2': _L0_tok_in['gb2'], 'L0_tok_cw3': _L0_tok_in['cw3'], 'L0_tok_cb3': _L0_tok_in['cb3'], 'L0_tok_gw3': _L0_tok_in['gw3'], 'L0_tok_gb3': _L0_tok_in['gb3'], 'L0_tok_cw4': _L0_tok_in['cw4'], 'L0_tok_cb4': _L0_tok_in['cb4'], 'L0_tok_gw4': _L0_tok_in['gw4'], 'L0_tok_gb4': _L0_tok_in['gb4'], 'L0_tok_cw5': _L0_tok_in['cw5'], 'L0_tok_cb5': _L0_tok_in['cb5'], 'L0_tok_gw5': _L0_tok_in['gw5'], 'L0_tok_gb5': _L0_tok_in['gb5'], 'L0_tok_pw': _L0_tok_in['pw'], 'L0_tok_pb': _L0_tok_in['pb'], 'L0_attn_W_Q': _L0_attn_in['W_Q'], 'L0_attn_b_Q': _L0_attn_in['b_Q'], 'L0_attn_W_K': _L0_attn_in['W_K'], 'L0_attn_b_K': _L0_attn_in['b_K'], 'L0_attn_W_V': _L0_attn_in['W_V'], 'L0_attn_b_V': _L0_attn_in['b_V'], 'L0_attn_W_O': _L0_attn_in['W_O'], 'L0_attn_b_O': _L0_attn_in['b_O'], 'L0_ffn_gate_w': _L0_ffn_in['gate_w'], 'L0_ffn_gate_b': _L0_ffn_in['gate_b'], 'L0_ffn_w1': _L0_ffn_in['w1'], 'L0_ffn_b1': _L0_ffn_in['b1'], 'L0_ffn_w2': _L0_ffn_in['w2'], 'L0_ffn_b2': _L0_ffn_in['b2']}

def reference(x, L0_tok_cw0, L0_tok_cb0, L0_tok_gw0, L0_tok_gb0, L0_tok_cw1, L0_tok_cb1, L0_tok_gw1, L0_tok_gb1, L0_tok_cw2, L0_tok_cb2, L0_tok_gw2, L0_tok_gb2, L0_tok_cw3, L0_tok_cb3, L0_tok_gw3, L0_tok_gb3, L0_tok_cw4, L0_tok_cb4, L0_tok_gw4, L0_tok_gb4, L0_tok_cw5, L0_tok_cb5, L0_tok_gw5, L0_tok_gb5, L0_tok_pw, L0_tok_pb, L0_attn_W_Q, L0_attn_b_Q, L0_attn_W_K, L0_attn_b_K, L0_attn_W_V, L0_attn_b_V, L0_attn_W_O, L0_attn_b_O, L0_ffn_gate_w, L0_ffn_gate_b, L0_ffn_w1, L0_ffn_b1, L0_ffn_w2, L0_ffn_b2):
    import jax
    import jax.numpy as jnp

    def _L0_tok_ref(x, cw0, cb0, gw0, gb0, cw1, cb1, gw1, gb1, cw2, cb2, gw2, gb2, cw3, cb3, gw3, gb3, cw4, cb4, gw4, gb4, cw5, cb5, gw5, gb5, pw, pb):
        import jax, jax.numpy as jnp
        import numpy as np
        from jax import lax
        CONV_LAYERS = [(128, 10, 5), (128, 3, 2), (128, 3, 2), (128, 3, 2), (128, 3, 2), (128, 2, 2)]
        NUM_GROUPS = 32
        EPS = 1e-05
        EMBED_DIM = 192

        def _block(x, cw, cb, gw, gb, stride):
            y = lax.conv_general_dilated(x, cw, (stride,), 'VALID', dimension_numbers=('NCH', 'OIH', 'NCH'))
            y = y + cb[None, :, None]
            B, C, T = y.shape
            yg = y.reshape(B, NUM_GROUPS, C // NUM_GROUPS * T)
            mu = yg.mean(axis=-1, keepdims=True)
            var = yg.var(axis=-1, keepdims=True)
            yn = ((yg - mu) * lax.rsqrt(var + EPS)).reshape(B, C, T)
            yn = yn * gw[None, :, None] + gb[None, :, None]
            return jax.nn.gelu(yn)

        def _forward(x, conv_params, pw, pb):
            h = x[:, None, :]
            for (cw, cb, gw, gb), (_, _, s) in zip(conv_params, CONV_LAYERS):
                h = _block(h, cw, cb, gw, gb, s)
            h = jnp.transpose(h, (0, 2, 1))
            return jnp.einsum('bfc,ec->bfe', h, pw) + pb
        conv_params = [(cw0, cb0, gw0, gb0), (cw1, cb1, gw1, gb1), (cw2, cb2, gw2, gb2), (cw3, cb3, gw3, gb3), (cw4, cb4, gw4, gb4), (cw5, cb5, gw5, gb5)]
        return _forward(x, conv_params, pw, pb)

    def _L0_attn_ref(x, W_Q, b_Q, W_K, b_K, W_V, b_V, W_O, b_O):
        import jax, jax.numpy as jnp
        import numpy as np
        D_HEAD = 64
        IGNORE = -100000.0
        q = jnp.einsum('bqd,hdm->bqhm', x, W_Q) + b_Q
        k = jnp.einsum('bkd,hdm->bkhm', x, W_K) + b_K
        v = jnp.einsum('bkd,hdm->bkhm', x, W_V) + b_V
        scores = jnp.einsum('bqhm,bkhm->bhqk', q, k) / jnp.sqrt(jnp.asarray(D_HEAD, q.dtype))
        S = x.shape[1]
        causal = jnp.arange(S)[:, None] >= jnp.arange(S)[None, :]
        scores = jnp.where(causal[None, None, :, :], scores, jnp.asarray(IGNORE, scores.dtype))
        pattern = jax.nn.softmax(scores, axis=-1)
        z = jnp.einsum('bhqk,bkhm->bqhm', pattern, v)
        attn_out = jnp.einsum('bqhm,hmd->bqd', z, W_O) + b_O
        return attn_out

    def _L0_ffn_ref(x, gate_w, gate_b, w1, b1, w2, b2):
        import jax, jax.numpy as jnp
        import numpy as np
        B, S, D, E = (8, 256, 192, 8)
        F = 4 * D
        orig_shape = x.shape
        xt = x.reshape(-1, x.shape[-1])
        gates = jax.nn.softmax(xt @ gate_w + gate_b, axis=-1)
        expert_idx = jnp.argmax(gates, axis=-1)
        out = jnp.zeros_like(xt)
        n_experts = w1.shape[0]
        for e in range(n_experts):
            h = jax.nn.gelu(xt @ w1[e] + b1[e], approximate=False)
            y = h @ w2[e] + b2[e]
            out = jnp.where((expert_idx == e)[:, None], y, out)
        return out.reshape(orig_shape)
    h = _L0_tok_ref(x, L0_tok_cw0, L0_tok_cb0, L0_tok_gw0, L0_tok_gb0, L0_tok_cw1, L0_tok_cb1, L0_tok_gw1, L0_tok_gb1, L0_tok_cw2, L0_tok_cb2, L0_tok_gw2, L0_tok_gb2, L0_tok_cw3, L0_tok_cb3, L0_tok_gw3, L0_tok_gb3, L0_tok_cw4, L0_tok_cb4, L0_tok_gw4, L0_tok_gb4, L0_tok_cw5, L0_tok_cb5, L0_tok_gw5, L0_tok_gb5, L0_tok_pw, L0_tok_pb)
    h = h + _L0_attn_ref(_layernorm(h, axis=-1), L0_attn_W_Q, L0_attn_b_Q, L0_attn_W_K, L0_attn_b_K, L0_attn_W_V, L0_attn_b_V, L0_attn_W_O, L0_attn_b_O)
    h = h + _L0_ffn_ref(_layernorm(h, axis=-1), L0_ffn_gate_w, L0_ffn_gate_b, L0_ffn_w1, L0_ffn_b1, L0_ffn_w2, L0_ffn_b2)
    return h

_drawn_inputs = setup_inputs


def setup_inputs(seed=0):
    import zlib

    import numpy as np

    out = dict(_drawn_inputs(seed))
    spreads = {'L0_tok_gw0': (1.0, 0.2),
     'L0_tok_gb0': (0.0, 0.1),
     'L0_tok_gw1': (1.0, 0.2),
     'L0_tok_gb1': (0.0, 0.1),
     'L0_tok_gw2': (1.0, 0.2),
     'L0_tok_gb2': (0.0, 0.1),
     'L0_tok_gw3': (1.0, 0.2),
     'L0_tok_gb3': (0.0, 0.1),
     'L0_tok_gw4': (1.0, 0.2),
     'L0_tok_gb4': (0.0, 0.1),
     'L0_tok_gw5': (1.0, 0.2),
     'L0_tok_gb5': (0.0, 0.1),
     'L0_attn_b_Q': (0.0, 0.729),
     'L0_attn_b_K': (0.0, 0.8),
     'L0_attn_b_V': (0.0, 0.1),
     'L0_attn_b_O': (0.0, 0.1),
     'L0_ffn_gate_b': (0.0, 0.1),
     'L0_ffn_b1': (0.0, 0.1),
     'L0_ffn_b2': (0.0, 0.1)}
    factors = {}
    for name, (base, spread) in spreads.items():
        noise = np.random.default_rng([zlib.crc32(name.encode()), seed]).standard_normal(out[name].shape)
        drawn = base * np.exp(spread * noise) if base else spread * noise
        out[name] = jnp.asarray(drawn.astype(out[name].dtype))
    for name, factor in factors.items():
        out[name] = (out[name] * factor).astype(out[name].dtype)
    return out
```

```python
from contextlib import ExitStack

import numpy as np
import concourse.bass as bass
from concourse import mybir

BATCH, SAMPLES = 4, 120000
COLS, PITCH = 125, 126
ROWS = [192, 96, 48, 24, 12, 6]
CONV_LAYERS, CH, GROUP = 6, 128, 4
TAPS0, STRIDE0 = 10, 5
PER_COL = SAMPLES // COLS
SUB, NBLK = 6, 32
WIN = STRIDE0 * (SUB - 1) + TAPS0
BLK_STEP = SUB * STRIDE0
D, HEADS, DH, EXPERTS, FF = 192, 12, 64, 8, 768
D1 = D - 128
PAIRS = HEADS // 2
TOK = ROWS[5] * COLS
SEQ = TOK - 1
TT = -(-TOK // 128)
LASTM = TOK - 128 * (TT - 1)
TILES = BATCH * TT
SLOT_TILES = (BATCH * SEQ + EXPERTS * 127) // 128
EPS = 1e-5
SCALE = DH ** -0.5
MASKED = -8.0e5
ACT_ENGINE, DVE_ENGINE = "act", "dve"


def tile_rows(i):
    return LASTM if i == TT - 1 else 128


def tower_jobs():
    jobs = [("xt", (i,), (DVE_ENGINE,)) for i in range(2)]
    jobs += [("stats0", (j, i), (DVE_ENGINE,)) for j in range(8) for i in range(3)]
    jobs.append(("group", (0,), (DVE_ENGINE,)))
    t = 0
    for j in range(8):
        jobs += [("conv0", (j, i), (ACT_ENGINE,)) for i in range(3)]
        while t < ROWS[1] // 8 and min(16 * t + 16, ROWS[0] - 1) // 24 <= j - 1:
            jobs.append(("conv", (1, 8 * t, (4, 4)), (ACT_ENGINE,)))
            t += 1
    while t < ROWS[1] // 8:
        jobs.append(("conv", (1, 8 * t, (4, 4)), (ACT_ENGINE,)))
        t += 1
    jobs.append(("group", (1,), (DVE_ENGINE,)))
    for layer in range(2, CONV_LAYERS):
        r = 0
        while r < ROWS[layer]:
            cut = (3, 3) if layer == 5 else (4, 4) if ROWS[layer] - r >= 8 else (4,)
            jobs.append(("conv", (layer, r, cut), (ACT_ENGINE,)))
            r += sum(cut)
        jobs.append(("group", (layer,), (DVE_ENGINE,)))
    jobs += [("embed", (0,), (DVE_ENGINE,)), ("embed", (1,), (DVE_ENGINE,))]
    jobs += [("tr", (0,), (DVE_ENGINE,)), ("tr", (1,), (ACT_ENGINE,))]
    return jobs


def pair_jobs():
    jobs = [("q", (), (ACT_ENGINE,)), ("k", (), (DVE_ENGINE,)), ("v", (), (ACT_ENGINE,))]
    steps = 2 * TT
    score = [("s", (n,), (ACT_ENGINE,)) for n in range(steps)]
    jobs.append(score[0])
    for n in range(steps):
        if n + 1 < steps:
            jobs.append(score[n + 1])
        jobs.append(("pt", (n,), (DVE_ENGINE, ACT_ENGINE) if n % TT >= 4 else (DVE_ENGINE,)))
        if n:
            jobs.append(("z", (n - 1,), (ACT_ENGINE,)))
    jobs += [("z", (steps - 1,), (ACT_ENGINE,)), ("zt", (), (DVE_ENGINE,))]
    return jobs


def post_jobs():
    return [("wo", (0,), (DVE_ENGINE,)), ("wo", (1,), (DVE_ENGINE,)),
            ("tr", (0,), (DVE_ENGINE,)), ("tr", (1,), (ACT_ENGINE,)),
            ("gate", (), (DVE_ENGINE,)), ("pad", (), (DVE_ENGINE,))]


def setup_jobs():
    return [("cwt", (1,), (DVE_ENGINE,)), ("cwt", (2,), (DVE_ENGINE,)), ("cwt", (3,), (DVE_ENGINE,)),
            ("cwt", (4,), (DVE_ENGINE,)), ("cwt", (5,), (DVE_ENGINE,)), ("cw0t", (), (ACT_ENGINE,)),
            ("pwt", (), (ACT_ENGINE,)), ("pad", (), (ACT_ENGINE,))]


SETUP, TOWER, PAIR, POST, MOE = range(5)
JOBS = {SETUP: setup_jobs(), TOWER: tower_jobs(), PAIR: pair_jobs(), POST: post_jobs()}
while (len(JOBS[TOWER]) + len(JOBS[POST])) % 4:
    JOBS[POST].append(("pad", (), (DVE_ENGINE,)))
assert len(JOBS[SETUP]) % 4 == 0 and len(JOBS[PAIR]) % 4 == 0
PHASES = (SETUP, TOWER, PAIR, POST)


def readers(phase, engine):
    return sum(engine in job[2] for job in JOBS[phase])


COUNTS = {
    "ps_full": tuple(len(JOBS[f]) for f in PHASES),
    "act_freed": tuple(readers(f, ACT_ENGINE) for f in PHASES),
    "dve_freed": tuple(readers(f, DVE_ENGINE) for f in PHASES),
    "x_loaded": (32, 32, 0, 0),
    "var_ready": (0, CONV_LAYERS + 1, 0, 1),
    "rstd_ready": (0, CONV_LAYERS + 1, 0, 1),
    "x_split": (1, 1, 0, 0),
    "channel_stats": (0, CONV_LAYERS, 0, 0),
    "affine_ready": (0, CONV_LAYERS, 0, 0),
    "norm_done": (0, 14, 0, 0),
    "halo_done": (0, 4, 0, 0),
    "xn_ready": (0, 1, 0, 1),
    "w_loaded": (96, 0, 96, 0),
    "smax_done": (0, 0, 2 * TT, 0),
    "rinv_ready": (0, 0, 2 * TT, 0),
    "h1_ready": (0, 0, 0, 1),
    "scratch_stored": (16, 0, 0, 64),
    "dve_step": (1, 38, 12, 9),
}
NORM_CHUNKS = {1: [16] * 6, 2: [16] * 3, 3: [8] * 3, 4: [12], 5: [6]}


def at(sem, phase, k, b=None, pr=None):
    s, t, p, o = COUNTS[sem]
    period = t + PAIRS * p + o
    if phase == SETUP:
        return k
    if phase == MOE:
        return s + BATCH * period + k
    base = b * period + s
    if phase == TOWER:
        return base + k
    if phase == PAIR:
        return base + pr * p + (t + k) if p else base + (t + k)
    return base + (t + PAIRS * p + k)


def freed(phase, engine, n):
    return sum(engine in job[2] for job in JOBS[phase][:n + 1])


def norm_chunk_of(layer, row):
    before = sum(len(NORM_CHUNKS[i]) for i in range(1, layer))
    edge = 0
    for n, rows in enumerate(NORM_CHUNKS[layer]):
        edge += rows
        if row < edge:
            return before + n + 1


def job_index(phase, kind, args):
    return next(n for n, job in enumerate(JOBS[phase]) if job[0] == kind and job[1] == args)


def audio_tower(nc, ins, out):
    fp32, fp16, bf16, i32 = mybir.dt.float32, mybir.dt.float16, mybir.dt.bfloat16, mybir.dt.int32
    ALU, ACT, AX = mybir.AluOpType, mybir.ActivationFunctionType, mybir.AxisListType

    h1_dram = nc.dram_tensor("h1_scratch", (TILES, 128, D), fp32, kind="Internal").ap()
    x2_dram = nc.dram_tensor("x2_scratch", (TILES, 128, D), fp32, kind="Internal").ap()
    xslot_dram = nc.dram_tensor("xslot_scratch", (SLOT_TILES * 128, D), fp32, kind="Internal").ap()
    yslot_dram = nc.dram_tensor("yslot_scratch", (SLOT_TILES * 128, D), fp32, kind="Internal").ap()

    ctx = ExitStack()
    with ctx:
        def sb(name, shape, dt=fp32):
            return ctx.enter_context(nc.sbuf_tensor(name, shape, dt))

        def sem(name):
            return ctx.enter_context(nc.semaphore(name))

        ident = sb("ident", [128, 128])
        ident_h = sb("ident_h", [128, 128], fp16)
        ident_b = sb("ident_b", [128, 128], bf16)
        causal_b = sb("causal_b", [128, 128], bf16)
        group_avg = sb("group_avg", [128, 128])
        cwt = [None] + [sb(f"cwt{l}", [CH, 2 if l == 5 else 3, CH]) for l in range(1, CONV_LAYERS)]
        cw0t = sb("cw0t", [3 * WIN, SUB, CH], fp16)
        pwt = sb("pwt", [CH, D])
        par = sb("par", [CH, 3, CONV_LAYERS])
        pb_b = sb("pb_b", [128, D])
        bo_b = sb("bo_b", [128, D])
        gate_b = sb("gate_b", [128, EXPERTS])
        gw0 = sb("gw0", [128, EXPERTS])
        gw1 = sb("gw1", [D1, EXPERTS])
        wo = sb("wo", [128, PAIRS, D])
        bqkv = sb("bqkv", [128, 3, PAIRS])
        wqkv0 = sb("wqkv0", [128, 3, 128])
        wqkv1 = sb("wqkv1", [D1, 3, 128])
        onehot = sb("onehot", [128, TILES, EXPERTS])
        prefer = sb("prefer", [128, EXPERTS])
        bn = sb("bn", [128, 49, 6])
        mv = sb("mv", [128, 2])
        ms = sb("ms", [128, 2])
        gm = sb("gm", [128, 2])
        tmp = sb("tmp", [128, 4])
        spare = sb("spare", [128, 16])
        affine = sb("affine", [128, 2])
        lnmv = sb("lnmv", [128, TT, 2])
        lnr = sb("lnr", [128, TT])
        lnv = sb("lnv", [128, TT])
        neg_half = sb("neg_half", [128, TT])
        smax = sb("smax", [128, 2 * TT])
        nmax = sb("nmax", [128, 2 * TT])
        rsum = sb("rsum", [128, 2 * TT])
        rinv = sb("rinv", [128, 2 * TT])
        logits = sb("logits", [128, TT, EXPERTS])
        pick = sb("pick", [128, TT, EXPERTS])
        best = sb("best", [128, TT])
        zeros = sb("zeros", [128, D])
        xa = sb("xa", [PITCH, PER_COL + BLK_STEP + 2])
        xstack = sb("xstack", [PITCH, NBLK, 3 * WIN], fp16)
        xt = sb("xt", [3 * WIN, NBLK, PITCH], fp16)

        H0, Y1 = (ROWS[0] + 1) * PITCH, (ROWS[1] + 1) * PITCH
        arena = sb("arena", [128, H0 + Y1 + 32])
        y0 = arena[:, 0:H0]
        y1 = arena[:, H0:H0 + Y1]
        acts, low = [y0, y1], 0
        for l in range(2, CONV_LAYERS):
            size = (ROWS[l] + 1) * PITCH
            acts.append(arena[:, low:low + size])
            low += size
        cursor = [low]

        def take(n):
            a = arena[:, cursor[0]:cursor[0] + n]
            cursor[0] += n
            return a

        h5t = take(TOK)
        h = take(TT * D).rearrange("p (t d) -> p t d", d=D)
        xn = take(TT * D).rearrange("p (t d) -> p t d", d=D)
        xnt0 = take(TT * 128)
        xnt1 = take(TT * 128)
        qt = take(TT * 128)
        kt = take(TT * 128)
        vt = take(TT * 128).rearrange("p (t c) -> p t c", c=128)
        prob = [take(TT * 128) for _ in range(2)]
        probt = [take(TT * 128).rearrange("p (t c) -> p t c", c=128) for _ in range(2)]
        z = take(TT * 128).rearrange("p (t c) -> p t c", c=128)
        zt = take(PAIRS * TT * 128).rearrange("p (a t) -> p a t", a=PAIRS)
        assert cursor[0] <= H0 + Y1 + 32

        cursor[0] = 0
        cwn = [None] + [take((2 if l == 5 else 3) * CH) for l in range(1, CONV_LAYERS)]
        cw0n = take(TAPS0)
        cw0pad = take(SUB * 3 * WIN // 2).bitcast(fp16).rearrange("p (m k) -> p m k", m=SUB)
        pwn = take(2 * CH).rearrange("p (a c) -> p a c", a=2)

        cursor[0] = 0
        w1a = take(EXPERTS * FF).rearrange("p (e f) -> p e f", e=EXPERTS)
        w1b = take(EXPERTS * FF).rearrange("p (e f) -> p e f", e=EXPERTS)
        w2 = take(EXPERTS * PAIRS * D).rearrange("p (e c d) -> p e c d", e=EXPERTS, c=FF // 128)
        b2 = take(EXPERTS * D).rearrange("p (e d) -> p e d", e=EXPERTS)
        h1 = take(TILES * D).rearrange("p (t d) -> p t d", d=D)
        x2 = take(TILES * D).rearrange("p (t d) -> p t d", d=D)
        before = take(128)
        ones = take(128)
        rank = take(TILES * EXPERTS).rearrange("p (t e) -> p t e", e=EXPERTS)
        per_tile = take(TILES * EXPERTS)
        running = take(TILES * EXPERTS)
        segment = take(TILES * EXPERTS)
        edges = take(TILES)
        counts = take(EXPERTS)
        ntiles = take(EXPERTS)
        tiles_end = take(EXPERTS)
        base = take(EXPERTS)
        slots_f = take(TILES)
        slots = take(TILES).bitcast(i32)
        tile_ids = take(32)
        tile_expert_f = take(32)
        tile_expert = take(32).bitcast(i32)
        over = take(32 * EXPERTS).rearrange("p (j e) -> p j e", e=EXPERTS)
        xtile = take(D)
        xe0 = take(128)
        xe1 = take(128)
        hid = take(FF)
        hidt = take(FF).rearrange("p (c t) -> p c t", c=FF // 128)
        ytile = take(D)
        assert cursor[0] <= H0 + Y1 + 32
        y_tok = x2

        ps = ctx.enter_context(nc.psum_tensor("ps", [128, 8 * 512], fp32))

        def slot(n):
            return ps[:, (n % 4) * 1024:(n % 4 + 1) * 1024]

        def bank(n, i):
            return ps[:, (n % 4) * 1024 + 512 * i:(n % 4) * 1024 + 512 * i + 512]

        S = {name: sem(name) for name in COUNTS}
        consts_ready = sem("consts_ready")
        weights_loaded = sem("weights_loaded")
        pads_ready = sem("pads_ready")
        cw0_stacked = sem("cw0_stacked")
        experts_loaded = sem("experts_loaded")
        tokens_loaded = sem("tokens_loaded")
        moe_consts = sem("moe_consts")
        slots_ready = sem("slots_ready")
        scattered = sem("scattered")
        xtile_loaded = sem("xtile_loaded")
        rank_full = sem("rank_full")
        xt_full, hid_full, hidt_full, y_full = sem("xt_full"), sem("hid_full"), sem("hidt_full"), sem("y_full")
        xt_taken, hid_taken, y_taken = sem("xt_taken"), sem("hid_taken"), sem("y_taken")
        hidt_taken_dve, hidt_taken_act = sem("hidt_taken_dve"), sem("hidt_taken_act")
        y_stored = sem("y_stored")
        gathered = sem("gathered")
        out_ready = sem("out_ready")
        out_stored = sem("out_stored")
        N_CONSTS = 13
        N_MOE_CONSTS = 10
        block = ctx.enter_context(nc.Block())

        def wait(eng, name, phase, k, b=None, pr=None):
            eng.wait_ge(S[name], at(name, phase, k, b, pr))

        SLOT0 = {SETUP: 0, TOWER: 0, PAIR: len(JOBS[TOWER]), POST: len(JOBS[TOWER])}

        n_weight_dmas = 0

        @block.sync
        def _(sp):
            nonlocal n_weight_dmas

            def load(dst, src):
                nonlocal n_weight_dmas
                sp.dma_start(dst, src, allow_slow_non_contiguous=True).then_inc(weights_loaded, 16)
                n_weight_dmas += 1

            def col(a):
                return a.rearrange("(p a) -> p a", a=1)

            load(cw0n, ins["L0_tok_cw0"].rearrange("o i k -> o (i k)"))
            for l in range(1, CONV_LAYERS):
                load(cwn[l], ins[f"L0_tok_cw{l}"].rearrange("o i k -> o (i k)"))
            load(pwn[:, 0, :], ins["L0_tok_pw"][0:128, :])
            load(pwn[0:D1, 1, :], ins["L0_tok_pw"][128:D, :])
            for l in range(CONV_LAYERS):
                for n, name in enumerate(("cb", "gw", "gb")):
                    load(par[:, n, l:l + 1], col(ins[f"L0_tok_{name}{l}"]))
            load(pb_b[:, :], ins["L0_tok_pb"].partition_broadcast(128))
            load(bo_b[:, :], ins["L0_attn_b_O"].partition_broadcast(128))
            load(gate_b[:, :], ins["L0_ffn_gate_b"].partition_broadcast(128))
            load(gw0[:, :], ins["L0_ffn_gate_w"][0:128, :])
            load(gw1[:, :], ins["L0_ffn_gate_w"][128:D, :])
            load(wo[:, :, :], ins["L0_attn_W_O"].rearrange("(a h) m d -> (h m) a d", h=2))
            for n, name in enumerate("QKV"):
                for hh in range(2):
                    load(bqkv[DH * hh:DH * hh + DH, n, :],
                         ins[f"L0_attn_b_{name}"].rearrange("(a h) m -> h m a", h=2)[hh, :, :])

            def load_pair(pr):
                for n, name in enumerate("QKV"):
                    w = ins[f"L0_attn_W_{name}"].rearrange("(a h) d m -> a d h m", h=2)
                    for buf, rows in ((wqkv0, (0, 128)), (wqkv1, (128, D))):
                        if isinstance(pr, int):
                            src = w[pr, rows[0]:rows[1], :, :]
                        else:
                            src = w[bass.ds(pr, 1), rows[0]:rows[1], :, :].rearrange("a d h m -> (a d) h m")
                        sp.dma_start(buf[:, n, :].rearrange("p (h m) -> p h m", h=2), src
                                     ).then_inc(S["w_loaded"], 16)

            load_pair(0)
            sp.wait_ge(pads_ready, 3)
            sp.dma_start(xslot_dram.rearrange("(t p) d -> p t d", p=128),
                         zeros[:, :].unsqueeze(1).to_broadcast([128, SLOT_TILES, D])).then_inc(S["scratch_stored"], 16)
            with sp.Fori(0, BATCH) as b:
                with sp.Fori(0, PAIRS - 1) as pr:
                    wait(sp, "ps_full", PAIR, 3, b, pr)
                    load_pair(pr + 1)
                wait(sp, "ps_full", PAIR, 3, b, PAIRS - 1)
                load_pair(0)
                wait(sp, "h1_ready", POST, 1, b)
                for src, dst in ((h, h1_dram), (xn, x2_dram)):
                    full = dst[bass.ds(b * TT, TT - 1), :, :].rearrange("t p d -> p t d")
                    sp.dma_start(full, src[:, 0:TT - 1, :]).then_inc(S["scratch_stored"], 16)
                    last = dst[bass.ds(b * TT + TT - 1, 1), 0:LASTM, :].rearrange("t p d -> p t d")
                    sp.dma_start(last, src[0:LASTM, TT - 1:TT, :]).then_inc(S["scratch_stored"], 16)

            wait(sp, "scratch_stored", MOE, 0)
            wait(sp, "ps_full", MOE, 0)
            for tile, dram in ((x2, x2_dram), (h1, h1_dram)):
                for b in range(BATCH):
                    sp.dma_start(tile[:, b * TT:b * TT + TT - 1, :],
                                 dram[b * TT:b * TT + TT - 1, :, :].rearrange("t p d -> p t d")
                                 ).then_inc(tokens_loaded, 16)
                    sp.dma_start(tile[0:LASTM, b * TT + TT - 1, :], dram[b * TT + TT - 1, 0:LASTM, :]
                                 ).then_inc(tokens_loaded, 16)
            for e in range(EXPERTS):
                sp.dma_start(w1a[:, e, :], ins["L0_ffn_w1"][e, 0:128, :]).then_inc(experts_loaded, 16)
                sp.dma_start(w1b[0:D1, e, :], ins["L0_ffn_w1"][e, 128:D, :]).then_inc(experts_loaded, 16)
                sp.dma_start(w2[:, e, :, :], ins["L0_ffn_w2"][e, :, :].rearrange("(c p) d -> p c d", p=128)
                             ).then_inc(experts_loaded, 16)
            sp.dma_start(w1b[D1:D1 + 1, :, :], ins["L0_ffn_b1"].unsqueeze(0)).then_inc(experts_loaded, 16)
            sp.dma_start(b2[0:1, :, :], ins["L0_ffn_b2"].unsqueeze(0)).then_inc(experts_loaded, 16)

            def xslot_tile(j):
                return xslot_dram[bass.ds(j * 128, 128), :]

            sp.wait_ge(scattered, 16 * TILES)
            sp.dma_start(xtile, xslot_dram[0:128, :]).then_inc(xtile_loaded, 16)
            sp.wait_ge(xt_full, 1)
            sp.dma_start(xtile, xslot_dram[128:256, :]).then_inc(xtile_loaded, 16)
            sp.wait_ge(xt_full, 2)
            sp.dma_start(xtile, xslot_dram[256:384, :]).then_inc(xtile_loaded, 16)
            sp.wait_ge(y_taken, 1)
            sp.dma_start(yslot_dram[0:128, :], ytile).then_inc(y_stored, 16)
            with sp.Fori(3, SLOT_TILES) as j:
                sp.wait_ge(xt_full, j)
                sp.dma_start(xtile, xslot_tile(j)).then_inc(xtile_loaded, 16)
                sp.wait_ge(y_taken, j - 1)
                sp.dma_start(yslot_dram[bass.ds(j * 128 - 256, 128), :], ytile).then_inc(y_stored, 16)
            for j in (SLOT_TILES - 2, SLOT_TILES - 1):
                sp.wait_ge(y_taken, j + 1)
                sp.dma_start(yslot_dram[j * 128:j * 128 + 128, :], ytile).then_inc(y_stored, 16)
            for b in range(BATCH):
                sp.wait_ge(out_ready, b + 1)
                n = TT - 1
                sp.dma_start(out[b, 0:128 * n, :].rearrange("(t p) d -> p t d", p=128),
                             h1[:, b * TT:b * TT + n, :]).then_inc(out_stored, 16)
                sp.dma_start(out[b, 128 * n:SEQ, :], h1[0:LASTM - 1, b * TT + n, :]).then_inc(out_stored, 16)
            sp.wait_ge(out_stored, 16 * 2 * BATCH)

        @block.gpsimd
        def _(pool):
            steps = [0]

            def const(ins_, wait_last=True):
                steps[0] += 1
                ins_.then_inc(consts_ready, 1)
                if wait_last:
                    pool.wait_ge(consts_ready, steps[0])

            g = nc.gpsimd
            for m in (ident, ident_h, ident_b):
                const(g.memset(m[:, :], 0.0))
                const(g.affine_select(out=m[:, :], in_=m[:, :], compare_op=ALU.not_equal, fill=1.0, base=0,
                                      pattern=[[-1, 128]], channel_multiplier=1))
            const(g.memset(causal_b[:, :], 0.0))
            const(g.affine_select(out=causal_b[:, :], in_=causal_b[:, :], compare_op=ALU.is_ge, fill=MASKED,
                                  base=0, pattern=[[-1, 128]], channel_multiplier=1))
            const(g.memset(group_avg[:, :], 1.0 / GROUP))
            const(g.affine_select(out=group_avg[:, :], in_=group_avg[:, :], compare_op=ALU.is_ge, fill=0.0,
                                  base=0, pattern=[[-GROUP, 128 // GROUP], [0, GROUP]], channel_multiplier=1))
            const(g.affine_select(out=group_avg[:, :], in_=group_avg[:, :], compare_op=ALU.is_ge, fill=0.0,
                                  base=GROUP - 1, pattern=[[GROUP, 128 // GROUP], [0, GROUP]],
                                  channel_multiplier=-1))
            const(g.iota(prefer[:, :], pattern=[[-1, EXPERTS]], base=EXPERTS, channel_multiplier=0,
                         allow_small_or_imprecise_dtypes=True))
            const(g.memset(neg_half[:, :], -0.5))
            assert steps[0] == N_CONSTS

            def load_samples(b):
                x = ins["x"][b:b + 1, :] if isinstance(b, int) else ins["x"][bass.ds(b, 1), :]
                rows = x.rearrange("a (p n) -> (a p) n", n=PER_COL)
                pool.dma_start(xa[0:COLS, 0:PER_COL], rows).then_inc(S["x_loaded"], 16)
                pool.dma_start(xa[0:COLS - 1, PER_COL:PER_COL + STRIDE0], rows[1:COLS, 0:STRIDE0]
                               ).then_inc(S["x_loaded"], 16)

            pool.wait_ge(S["x_split"], 1)
            load_samples(0)
            with pool.Fori(0, BATCH) as b:
                for n in range(CONV_LAYERS):
                    wait(pool, "var_ready", TOWER, n + 1, b)
                    g.tensor_tensor(tmp[:, 2:3], tmp[:, 1:2], neg_half[:, 0:1], ALU.pow
                                    ).then_inc(S["rstd_ready"], 1)
                    if n == 0:
                        wait(pool, "x_split", TOWER, 1, b)
                        load_samples((b + 1) & (BATCH - 1))
                for phase, k in ((TOWER, CONV_LAYERS + 1), (POST, 1)):
                    wait(pool, "var_ready", phase, k, b)
                    g.tensor_tensor(lnr[:, :], lnv[:, :], neg_half[:, 0:TT], ALU.pow
                                    ).then_inc(S["rstd_ready"], 1)

            wait(pool, "ps_full", MOE, 0)
            wait(pool, "scratch_stored", MOE, 0)
            steps[0] = 0

            def moe_const(ins_):
                steps[0] += 1
                ins_.then_inc(moe_consts, 1)
                pool.wait_ge(moe_consts, steps[0])

            moe_const(g.memset(ones, 1.0))
            moe_const(g.memset(before, 1.0))
            moe_const(g.affine_select(out=before, in_=before, compare_op=ALU.is_gt, fill=0.0, base=0,
                                      pattern=[[1, 128]], channel_multiplier=-1))
            moe_const(g.memset(segment, 1.0))
            moe_const(g.memset(segment.rearrange("p (e t) -> p e t", t=TILES)[:, :, 0:1], 0.0))
            moe_const(g.iota(edges, pattern=[[128, TILES]], base=0, channel_multiplier=0,
                             allow_small_or_imprecise_dtypes=True))
            moe_const(g.iota(tile_ids, pattern=[[1, 32]], base=0, channel_multiplier=0,
                             allow_small_or_imprecise_dtypes=True))
            moe_const(g.memset(xe1[D1:D1 + 1, :], 1.0))
            moe_const(g.memset(counts, 0.0))
            moe_const(g.memset(tiles_end, 0.0))
            assert steps[0] == N_MOE_CONSTS
            pool.wait_ge(slots_ready, 1)
            pool.wait_ge(tokens_loaded, 16 * 4 * BATCH)
            for t in range(TILES):
                rows = SEQ - 128 * (TT - 1) if t % TT == TT - 1 else 128
                pool.indirect_dma_start(out=xslot_dram,
                                        out_offset=bass.IndirectOffsetOnAxis(ap=slots[0:rows, t:t + 1], axis=0),
                                        in_=x2[0:rows, t, :], in_offset=None).then_inc(scattered, 16)
            pool.wait_ge(y_stored, 16 * SLOT_TILES)
            for t in range(TILES):
                rows = SEQ - 128 * (TT - 1) if t % TT == TT - 1 else 128
                pool.indirect_dma_start(out=y_tok[0:rows, t, :], out_offset=None, in_=yslot_dram,
                                        in_offset=bass.IndirectOffsetOnAxis(ap=slots[0:rows, t:t + 1], axis=0)
                                        ).then_inc(gathered, 16)

        @block.scalar
        def _(act):
            a = nc.scalar

            def jobs_of(phase, b=None, pr=None):
                for n, (kind, args, who) in enumerate(JOBS[phase]):
                    if ACT_ENGINE in who:
                        yield n + SLOT0[phase], n, kind, args

            for g, n, kind, args in jobs_of(SETUP):
                wait(act, "ps_full", SETUP, n + 1)
                if kind == "cw0t":
                    src = bank(g, 0).bitcast(fp16)[0:3 * WIN, 0:SUB * CH].rearrange("p (m c) -> p m c", m=SUB)
                    a.activation(cw0t[:, :, :], src, ACT.Copy).then_inc(S["act_freed"], 1)
                elif kind == "pwt":
                    a.activation(pwt[:, :], bank(g, 0)[:, 0:D], ACT.Copy).then_inc(S["act_freed"], 1)
                else:
                    a.activation(spare[:, 0:1], bank(g, 0)[:, 0:1], ACT.Copy).then_inc(S["act_freed"], 1)

            def normalise(layer, b):
                wait(act, "affine_ready", TOWER, layer + 1, b)
                r = 0
                for rows in NORM_CHUNKS[layer]:
                    src = acts[layer][:, r * PITCH:(r + rows) * PITCH]
                    dst = src
                    if layer == 5:
                        src = src.rearrange("p (r c) -> p r c", c=PITCH)[:, :, 0:COLS]
                        dst = h5t.rearrange("p (c r) -> p r c", r=rows)
                    a.activation(dst, src, ACT.Gelu_apprx_tanh, bias=affine[:, 1:2], scale=affine[:, 0:1]
                                 ).then_inc(S["norm_done"], 1)
                    r += rows

            with act.Fori(0, BATCH) as b:
                layer = 0
                for g, n, kind, args in jobs_of(TOWER):
                    if kind == "conv":
                        if args[0] > 1 and args[1] == 0:
                            normalise(args[0] - 1, b)
                        layer, r, cut = args
                        wait(act, "ps_full", TOWER, n + 1, b)
                        rows = cut[0]
                        dst = acts[layer][:, r * PITCH:(r + sum(cut)) * PITCH]
                        src = slot(g).rearrange("p (k n) -> p k n", k=2)[:, 0:len(cut), 0:rows * PITCH]
                        a.activation(dst.rearrange("p (k n) -> p k n", k=len(cut)), src, ACT.Identity,
                                     scale=1.0).then_inc(S["act_freed"], 1)
                    elif kind == "conv0":
                        j, i = args
                        if args == (0, 0):
                            wait(act, "affine_ready", TOWER, 1, b)
                            wait(act, "scratch_stored", TOWER, 0, b)
                        wait(act, "ps_full", TOWER, n + 1, b)
                        rows = acts[0][:, 24 * j * PITCH:24 * (j + 1) * PITCH].rearrange(
                            "p (k m c) -> p m k c", m=SUB, c=PITCH)
                        src = slot(g).rearrange("p (m n) -> p m n", m=2)[:, :, 0:4 * PITCH].rearrange(
                            "p m (k c) -> p m k c", c=PITCH)
                        a.activation(rows[:, 2 * i:2 * i + 2, :, :], src, ACT.Gelu_apprx_tanh,
                                     bias=affine[:, 1:2], scale=affine[:, 0:1]).then_inc(S["act_freed"], 1)
                    else:
                        assert kind == "tr"
                        if layer == 5:
                            normalise(5, b)
                            layer = None
                        wait(act, "ps_full", TOWER, n + 1, b)
                        a.activation(xnt1[0:D1, 0:TOK], slot(g)[0:D1, 0:TOK], ACT.Copy).then_inc(S["act_freed"], 1)
                with act.Fori(0, PAIRS) as pr:
                    for g, n, kind, args in jobs_of(PAIR):
                        if kind == "s":
                            (k,) = args
                            i = k % TT
                            m = tile_rows(i)
                            wait(act, "smax_done", PAIR, k + 1, b, pr)
                            a.activation(prob[k % 2][0:m, 0:128 * i + m], slot(g)[0:m, 0:128 * i + m], ACT.Exp,
                                         bias=nmax[0:m, k:k + 1], scale=SCALE, accum_out=rsum[0:m, k:k + 1]
                                         ).then_inc(S["act_freed"], 1)
                            continue
                        wait(act, "ps_full", PAIR, n + 1, b, pr)
                        if kind == "q":
                            src = slot(g).rearrange("p (k n) -> p k n", k=2)[:, :, 0:TOK // 2]
                            a.activation(qt[:, 0:TOK].rearrange("p (k n) -> p k n", k=2), src, ACT.Identity,
                                         bias=bqkv[:, 0, bass.ds(pr, 1)]).then_inc(S["act_freed"], 1)
                        elif kind == "v":
                            src = slot(g).rearrange("p (t c) -> p t c", c=128)
                            a.activation(vt[:, 0:TT, :], src[:, 0:TT, :], ACT.Copy).then_inc(S["act_freed"], 1)
                        elif kind == "pt":
                            (k,) = args
                            i = k % TT
                            m = tile_rows(i)
                            src = slot(g).rearrange("p (t c) -> p t c", c=128)
                            if i == 4:
                                a.activation(probt[k % 2][:, 4, 0:m], src[:, 4, 0:m], ACT.Copy
                                             ).then_inc(S["act_freed"], 1)
                            else:
                                a.activation(probt[k % 2][:, 4:6, 0:m], src[:, 4:6, 0:m], ACT.Copy
                                             ).then_inc(S["act_freed"], 1)
                        else:
                            assert kind == "z"
                            (k,) = args
                            i, hh = k % TT, k // TT
                            m = tile_rows(i)
                            wait(act, "rinv_ready", PAIR, k + 1, b, pr)
                            a.activation(z[0:m, i, DH * hh:DH * hh + DH], slot(g)[0:m, 0:DH], ACT.Copy,
                                         scale=rinv[0:m, k:k + 1]).then_inc(S["act_freed"], 1)
                for g, n, kind, args in jobs_of(POST):
                    wait(act, "ps_full", POST, n + 1, b)
                    a.activation(xnt1[0:D1, 0:TOK], slot(g)[0:D1, 0:TOK], ACT.Copy).then_inc(S["act_freed"], 1)

            def expert_tile(j):
                act.wait_ge(hid_full, j + 1)
                src = slot(1).rearrange("p (k n) -> p k n", k=2)[:, :, 0:FF // 2]
                a.activation(hid.rearrange("p (k n) -> p k n", k=2), src, ACT.Gelu).then_inc(hid_taken, 1)
                act.wait_ge(hidt_full, j + 1)
                a.activation(hidt[:, 4:6, :], bank(2, 1)[:, 0:256].rearrange("p (c t) -> p c t", c=2), ACT.Copy
                             ).then_inc(hidt_taken_act, 1)

            expert_tile(0)
            with act.Fori(1, SLOT_TILES) as j:
                expert_tile(j)

        @block.vector
        def _(dve):
            v = nc.vector
            state = {"phase": SETUP, "n": 0, "b": None, "pr": None}

            def enter(phase, b=None, pr=None):
                state.update(phase=phase, n=0, b=b, pr=pr)

            def step(ins_):
                state["n"] += 1
                ins_.then_inc(S["dve_step"], 1)
                dve.wait_ge(S["dve_step"], at("dve_step", state["phase"], state["n"], state["b"], state["pr"]))

            def carry_wait():
                v.memset(spare[:, 3:4], 0.0)

            def leave():
                index = {SETUP: 0, TOWER: 1, PAIR: 2, POST: 3}[state["phase"]]
                assert state["n"] == COUNTS["dve_step"][index], (index, state["n"])

            v.memset(xa[:, :], 0.0).then_inc(S["x_split"], 1)
            v.memset(cw0pad, 0.0).then_inc(pads_ready, 1)
            v.memset(xstack[:, :, :], 0.0).then_inc(pads_ready, 1)
            v.memset(zeros[:, :], 0.0).then_inc(pads_ready, 1)
            v.memset(onehot[:, :, :], 0.0).then_inc(pads_ready, 1)
            v.memset(logits[:, :, :], 0.0).then_inc(pads_ready, 1)
            v.memset(lnmv[:, :, :], 0.0).then_inc(pads_ready, 1)
            dve.wait_ge(pads_ready, 6)
            dve.wait_ge(weights_loaded, 16 * n_weight_dmas)
            for m in range(SUB):
                o = STRIDE0 * m
                last = v.tensor_copy(cw0pad[:, m, o:o + TAPS0], cw0n)
            step(last)
            for m in range(SUB):
                o = STRIDE0 * m
                v.tensor_copy(cw0pad[:, m, WIN + o:WIN + o + TAPS0], cw0pad[:, m, o:o + TAPS0])
                last = v.tensor_tensor(cw0pad[:, m, 2 * WIN + o:2 * WIN + o + TAPS0], cw0n,
                                       cw0pad[:, m, o:o + TAPS0], ALU.subtract)
            last.then_inc(cw0_stacked, 1)
            for n, (kind, args, who) in enumerate(JOBS[SETUP]):
                if DVE_ENGINE not in who:
                    continue
                wait(dve, "ps_full", SETUP, n + 1)
                (l,) = args
                taps = 2 if l == 5 else 3
                v.tensor_copy(cwt[l][:, :, :], bank(n, 0)[:, 0:taps * CH].rearrange("p (k c) -> p k c", k=taps)
                              ).then_inc(S["dve_freed"], 1)
            leave()

            def group_stats(layer, pieces, b):
                step(last_bn[0])
                carry_wait()
                step(v.bn_aggr(mv[:, :], bn[:, 0:pieces, :].rearrange("p n s -> p (n s)")))
                step(v.tensor_tensor(ms[:, 0:1], mv[:, 0:1], par[:, 0, layer:layer + 1], ALU.add))
                v.scalar_tensor_tensor(out=ms[:, 1:2], in0=ms[:, 0:1], scalar=ms[:, 0:1], in1=mv[:, 1:2],
                                       op0=ALU.mult, op1=ALU.add).then_inc(S["channel_stats"], 1)

            def group_affine(layer, g, n, b):
                wait(dve, "ps_full", TOWER, n + 1, b)
                ins_ = v.tensor_copy(gm[:, :], bank(g, 0)[:, 0:2])
                ins_.then_inc(S["dve_freed"], 1)
                dve.wait_ge(S["dve_freed"], at("dve_freed", TOWER, freed(TOWER, DVE_ENGINE, n), b))
                step(v.scalar_tensor_tensor(out=tmp[:, 0:1], in0=gm[:, 0:1], scalar=gm[:, 0:1], in1=gm[:, 1:2],
                                            op0=ALU.mult, op1=ALU.subtract))
                v.tensor_scalar(tmp[:, 1:2], tmp[:, 0:1], -1.0, EPS, ALU.mult, ALU.add
                                ).then_inc(S["var_ready"], 1)
                step(v.tensor_tensor(tmp[:, 3:4], par[:, 0, layer:layer + 1], gm[:, 0:1], ALU.subtract))
                wait(dve, "rstd_ready", TOWER, layer + 1, b)
                step(v.tensor_tensor(affine[:, 0:1], tmp[:, 2:3], par[:, 1, layer:layer + 1], ALU.mult))
                v.scalar_tensor_tensor(out=affine[:, 1:2], in0=tmp[:, 3:4], scalar=affine[:, 0:1],
                                       in1=par[:, 2, layer:layer + 1], op0=ALU.mult, op1=ALU.add
                                       ).then_inc(S["affine_ready"], 1)

            def layernorm():
                for i in range(TT):
                    m = tile_rows(i)
                    last = v.bn_stats(bn[0:m, i, :], h[0:m, i, :])
                step(last)
                carry_wait()
                for i in range(TT):
                    m = tile_rows(i)
                    last = v.bn_aggr(lnmv[0:m, i, :], bn[0:m, i, :])
                step(last)
                v.tensor_scalar(lnv[:, :], lnmv[:, :, 1], EPS, None, ALU.add).then_inc(S["var_ready"], 1)
                wait(dve, "rstd_ready", state["phase"], CONV_LAYERS + 1 if state["phase"] == TOWER else 1, state["b"])
                for i in range(TT):
                    m = tile_rows(i)
                    last = v.tensor_scalar(xn[0:m, i, :], h[0:m, i, :], lnmv[0:m, i, 0:1], lnr[0:m, i:i + 1],
                                           ALU.subtract, ALU.mult)
                last.then_inc(S["xn_ready"], 1)

            def take_token_rows(g, part, in1, last_inc=True):
                if part == 0:
                    for k in range(2):
                        last = v.tensor_tensor(h[:, 2 * k:2 * k + 2, :],
                                               bank(g, k)[:, 0:2 * D].rearrange("p (t d) -> p t d", t=2),
                                               in1(2 * k, 2, 128), ALU.add)
                else:
                    v.tensor_tensor(h[:, 4, :], bank(g, 0)[:, 0:D], in1(4, 1, 128), ALU.add)
                    last = v.tensor_tensor(h[0:LASTM, 5, :], bank(g, 0)[0:LASTM, D:2 * D], in1(5, 1, LASTM),
                                           ALU.add)
                last.then_inc(S["dve_freed"], 1)

            def halo(layer, b):
                r = ROWS[layer] * PITCH
                v.tensor_copy(acts[layer][:, r:r + PITCH], acts[layer][:, 1:1 + PITCH]).then_inc(S["halo_done"], 1)

            last_bn = [None]
            with dve.Fori(0, BATCH) as b:
                enter(TOWER, b)
                wait(dve, "x_loaded", TOWER, 0, b)
                main = xa[:, 0:PER_COL].rearrange("p (n k) -> p n k", k=BLK_STEP)
                tail = xa[:, BLK_STEP:BLK_STEP + PER_COL].rearrange("p (n k) -> p n k", k=BLK_STEP)[:, :, 0:WIN - BLK_STEP]
                v.tensor_copy(xstack[:, :, 0:BLK_STEP], main)
                step(v.tensor_copy(xstack[:, :, BLK_STEP:WIN], tail))
                v.tensor_tensor(xstack[:, :, WIN:WIN + BLK_STEP], main, xstack[:, :, 0:BLK_STEP], ALU.subtract)
                v.tensor_tensor(xstack[:, :, WIN + BLK_STEP:2 * WIN], tail, xstack[:, :, BLK_STEP:WIN], ALU.subtract)
                v.tensor_copy(xstack[:, :, 2 * WIN:3 * WIN], xstack[:, :, 0:WIN]).then_inc(S["x_split"], 1)
                pieces = 0
                for n, (kind, args, who) in enumerate(JOBS[TOWER]):
                    g = n
                    if kind == "xt":
                        (i,) = args
                        wait(dve, "ps_full", TOWER, n + 1, b)
                        half = NBLK // 2
                        src = slot(g).bitcast(fp16)[0:3 * WIN, :].rearrange("p (k n) -> p k n", k=2)[:, :, 0:8 * PITCH]
                        dst = xt[:, half * i:half * i + half, :].rearrange("p (k n) c -> p k (n c)", k=2)
                        v.tensor_copy(dst, src).then_inc(S["dve_freed"], 1)
                    elif kind == "stats0":
                        j, i = args
                        wait(dve, "ps_full", TOWER, n + 1, b)
                        for k in range(2):
                            rows = bank(g, k)[:, 0:4 * PITCH].rearrange("p (k c) -> p k c", c=PITCH)
                            if (j, i, k) == (7, 2, 1):
                                v.bn_stats(bn[:, pieces, :], rows[:, 0:3, 0:COLS])
                                last = v.bn_stats(bn[:, pieces + 1, :], rows[:, 3, 0:COLS - 1])
                                pieces += 2
                            else:
                                last = v.bn_stats(bn[:, pieces, :], rows[:, :, 0:COLS])
                                pieces += 1
                        last.then_inc(S["dve_freed"], 1)
                        if (j, i) == (7, 2):
                            last_bn[0] = None
                            dve.wait_ge(S["dve_freed"], at("dve_freed", TOWER, freed(TOWER, DVE_ENGINE, n), b))
                            carry_wait()
                            step(v.bn_aggr(mv[:, :], bn[:, 0:pieces, :].rearrange("p n s -> p (n s)")))
                            step(v.tensor_tensor(ms[:, 0:1], mv[:, 0:1], par[:, 0, 0:1], ALU.add))
                            v.scalar_tensor_tensor(out=ms[:, 1:2], in0=ms[:, 0:1], scalar=ms[:, 0:1],
                                                   in1=mv[:, 1:2], op0=ALU.mult, op1=ALU.add
                                                   ).then_inc(S["channel_stats"], 1)
                            pieces = 0
                    elif kind == "group":
                        (layer,) = args
                        if layer:
                            group_stats(layer, pieces, b)
                            pieces = 0
                        group_affine(layer, g, n, b)
                        if 1 <= layer <= 3:
                            wait(dve, "norm_done", TOWER, norm_chunk_of(layer, 1), b)
                            halo(layer, b)
                    elif kind == "conv":
                        layer, r, cut = args
                        if layer == 1 and r == 0:
                            wait(dve, "act_freed", TOWER, freed(TOWER, ACT_ENGINE, job_index(TOWER, "conv0", (0, 2))), b)
                            halo(0, b)
                        wait(dve, "act_freed", TOWER, freed(TOWER, ACT_ENGINE, n), b)
                        rows = acts[layer].rearrange("p (r c) -> p r c", c=PITCH)
                        for c in cut:
                            if r + c == ROWS[layer]:
                                v.bn_stats(bn[:, pieces, :], rows[:, r:r + c - 1, 0:COLS])
                                last_bn[0] = v.bn_stats(bn[:, pieces + 1, :], rows[:, r + c - 1, 0:COLS - 1])
                                pieces += 2
                            else:
                                last_bn[0] = v.bn_stats(bn[:, pieces, :], rows[:, r:r + c, 0:COLS])
                                pieces += 1
                            r += c
                    elif kind == "embed":
                        wait(dve, "ps_full", TOWER, n + 1, b)
                        take_token_rows(g, args[0], lambda i, k, m: pb_b[0:m, :] if k == 1 else
                                        pb_b[:, :].unsqueeze(1).to_broadcast([128, 2, D]))
                        if args[0] == 1:
                            dve.wait_ge(S["dve_freed"], at("dve_freed", TOWER, freed(TOWER, DVE_ENGINE, n), b))
                            layernorm()
                    elif kind == "tr" and DVE_ENGINE in who:
                        wait(dve, "ps_full", TOWER, n + 1, b)
                        v.tensor_copy(xnt0[:, 0:TOK], slot(g)[:, 0:TOK]).then_inc(S["dve_freed"], 1)
                leave()

                with dve.Fori(0, PAIRS) as pr:
                    enter(PAIR, b, pr)
                    for n, (kind, args, who) in enumerate(JOBS[PAIR]):
                        g = n + SLOT0[PAIR]
                        if kind == "k":
                            wait(dve, "ps_full", PAIR, n + 1, b, pr)
                            src = slot(g).rearrange("p (k n) -> p k n", k=2)[:, :, 0:TOK // 2]
                            v.tensor_scalar(kt[:, 0:TOK].rearrange("p (k n) -> p k n", k=2), src,
                                            bqkv[:, 1, bass.ds(pr, 1)], None, ALU.add).then_inc(S["dve_freed"], 1)
                        elif kind == "s":
                            (k,) = args
                            i = k % TT
                            m = tile_rows(i)
                            wait(dve, "ps_full", PAIR, n + 1, b, pr)
                            step(v.reduce_max(smax[0:m, k:k + 1], slot(g)[0:m, 0:128 * i + m], AX.X))
                            v.tensor_scalar(nmax[0:m, k:k + 1], smax[0:m, k:k + 1], -SCALE, None, ALU.mult
                                            ).then_inc(S["smax_done"], 1)
                        elif kind == "pt":
                            (k,) = args
                            i = k % TT
                            m = tile_rows(i)
                            wait(dve, "ps_full", PAIR, n + 1, b, pr)
                            src = slot(g).rearrange("p (t c) -> p t c", c=128)
                            w = min(i + 1, 4)
                            full = w if i < TT - 1 or w <= 4 else w
                            v.tensor_copy(probt[k % 2][:, 0:full, 0:m], src[:, 0:full, 0:m]).then_inc(S["dve_freed"], 1)
                            wait(dve, "act_freed", PAIR, freed(PAIR, ACT_ENGINE, job_index(PAIR, "s", (k,))), b, pr)
                            v.reciprocal(rinv[0:m, k:k + 1], rsum[0:m, k:k + 1]).then_inc(S["rinv_ready"], 1)
                        elif kind == "zt":
                            wait(dve, "ps_full", PAIR, n + 1, b, pr)
                            v.tensor_scalar(zt[:, bass.ds(pr, 1), 0:TOK].rearrange("p a t -> p (a t)"),
                                            slot(g)[:, 0:TOK], bqkv[:, 2, bass.ds(pr, 1)], None, ALU.add
                                            ).then_inc(S["dve_freed"], 1)
                    leave()

                enter(POST, b)
                for n, (kind, args, who) in enumerate(JOBS[POST]):
                    g = n + SLOT0[POST]
                    if DVE_ENGINE not in who:
                        continue
                    wait(dve, "ps_full", POST, n + 1, b)
                    if kind == "wo":
                        if args[0] == 0:
                            for i in range(TT):
                                m = tile_rows(i)
                                last = v.tensor_tensor(h[0:m, i, :], h[0:m, i, :], bo_b[0:m, :], ALU.add)
                            step(last)
                        take_token_rows(g, args[0], lambda i, k, m: h[0:m, i, :] if k == 1 else h[:, i:i + 2, :])
                        if args[0] == 1:
                            dve.wait_ge(S["dve_freed"], at("dve_freed", POST, freed(POST, DVE_ENGINE, n), b))
                            layernorm()
                            wait(dve, "xn_ready", POST, 1, b)
                            v.memset(spare[:, 2:3], 0.0).then_inc(S["h1_ready"], 1)
                    elif kind == "tr":
                        v.tensor_copy(xnt0[:, 0:TOK], slot(g)[:, 0:TOK]).then_inc(S["dve_freed"], 1)
                    elif kind == "gate":
                        src = bank(g, 0)[:, 0:TT * EXPERTS].rearrange("p (t e) -> p t e", e=EXPERTS)
                        v.tensor_tensor(logits[:, 0:TT - 1, :], src[:, 0:TT - 1, :],
                                        gate_b[:, :].unsqueeze(1).to_broadcast([128, TT - 1, EXPERTS]), ALU.add)
                        v.tensor_tensor(logits[0:LASTM, TT - 1, :], src[0:LASTM, TT - 1, :], gate_b[0:LASTM, :],
                                        ALU.add).then_inc(S["dve_freed"], 1)
                        dve.wait_ge(S["dve_freed"], at("dve_freed", POST, freed(POST, DVE_ENGINE, n), b))
                        step(v.reduce_max(best[:, :], logits[:, :, :], AX.X))
                        step(v.tensor_tensor(pick[:, :, :], logits[:, :, :],
                                             best[:, :].unsqueeze(2).to_broadcast([128, TT, EXPERTS]), ALU.is_ge))
                        step(v.tensor_tensor(pick[:, :, :], pick[:, :, :],
                                             prefer[:, :].unsqueeze(1).to_broadcast([128, TT, EXPERTS]), ALU.mult))
                        step(v.reduce_max(best[:, :], pick[:, :, :], AX.X))
                        step(v.tensor_tensor(pick[:, :, :], pick[:, :, :],
                                             best[:, :].unsqueeze(2).to_broadcast([128, TT, EXPERTS]), ALU.is_ge))
                        v.tensor_copy(onehot[:, bass.ds(b * TT, TT - 1), :], pick[:, 0:TT - 1, :])
                        step(v.tensor_copy(onehot[0:LASTM - 1, bass.ds(b * TT + TT - 1, 1), :],
                                           pick[0:LASTM - 1, TT - 1:TT, :]))
                    else:
                        v.tensor_copy(spare[:, 4 + n:5 + n], bank(g, 0)[:, 0:1]).then_inc(S["dve_freed"], 1)
                leave()

            total = [0]

            def chain(ins_):
                total[0] += 1
                ins_.then_inc(S["dve_step"], 1)
                dve.wait_ge(S["dve_step"], at("dve_step", MOE, total[0]))

            dve.wait_ge(rank_full, 1)
            dve.wait_ge(moe_consts, N_MOE_CONSTS)
            v.tensor_copy(rank, bank(0, 0)[:, 0:TILES * EXPERTS].rearrange("p (t e) -> p t e", e=EXPERTS))
            chain(v.tensor_copy(per_tile.rearrange("p (e t) -> p e t", t=TILES),
                                bank(0, 1)[:, 0:TILES * EXPERTS].rearrange("p (t e) -> p e t", e=EXPERTS)))
            chain(v.tensor_tensor_scan(running, segment, per_tile, 0.0, ALU.mult, ALU.add))
            run_et = running.rearrange("p (e t) -> p e t", t=TILES)
            chain(v.tensor_copy(counts, run_et[:, :, TILES - 1]))
            chain(v.tensor_tensor(over[:, 0:TILES, :].rearrange("p t e -> p e t"),
                                  counts.unsqueeze(2).to_broadcast([128, EXPERTS, TILES]),
                                  edges.unsqueeze(1).to_broadcast([128, EXPERTS, TILES]), ALU.is_gt))
            chain(v.reduce_sum(ntiles, over[:, 0:TILES, :].rearrange("p t e -> p e t"), AX.X))
            chain(v.tensor_tensor_scan(tiles_end, ones[:, 0:EXPERTS], ntiles, 0.0, ALU.mult, ALU.add))
            chain(v.tensor_tensor(base, tiles_end, ntiles, ALU.subtract))
            chain(v.tensor_scalar(base, base, 128.0, None, ALU.mult))
            chain(v.tensor_tensor(running, running, per_tile, ALU.subtract))
            chain(v.tensor_tensor(rank, rank, run_et.rearrange("p e t -> p t e"), ALU.add))
            chain(v.tensor_tensor(rank, rank, base.unsqueeze(1).to_broadcast([128, TILES, EXPERTS]), ALU.add))
            chain(v.tensor_tensor(rank, rank, onehot[:, :, :], ALU.mult))
            chain(v.reduce_sum(slots_f, rank, AX.X))
            v.tensor_copy(slots, slots_f).then_inc(slots_ready, 1)
            chain(v.tensor_tensor(over, tiles_end.unsqueeze(1).to_broadcast([128, 32, EXPERTS]),
                                  tile_ids.unsqueeze(2).to_broadcast([128, 32, EXPERTS]), ALU.is_le))
            chain(v.reduce_sum(tile_expert_f, over, AX.X))
            chain(v.tensor_scalar(tile_expert_f, tile_expert_f, float(EXPERTS - 1), None, ALU.min))
            v.tensor_copy(tile_expert, tile_expert_f).then_inc(slots_ready, 1)

            def take_xt(j):
                dve.wait_ge(xt_full, j + 1)
                v.tensor_copy(xe0, bank(0, 0)[:, 0:128])
                v.tensor_copy(xe1[0:D1, :], bank(0, 1)[0:D1, 0:128]).then_inc(xt_taken, 1)

            def take_hidt(j):
                dve.wait_ge(hidt_full, j + 1)
                v.tensor_copy(hidt[:, 0:4, :], bank(2, 0).rearrange("p (c t) -> p c t", c=4)
                              ).then_inc(hidt_taken_dve, 1)

            def take_y(j, first=False):
                dve.wait_ge(y_full, j + 1)
                if not first:
                    dve.wait_ge(y_stored, 16 * j)
                v.tensor_copy(ytile, bank(3, 0)[:, 0:D]).then_inc(y_taken, 1)

            take_xt(0)
            take_xt(1)
            take_hidt(0)
            take_xt(2)
            take_y(0, first=True)
            take_hidt(1)
            with dve.Fori(2, SLOT_TILES - 1) as j:
                take_xt(j + 1)
                take_y(j - 1)
                take_hidt(j)
            take_y(SLOT_TILES - 2)
            take_hidt(SLOT_TILES - 1)
            take_y(SLOT_TILES - 1)

            dve.wait_ge(gathered, 16 * TILES)
            for b in range(BATCH):
                t = b * TT
                v.tensor_tensor(h1[:, t:t + TT - 1, :], h1[:, t:t + TT - 1, :], y_tok[:, t:t + TT - 1, :], ALU.add)
                m = LASTM - 1
                v.tensor_tensor(h1[0:m, t + TT - 1, :], h1[0:m, t + TT - 1, :], y_tok[0:m, t + TT - 1, :], ALU.add
                                ).then_inc(out_ready, 1)

        @block.tensor
        def _(pe):
            t = nc.tensor

            def slot_free(phase, n, b=None, pr=None):
                if phase == SETUP and n < 4:
                    return
                if phase != SETUP and n == 0:
                    wait(pe, "act_freed", phase, 0, b, pr)
                    wait(pe, "dve_freed", phase, 0, b, pr)
                if n >= 4:
                    for engine, name in ((ACT_ENGINE, "act_freed"), (DVE_ENGINE, "dve_freed")):
                        if engine in JOBS[phase][n - 4][2]:
                            wait(pe, name, phase, freed(phase, engine, n - 4), b, pr)

            pe.wait_ge(consts_ready, N_CONSTS)
            pe.wait_ge(weights_loaded, 16 * n_weight_dmas)
            for n, (kind, args, who) in enumerate(JOBS[SETUP]):
                slot_free(SETUP, n)
                if kind == "cwt":
                    (l,) = args
                    taps = 2 if l == 5 else 3
                    w = cwn[l].rearrange("p (i k) -> p k i", k=taps)
                    for k in range(taps):
                        last = t.transpose(bank(n, 0)[:, k * CH:(k + 1) * CH], w[:, k, :], ident[:, :])
                elif kind == "cw0t":
                    pe.wait_ge(cw0_stacked, 1)
                    dst = bank(n, 0).bitcast(fp16)
                    for m in range(SUB):
                        last = t.transpose(dst[0:3 * WIN, m * CH:(m + 1) * CH], cw0pad[:, m, :], ident_h[:, :])
                elif kind == "pwt":
                    t.transpose(bank(n, 0)[:, 0:128], pwn[:, 0, :], ident[:, :])
                    last = t.transpose(bank(n, 0)[:, 128:D], pwn[0:D1, 1, :], ident[0:D1, 0:D1])
                else:
                    last = t.transpose(bank(n, 0)[:, 0:128], ident[:, :], ident[:, :])
                last.then_inc(S["ps_full"], 1)

            def token_transposes(g, part):
                for i in range(TT):
                    m = tile_rows(i)
                    if part == 0:
                        last = t.transpose(slot(g)[:, 128 * i:128 * i + m], xn[0:m, i, 0:128], ident[0:m, 0:m])
                    else:
                        last = t.transpose(slot(g)[0:D1, 128 * i:128 * i + m], xn[0:m, i, 128:D], ident[0:m, 0:m])
                return last

            with pe.Fori(0, BATCH) as b:
                for n, (kind, args, who) in enumerate(JOBS[TOWER]):
                    g = n
                    if (kind, args) != ("tr", (1,)):
                        slot_free(TOWER, n, b)
                    if (kind, args) == ("tr", (0,)):
                        slot_free(TOWER, n + 1, b)
                    if kind == "xt":
                        if args[0] == 0:
                            wait(pe, "x_split", TOWER, 1, b)
                        half = NBLK // 2
                        for i in range(half):
                            dst = bank(g, i // 8).bitcast(fp16)[0:3 * WIN, (i % 8) * PITCH:(i % 8 + 1) * PITCH]
                            last = t.transpose(dst, xstack[:, half * args[0] + i, :], ident_h[0:PITCH, 0:PITCH])
                    elif kind in ("stats0", "conv0"):
                        j, i = args
                        if kind == "stats0" and args == (0, 0):
                            wait(pe, "dve_freed", TOWER, freed(TOWER, DVE_ENGINE, 1), b)
                        for k in range(2):
                            last = t.matmul(bank(g, k)[:, 0:4 * PITCH], cw0t[:, 2 * i + k, :],
                                            xt[:, 4 * j:4 * j + 4, :].rearrange("p k c -> p (k c)"),
                                            start=True, stop=True)
                    elif kind == "group":
                        wait(pe, "channel_stats", TOWER, args[0] + 1, b)
                        last = t.matmul(bank(g, 0)[:, 0:2], group_avg[:, :], ms[:, :], start=True, stop=True)
                    elif kind == "conv":
                        layer, r, cut = args
                        taps = 2 if layer == 5 else 3
                        src = acts[layer - 1].rearrange("p (r c) -> p r c", c=PITCH)
                        need = 2 * (r + sum(cut)) - 2 + taps - 1
                        if need >= ROWS[layer - 1]:
                            wait(pe, "halo_done", TOWER, layer, b)
                            need = ROWS[layer - 1] - 1
                        if layer == 1:
                            done = job_index(TOWER, "conv0", (need // 24, 2))
                            wait(pe, "act_freed", TOWER, freed(TOWER, ACT_ENGINE, done), b)
                        else:
                            wait(pe, "norm_done", TOWER, norm_chunk_of(layer - 1, need), b)
                        for k, c in enumerate(cut):
                            for tap in range(taps):
                                f = 2 * r + tap
                                last = t.matmul(bank(g, k)[:, 0:c * PITCH].rearrange("p (r c) -> p r c", c=PITCH),
                                                cwt[layer][:, tap, :], src[:, f:f + 2 * c - 1:2, :],
                                                start=tap == 0, stop=tap == taps - 1)
                            r += c
                    elif kind == "embed":
                        if args[0] == 0:
                            wait(pe, "norm_done", TOWER, 14, b)
                        tiles = range(4) if args[0] == 0 else range(4, TT)
                        for q, i in enumerate(tiles):
                            m = tile_rows(i)
                            last = t.matmul(bank(g, q // 2)[0:m, (q % 2) * D:(q % 2 + 1) * D],
                                            h5t[:, 128 * i:128 * i + m], pwt[:, :], start=True, stop=True)
                    else:
                        assert kind == "tr"
                        if args[0] == 0:
                            wait(pe, "xn_ready", TOWER, 1, b)
                        last = token_transposes(g, args[0])
                    last.then_inc(S["ps_full"], 1)

                with pe.Fori(0, PAIRS) as pr:
                    for n, (kind, args, who) in enumerate(JOBS[PAIR]):
                        g = n + SLOT0[PAIR]
                        slot_free(PAIR, n, b, pr)
                        if kind in ("q", "k"):
                            if kind == "q":
                                wait(pe, "w_loaded", PAIR, 0, b, pr)
                            w = 0 if kind == "q" else 1
                            for k in range(2):
                                cols = slice(k * TOK // 2, (k + 1) * TOK // 2)
                                t.matmul(bank(g, k)[:, 0:TOK // 2], wqkv0[:, w, :], xnt0[:, cols], start=True,
                                         stop=False)
                                last = t.matmul(bank(g, k)[:, 0:TOK // 2], wqkv1[:, w, :], xnt1[0:D1, cols],
                                                start=False, stop=True)
                        elif kind == "v":
                            for i in range(TT):
                                m = tile_rows(i)
                                dst = slot(g)[0:m, 128 * i:128 * i + 128]
                                t.matmul(dst, xnt0[:, 128 * i:128 * i + m], wqkv0[:, 2, :], start=True, stop=False)
                                last = t.matmul(dst, xnt1[0:D1, 128 * i:128 * i + m], wqkv1[:, 2, :], start=False,
                                                stop=True)
                        elif kind == "s":
                            (k,) = args
                            i, hh = k % TT, k // TT
                            m = tile_rows(i)
                            if k == 0:
                                wait(pe, "act_freed", PAIR, 2, b, pr)
                                wait(pe, "dve_freed", PAIR, 1, b, pr)
                            head = slice(DH * hh, DH * hh + DH)
                            q = qt[head, 128 * i:128 * i + m]
                            end = 128 * i + m
                            for lo in range(0, end, 512):
                                hi = min(lo + 512, end)
                                diagonal = lo <= 128 * i < hi
                                last = t.matmul(slot(g)[0:m, lo:hi], q, kt[head, lo:hi], start=True,
                                                stop=not diagonal)
                                if diagonal:
                                    last = t.matmul(slot(g)[0:m, 128 * i:end], ident_b[0:m, 0:m],
                                                    causal_b[0:m, 0:m], start=False, stop=True)
                        elif kind == "pt":
                            (k,) = args
                            i = k % TT
                            m = tile_rows(i)
                            wait(pe, "act_freed", PAIR, freed(PAIR, ACT_ENGINE, job_index(PAIR, "s", (k,))), b, pr)
                            for c in range(i + 1):
                                kk = tile_rows(c)
                                last = t.transpose(slot(g)[0:kk, 128 * c:128 * c + m],
                                                   prob[k % 2][0:m, 128 * c:128 * c + kk], ident[0:m, 0:m])
                        elif kind == "z":
                            (k,) = args
                            i, hh = k % TT, k // TT
                            m = tile_rows(i)
                            done = job_index(PAIR, "pt", (k,))
                            wait(pe, "dve_freed", PAIR, freed(PAIR, DVE_ENGINE, done), b, pr)
                            if i >= 4:
                                wait(pe, "act_freed", PAIR, freed(PAIR, ACT_ENGINE, done), b, pr)
                            for c in range(i + 1):
                                kk = tile_rows(c)
                                last = t.matmul(slot(g)[0:m, 0:DH], probt[k % 2][0:kk, c, 0:m],
                                                vt[0:kk, c, DH * hh:DH * hh + DH], start=c == 0, stop=c == i)
                        else:
                            assert kind == "zt"
                            wait(pe, "act_freed", PAIR, freed(PAIR, ACT_ENGINE, n - 1), b, pr)
                            for i in range(TT):
                                m = tile_rows(i)
                                last = t.transpose(slot(g)[:, 128 * i:128 * i + m], z[0:m, i, :], ident[0:m, 0:m])
                        last.then_inc(S["ps_full"], 1)

                for n, (kind, args, who) in enumerate(JOBS[POST]):
                    g = n + SLOT0[POST]
                    if (kind, args) != ("tr", (1,)):
                        slot_free(POST, n, b)
                    if (kind, args) == ("tr", (0,)):
                        slot_free(POST, n + 1, b)
                    if kind == "wo":
                        tiles = range(4) if args[0] == 0 else range(4, TT)
                        for q, i in enumerate(tiles):
                            m = tile_rows(i)
                            for a in range(PAIRS):
                                last = t.matmul(bank(g, q // 2)[0:m, (q % 2) * D:(q % 2 + 1) * D],
                                                zt[:, a, 128 * i:128 * i + m], wo[:, a, :], start=a == 0,
                                                stop=a == PAIRS - 1)
                    elif kind == "tr":
                        if args[0] == 0:
                            wait(pe, "xn_ready", POST, 1, b)
                        last = token_transposes(g, args[0])
                    elif kind == "gate":
                        wait(pe, "dve_freed", POST, freed(POST, DVE_ENGINE, n - 1), b)
                        wait(pe, "act_freed", POST, freed(POST, ACT_ENGINE, n - 1), b)
                        for i in range(TT):
                            m = tile_rows(i)
                            dst = bank(g, 0)[0:m, EXPERTS * i:EXPERTS * (i + 1)]
                            t.matmul(dst, xnt0[:, 128 * i:128 * i + m], gw0[:, :], start=True, stop=False)
                            last = t.matmul(dst, xnt1[0:D1, 128 * i:128 * i + m], gw1[:, :], start=False, stop=True)
                    else:
                        last = t.transpose(bank(g, 0)[:, 0:128], ident[:, :], ident[:, :])
                    last.then_inc(S["ps_full"], 1)

            wait(pe, "dve_step", MOE, 0)
            wait(pe, "act_freed", MOE, 0)
            wait(pe, "dve_freed", MOE, 0)
            pe.wait_ge(moe_consts, 3)
            choice = onehot[:, :, :].rearrange("p t e -> p (t e)")
            t.matmul(bank(0, 0)[:, 0:TILES * EXPERTS], before, choice, start=True, stop=True)
            t.matmul(bank(0, 1)[:, 0:TILES * EXPERTS], ones, choice, start=True, stop=True).then_inc(rank_full, 1)
            pe.wait_ge(slots_ready, 2)

            def make_xt(j):
                pe.wait_ge(xtile_loaded, 16 * j + 16)
                t.transpose(bank(0, 0)[:, 0:128], xtile[:, 0:128], ident[:, :])
                t.transpose(bank(0, 1)[0:D1, 0:128], xtile[:, 128:D], ident[:, :]).then_inc(xt_full, 1)

            def make_hidden(e, j):
                pe.wait_ge(xt_taken, j + 1)
                for k in range(2):
                    f = slice(k * FF // 2, (k + 1) * FF // 2)
                    wa = w1a[:, bass.ds(e, 1), f].rearrange("p a f -> p (a f)")
                    wb = w1b[0:D1 + 1, bass.ds(e, 1), f].rearrange("p a f -> p (a f)")
                    t.matmul(bank(1, k)[:, 0:FF // 2], xe0, wa, start=True, stop=False)
                    last = t.matmul(bank(1, k)[:, 0:FF // 2], xe1[0:D1 + 1, :], wb, start=False, stop=True)
                last.then_inc(hid_full, 1)

            def make_hidt(j):
                pe.wait_ge(hid_taken, j + 1)
                for c in range(FF // 128):
                    last = t.transpose(slot(2)[:, 128 * c:128 * c + 128], hid[:, 128 * c:128 * c + 128], ident[:, :])
                last.then_inc(hidt_full, 1)

            def make_y(e, j, first=False):
                pe.wait_ge(hidt_taken_dve, j + 1)
                pe.wait_ge(hidt_taken_act, j + 1)
                if not first:
                    pe.wait_ge(y_taken, j)
                dst = bank(3, 0)[:, 0:D]
                for c in range(FF // 128):
                    w = w2[:, bass.ds(e, 1), c, :].rearrange("p a d -> p (a d)")
                    t.matmul(dst, hidt[:, c, :], w, start=c == 0, stop=False)
                t.matmul(dst, ones[0:1, :], b2[0:1, bass.ds(e, 1), :].rearrange("p a d -> p (a d)"), start=False,
                         stop=True).then_inc(y_full, 1)

            def expert_of(j):
                return pe.value_load(tile_expert[0:1, bass.ds(j, 1)] if not isinstance(j, int)
                                     else tile_expert[0:1, j:j + 1], min_val=0, max_val=EXPERTS - 1)

            pe.wait_ge(moe_consts, N_MOE_CONSTS)
            make_xt(0)
            pe.wait_ge(experts_loaded, 16 * (3 * EXPERTS + 2))
            make_hidden(expert_of(0), 0)
            make_xt(1)
            make_hidt(0)
            make_hidden(expert_of(1), 1)
            make_xt(2)
            make_y(expert_of(0), 0, first=True)
            make_hidt(1)
            with pe.Fori(2, SLOT_TILES - 1) as j:
                make_hidden(expert_of(j), j)
                make_xt(j + 1)
                make_y(expert_of(j - 1), j - 1)
                make_hidt(j)
            last_tile = SLOT_TILES - 1
            make_hidden(expert_of(last_tile), last_tile)
            make_y(expert_of(last_tile - 1), last_tile - 1)
            make_hidt(last_tile)
            make_y(expert_of(last_tile), last_tile)


_INS = (["x"] + [f"L0_tok_{p}{l}" for l in range(CONV_LAYERS) for p in ("cw", "cb", "gw", "gb")]
        + ["L0_tok_pw", "L0_tok_pb"] + [f"L0_attn_{p}_{q}" for q in "QKVO" for p in ("W", "b")]
        + ["L0_ffn_gate_w", "L0_ffn_gate_b", "L0_ffn_w1", "L0_ffn_b1", "L0_ffn_w2", "L0_ffn_b2"])


def kernel(**inputs):
    import concourse.bacc as bacc
    from concourse.bass_utils import run_bass_kernel_spmd

    nc = bacc.Bacc("TRN2", target_bir_lowering=False, num_devices=1)
    arrays, args = {}, {}
    for name in _INS:
        a = np.ascontiguousarray(inputs[name])
        arrays[f"in_{name}"] = a
        args[name] = nc.dram_tensor(f"in_{name}", a.shape, mybir.dt.from_np(a.dtype), kind="ExternalInput").ap()
    out = nc.dram_tensor("out", (BATCH, SEQ, D), mybir.dt.float32, kind="ExternalOutput").ap()
    audio_tower(nc, args, out)
    r = run_bass_kernel_spmd(nc, [arrays], core_ids=[0])
    return r.results[0]["out"]
```

```python
from contextlib import ExitStack

import numpy as np
import concourse.bass as bass
from concourse import mybir

BATCH, SAMPLES = 4, 120000
COLS, PITCH = 125, 126
ROWS = [192, 96, 48, 24, 12, 6]
CONV_LAYERS, CH, GROUP = 6, 128, 4
TAPS0, STRIDE0 = 10, 5
PER_COL = SAMPLES // COLS
SUB, NBLK = 6, 32
WIN = STRIDE0 * (SUB - 1) + TAPS0
WSCALE = 64.0
BLK_STEP = SUB * STRIDE0
D, HEADS, DH, EXPERTS, FF = 192, 12, 64, 8, 768
D1 = D - 128
PAIRS = HEADS // 2
TOK = ROWS[5] * COLS
SEQ = TOK - 1
TT = -(-TOK // 128)
LASTM = TOK - 128 * (TT - 1)
TILES = BATCH * TT
SLOT_TILES = (BATCH * SEQ + EXPERTS * 127) // 128
EPS = 1e-5
SCALE = DH ** -0.5
MASKED = -8.0e5
ACT_ENGINE, DVE_ENGINE = "act", "dve"


def tile_rows(i):
    return LASTM if i == TT - 1 else 128


def tower_jobs():
    jobs = [("xt", (i,), (DVE_ENGINE,)) for i in range(2)]
    jobs += [("gram", (), (DVE_ENGINE,)), ("taps", (), (DVE_ENGINE,)), ("chan", (), (DVE_ENGINE,))]
    jobs.append(("group", (0,), (DVE_ENGINE,)))
    t = 0
    for j in range(8):
        jobs += [("conv0", (j, i), (ACT_ENGINE,)) for i in range(3)]
        while t < ROWS[1] // 8 and min(16 * t + 16, ROWS[0] - 1) // 24 <= j - 1:
            jobs.append(("conv", (1, 8 * t, (4, 4)), (ACT_ENGINE,)))
            t += 1
    while t < ROWS[1] // 8:
        jobs.append(("conv", (1, 8 * t, (4, 4)), (ACT_ENGINE,)))
        t += 1
    jobs.append(("group", (1,), (DVE_ENGINE,)))
    for layer in range(2, CONV_LAYERS):
        r = 0
        while r < ROWS[layer]:
            cut = (3, 3) if layer == 5 else (4, 4) if ROWS[layer] - r >= 8 else (4,)
            jobs.append(("conv", (layer, r, cut), (ACT_ENGINE,)))
            r += sum(cut)
        jobs.append(("group", (layer,), (DVE_ENGINE,)))
    jobs += [("embed", (0,), (DVE_ENGINE,)), ("embed", (1,), (DVE_ENGINE,))]
    jobs += [("xtr", (0,), (DVE_ENGINE,)), ("xtr", (1,), (ACT_ENGINE,)), ("xtr", (2,), (DVE_ENGINE,))]
    jobs += [("q", (), (ACT_ENGINE,)), ("k", (), (ACT_ENGINE,)), ("v", (), (ACT_ENGINE,))]
    jobs += [("s", (k,), (ACT_ENGINE,)) for k in range(2)]
    return jobs


PROBS = 3
Z_AT = TT * 128
STEPS = 2 * TT


def pair_jobs(last):
    jobs = []
    for k in range(STEPS):
        ahead = k + 2
        if ahead < STEPS:
            jobs.append(("s", (ahead,), (ACT_ENGINE,)))
        elif ahead == STEPS + 1 and not last:
            jobs.append(("s", (STEPS,), (ACT_ENGINE,)))
        if k in (TT - 1, TT) and not last:
            jobs.append(("q" if k == TT - 1 else "k", (), (ACT_ENGINE,)))
        jobs.append(("pt", (k,), (DVE_ENGINE, ACT_ENGINE) if k % TT >= 4 else (DVE_ENGINE,)))
        if k:
            jobs.append(("z", (k - 1,), (ACT_ENGINE,)))
    if not last:
        jobs.append(("s", (STEPS + 1,), (ACT_ENGINE,)))
    jobs.append(("z", (STEPS - 1,), (ACT_ENGINE,)))
    if not last:
        jobs.append(("v", (), (ACT_ENGINE,)))
    jobs.append(("zt", (), (DVE_ENGINE,)))
    return jobs


def post_jobs():
    return [("wo", (0,), (DVE_ENGINE,)), ("wo", (1,), (DVE_ENGINE,)),
            ("tr", (0,), (DVE_ENGINE,)), ("tr", (1,), (ACT_ENGINE,)),
            ("gate", (), (DVE_ENGINE,)), ("pad", (), (DVE_ENGINE,))]


def setup_jobs():
    return [("cwt", (1,), (DVE_ENGINE,)), ("cwt", (2,), (DVE_ENGINE,)), ("cwt", (3,), (DVE_ENGINE,)),
            ("cwt", (4,), (DVE_ENGINE,)), ("cwt", (5,), (DVE_ENGINE,)), ("cw0t", (), (ACT_ENGINE,)),
            ("pwt", (), (ACT_ENGINE,)), ("pad", (), (ACT_ENGINE,))]


SETUP, TOWER, PAIR, LAST_PAIR, POST, MOE = range(6)
JOBS = {SETUP: setup_jobs(), TOWER: tower_jobs(), PAIR: pair_jobs(False), LAST_PAIR: pair_jobs(True),
        POST: post_jobs()}


def ring_length(phase):
    return sum(job[0] != "z" for job in JOBS[phase])


while (ring_length(TOWER) + ring_length(LAST_PAIR) + ring_length(POST)) % 4:
    JOBS[POST].append(("pad", (), (DVE_ENGINE,)))
assert ring_length(SETUP) % 4 == 0 and ring_length(PAIR) % 4 == 0
PHASES = (SETUP, TOWER, PAIR, LAST_PAIR, POST)


def ring_positions(phase):
    positions, r, of_pt = [], 0, {}
    for kind, args, _ in JOBS[phase]:
        if kind == "z":
            positions.append(of_pt[args])
            continue
        if kind == "pt":
            of_pt[args] = r
        positions.append(r)
        r += 1
    return positions


RING = {f: ring_positions(f) for f in PHASES}
RING0 = {SETUP: 0, TOWER: 0, PAIR: ring_length(TOWER), LAST_PAIR: ring_length(TOWER),
         POST: ring_length(TOWER) + ring_length(LAST_PAIR)}


def slot_of(phase, n):
    return RING0[phase] + RING[phase][n]


def readers(phase, engine):
    return sum(engine in job[2] for job in JOBS[phase])


NORM_CHUNKS = {1: [9] + [8] * 10 + [7], 2: [9] + [8] * 4 + [7], 3: [9, 8, 7], 4: [9, 3], 5: [6]}
SPLITS = [(0, d) for d in range(24)] + [(l, c) for l in range(1, 5) for c in range(len(NORM_CHUNKS[l]))]
STAGES = 4


def low_engine(layer, piece):
    if layer == 0:
        return DVE_ENGINE if piece % 3 == 2 else "pool"
    return "pool" if piece % 2 else DVE_ENGINE


COUNTS = {
    "ps_full": tuple(len(JOBS[f]) for f in PHASES),
    "act_freed": tuple(readers(f, ACT_ENGINE) for f in PHASES),
    "dve_freed": tuple(readers(f, DVE_ENGINE) for f in PHASES),
    "x_loaded": (32, 32, 0, 0, 0),
    "var_ready": (0, CONV_LAYERS + 1, 0, 0, 1),
    "rstd_ready": (0, CONV_LAYERS + 1, 0, 0, 1),
    "x_split": (1, 1, 0, 0, 0),
    "channel_stats": (0, CONV_LAYERS, 0, 0, 0),
    "affine_ready": (0, CONV_LAYERS, 0, 0, 0),
    "norm_done": (0, sum(len(c) for c in NORM_CHUNKS.values()), 0, 0, 0),
    "hi_done": (0, len(SPLITS), 0, 0, 0),
    "lo_dve": (0, sum(low_engine(*u) == DVE_ENGINE for u in SPLITS), 0, 0, 0),
    "lo_pool": (0, sum(low_engine(*u) == "pool" for u in SPLITS), 0, 0, 0),
    "halo_done": (0, 4, 0, 0, 0),
    "xn_ready": (0, 1, 0, 0, 1),
    "w_loaded": (288, 144, 144, 0, 0),
    "w_split": (1, 1, 1, 0, 0),
    "w_step": (1, 1, 1, 0, 0),
    "xn_high": (0, 1, 0, 0, 0),
    "q_high": (0, 0, 1, 0, 0),
    "k_high": (0, 0, 1, 0, 0),
    "parts_ready": (0, 1, 1, 0, 0),
    "head0_stacked": (0, 64, 64, 0, 0),
    "head1_stacked": (0, 64, 64, 0, 0),
    "smax_done": (0, 2, STEPS, STEPS - 2, 0),
    "rinv_ready": (0, 0, STEPS, STEPS, 0),
    "h1_ready": (0, 0, 0, 0, 1),
    "scratch_stored": (16, 0, 0, 0, 64),
    "dve_step": (7, 42, STEPS, STEPS - 2, 9),
}
def lows(engine, unit):
    return sum(low_engine(*u) == engine for u in SPLITS[:SPLITS.index(unit) + 1])


def split_unit_of(layer, row):
    if layer == 0:
        return (0, 3 * (row // 24) + 2)
    return (layer, next(c for c in range(len(NORM_CHUNKS[layer])) if row < sum(NORM_CHUNKS[layer][:c + 1])))


def at(sem, phase, k, b=None, pr=None):
    setup, *each = COUNTS[sem]
    tower, pair, last_pair, post = each
    before_last = tower + (PAIRS - 1) * pair
    if phase == SETUP:
        return k
    period = before_last + last_pair + post
    if phase == MOE:
        return setup + BATCH * period + k
    base = b * period + setup
    if phase == PAIR:
        return base + pr * pair + (tower + k) if pair else base + (tower + k)
    return base + ({TOWER: 0, LAST_PAIR: before_last, POST: before_last + last_pair}[phase] + k)


def act_order(phase):
    order, held = [], None
    for n, (kind, args, who) in enumerate(JOBS[phase]):
        if ACT_ENGINE not in who:
            continue
        if kind == "s" and phase in (PAIR, LAST_PAIR):
            if held is not None:
                order.append(held)
            held = n
            continue
        order.append(n)
        if kind == "z" and held is not None:
            order.append(held)
            held = None
    assert held is None
    return order


ACT_ORDER = {f: act_order(f) for f in PHASES}


def freed(phase, engine, n):
    if engine == ACT_ENGINE and phase in (PAIR, LAST_PAIR):
        return ACT_ORDER[phase].index(n) + 1
    return sum(engine in job[2] for job in JOBS[phase][:n + 1])


def norm_chunk_of(layer, row):
    before = sum(len(NORM_CHUNKS[i]) for i in range(1, layer))
    edge = 0
    for n, rows in enumerate(NORM_CHUNKS[layer]):
        edge += rows
        if row < edge:
            return before + n + 1


def job_index(phase, kind, args):
    return next(n for n, job in enumerate(JOBS[phase]) if job[0] == kind and job[1] == args)


def exp_done(phase, k):
    if k < 2 and phase != TOWER:
        return k - 1
    return freed(phase, ACT_ENGINE, job_index(phase, "s", (k,)))


def transposed_before(phase, k):
    if k < 0:
        return job_index(PAIR, "pt", (k + STEPS,)) + 1 - len(JOBS[PAIR])
    return job_index(phase, "pt", (k,)) + 1


def audio_tower(nc, ins, out):
    fp32, fp16, bf16, i32 = mybir.dt.float32, mybir.dt.float16, mybir.dt.bfloat16, mybir.dt.int32
    ALU, ACT, AX = mybir.AluOpType, mybir.ActivationFunctionType, mybir.AxisListType

    h1_dram = nc.dram_tensor("h1_scratch", (TILES, 128, D), fp32, kind="Internal").ap()
    x2_dram = nc.dram_tensor("x2_scratch", (TILES, 128, D), fp32, kind="Internal").ap()
    xslot_dram = nc.dram_tensor("xslot_scratch", (SLOT_TILES * 128, D), fp32, kind="Internal").ap()
    yslot_dram = nc.dram_tensor("yslot_scratch", (SLOT_TILES * 128, D), fp32, kind="Internal").ap()

    ctx = ExitStack()
    with ctx:
        def sb(name, shape, dt=fp32):
            return ctx.enter_context(nc.sbuf_tensor(name, shape, dt))

        def sem(name):
            return ctx.enter_context(nc.semaphore(name))

        ident = sb("ident", [128, 128])
        ident_h = sb("ident_h", [128, 128], fp16)
        ident_b = sb("ident_b", [128, 128], bf16)
        causal_b = sb("causal_b", [128, 128], bf16)
        group_avg = sb("group_avg", [128, 128])
        cwt = [None] + [sb(f"cwt{l}", [CH, 2, 2 if l == 5 else 3, CH], fp16) for l in range(1, CONV_LAYERS)]
        cw0t = sb("cw0t", [3 * WIN, SUB, CH], fp16)
        cw0n = sb("cw0n", [CH, TAPS0])
        cw0s = sb("cw0s", [CH, TAPS0])
        cw0f = sb("cw0f", [TAPS0, CH])
        gram = sb("gram", [WIN, WIN + 1])
        tap_sums = sb("tap_sums", [TAPS0, TAPS0 + 1])
        quad = sb("quad", [CH, TAPS0])
        ones_col = sb("ones_col", [128, 1])
        wscale_col = sb("wscale_col", [128, 1])
        pwt = sb("pwt", [CH, D])
        par = sb("par", [CH, 3, CONV_LAYERS])
        pb_b = sb("pb_b", [128, D])
        bo_b = sb("bo_b", [128, D])
        gate_b = sb("gate_b", [128, EXPERTS])
        gw0 = sb("gw0", [128, EXPERTS])
        gw1 = sb("gw1", [D1, EXPERTS])
        wo = sb("wo", [128, PAIRS, D])
        bqkv = sb("bqkv", [128, 3, PAIRS])
        wqkv0 = sb("wqkv0", [128, 3, 128])
        wqkv1 = sb("wqkv1", [128, 3, 128])
        w0_parts = sb("w0_parts", [128, 2, 3, 128], fp16)
        w1_high = sb("w1_high", [128, 3, 128], fp16)
        w1_low = sb("w1_low", [D1, 3, 128], fp16)
        onehot = sb("onehot", [128, TILES, EXPERTS])
        prefer = sb("prefer", [128, EXPERTS])
        bn = sb("bn", [128, 49, 6])
        mv = sb("mv", [128, 2])
        ms = sb("ms", [128, 2])
        gm = sb("gm", [128, 2])
        tmp = sb("tmp", [128, 4])
        spare = sb("spare", [128, 16])
        affine = sb("affine", [128, 2])
        lnmv = sb("lnmv", [128, TT, 2])
        lnr = sb("lnr", [128, TT])
        lnv = sb("lnv", [128, TT])
        neg_half = sb("neg_half", [128, TT])
        smax = sb("smax", [128, STEPS])
        nmax = sb("nmax", [128, STEPS])
        rsum = sb("rsum", [128, STEPS])
        rinv = sb("rinv", [128, STEPS])
        logits = sb("logits", [128, TT, EXPERTS])
        pick = sb("pick", [128, TT, EXPERTS])
        best = sb("best", [128, TT])
        zeros = sb("zeros", [128, D])
        xa = sb("xa", [PITCH, PER_COL + BLK_STEP + 2])
        xstack = sb("xstack", [PITCH, NBLK, 3 * WIN], fp16)
        xt = sb("xt", [3 * WIN, NBLK, PITCH], fp16)

        H0, Y1 = (ROWS[0] + 1) * PITCH, (ROWS[1] + 1) * PITCH
        STAGE = 8 * PITCH
        ARENA = H0 + Y1 + STAGES * STAGE
        arena = sb("arena", [128, ARENA])
        stage = arena[:, H0 + Y1:ARENA].rearrange("p (s n) -> p s n", s=STAGES)

        def rows_at(first, layer):
            return arena[:, first:first + (ROWS[layer] + 1) * PITCH]

        Y2, Y3, Y4, Y5 = Y1, H0 + 49 * PITCH, 30 * PITCH, H0 + 80 * PITCH
        ys = [None, rows_at(H0, 1), rows_at(Y2, 2), rows_at(Y3, 3), rows_at(Y4, 4), rows_at(Y5, 5)]
        hs = []
        for l, first in enumerate((0, 0, H0, 0, H0)):
            both = rows_at(first, l).bitcast(fp16)
            n = (ROWS[l] + 1) * PITCH
            hs.append((both[:, 0:n], both[:, n:2 * n]))
        cursor = [0]

        def take(n):
            a = arena[:, cursor[0]:cursor[0] + n]
            cursor[0] += n
            return a

        h5t = take(TOK)
        h = take(TT * D).rearrange("p (t d) -> p t d", d=D)
        xn = take(TT * D).rearrange("p (t d) -> p t d", d=D)
        xn_parts = take(TT * D).bitcast(fp16).rearrange("p (t a d) -> p t a d", t=TT, a=3)
        xt_parts = take(3 * TOK // 2).bitcast(fp16).rearrange("p (a t) -> p a t", a=3)
        q_full, k_full = take(TOK), take(TOK)
        xnt0 = take(TT * 128)
        xnt1 = take(TT * 128)
        q_parts = take(TOK).bitcast(fp16).rearrange("p (a t) -> p a t", a=2)
        k_parts = take(TOK).bitcast(fp16).rearrange("p (a t) -> p a t", a=2)
        q_stack = take(TOK).bitcast(fp16).rearrange("p (h t) -> p h t", h=2)
        k_stack = take(2 * TOK).bitcast(fp16).rearrange("p (h a t) -> p h a t", h=2, a=2)
        vt = take(TT * 128).rearrange("p (t c) -> p t c", c=128)
        prob = [take(TT * 128) for _ in range(PROBS)]
        probt = [take(TT * 128).rearrange("p (t c) -> p t c", c=128) for _ in range(2)]
        z = take(TT * 128).rearrange("p (t c) -> p t c", c=128)
        zt = take(PAIRS * TT * 128).rearrange("p (a t) -> p a t", a=PAIRS)
        assert cursor[0] <= ARENA

        cursor[0] = 0
        cwn = [None] + [take((2 if l == 5 else 3) * CH) for l in range(1, CONV_LAYERS)]
        cw0pad = take(SUB * 3 * WIN // 2).bitcast(fp16).rearrange("p (m k) -> p m k", m=SUB)
        pwn = take(2 * CH).rearrange("p (a c) -> p a c", a=2)

        cursor[0] = 0
        w1a = take(EXPERTS * FF).rearrange("p (e f) -> p e f", e=EXPERTS)
        w1b = take(EXPERTS * FF).rearrange("p (e f) -> p e f", e=EXPERTS)
        w2 = take(EXPERTS * PAIRS * D).rearrange("p (e c d) -> p e c d", e=EXPERTS, c=FF // 128)
        b2 = take(EXPERTS * D).rearrange("p (e d) -> p e d", e=EXPERTS)
        h1 = take(TILES * D).rearrange("p (t d) -> p t d", d=D)
        x2 = take(TILES * D).rearrange("p (t d) -> p t d", d=D)
        before = take(128)
        ones = take(128)
        rank = take(TILES * EXPERTS).rearrange("p (t e) -> p t e", e=EXPERTS)
        per_tile = take(TILES * EXPERTS)
        running = take(TILES * EXPERTS)
        segment = take(TILES * EXPERTS)
        edges = take(TILES)
        counts = take(EXPERTS)
        ntiles = take(EXPERTS)
        tiles_end = take(EXPERTS)
        base = take(EXPERTS)
        slots_f = take(TILES)
        slots = take(TILES).bitcast(i32)
        tile_ids = take(32)
        tile_expert_f = take(32)
        tile_expert = take(32).bitcast(i32)
        over = take(32 * EXPERTS).rearrange("p (j e) -> p j e", e=EXPERTS)
        xtile = take(D)
        xe0 = take(128)
        xe1 = take(128)
        hid = take(FF)
        hidt = take(FF).rearrange("p (c t) -> p c t", c=FF // 128)
        ytile = take(D)
        assert cursor[0] <= ARENA
        y_tok = x2

        ps = ctx.enter_context(nc.psum_tensor("ps", [128, 8 * 512], fp32))

        def slot(n):
            return ps[:, (n % 4) * 1024:(n % 4 + 1) * 1024]

        def bank(n, i):
            return ps[:, (n % 4) * 1024 + 512 * i:(n % 4) * 1024 + 512 * i + 512]

        S = {name: sem(name) for name in COUNTS}
        consts_ready = sem("consts_ready")
        weights_loaded = sem("weights_loaded")
        pads_ready = sem("pads_ready")
        cw0_stacked = sem("cw0_stacked")
        experts_loaded = sem("experts_loaded")
        tokens_loaded = sem("tokens_loaded")
        moe_consts = sem("moe_consts")
        slots_ready = sem("slots_ready")
        scattered = sem("scattered")
        xtile_loaded = sem("xtile_loaded")
        rank_full = sem("rank_full")
        xt_full, hid_full, hidt_full, y_full = sem("xt_full"), sem("hid_full"), sem("hidt_full"), sem("y_full")
        xt_taken, hid_taken, y_taken = sem("xt_taken"), sem("hid_taken"), sem("y_taken")
        hidt_taken_dve, hidt_taken_act = sem("hidt_taken_dve"), sem("hidt_taken_act")
        y_stored = sem("y_stored")
        gathered = sem("gathered")
        out_ready = sem("out_ready")
        out_stored = sem("out_stored")
        N_CONSTS = 15
        N_MOE_CONSTS = 10
        block = ctx.enter_context(nc.Block())

        def wait(eng, name, phase, k, b=None, pr=None):
            assert at(name, phase, k, 0, 0) > 0, (name, phase, k)
            eng.wait_ge(S[name], at(name, phase, k, b, pr))

        def first_layer_rows(a, piece):
            j, i = piece // 3, piece % 3
            rows = a[:, 24 * j * PITCH:24 * (j + 1) * PITCH].rearrange("p (k m c) -> p m k c", m=SUB, c=PITCH)
            return rows[:, 2 * i:2 * i + 2, :, :]

        def split_views(layer, piece):
            if layer == 0:
                src = stage[:, piece % STAGES, :].rearrange("p (m k c) -> p m k c", m=2, c=PITCH)
                return src, first_layer_rows(hs[0][0], piece), first_layer_rows(hs[0][1], piece)
            r = sum(NORM_CHUNKS[layer][:piece])
            cut = slice(r * PITCH, (r + NORM_CHUNKS[layer][piece]) * PITCH)
            return ys[layer][:, cut], hs[layer][0][:, cut], hs[layer][1][:, cut]

        n_weight_dmas = 0

        @block.sync
        def _(sp):
            nonlocal n_weight_dmas

            def load(dst, src):
                nonlocal n_weight_dmas
                sp.dma_start(dst, src, allow_slow_non_contiguous=True).then_inc(weights_loaded, 16)
                n_weight_dmas += 1

            def col(a):
                return a.rearrange("(p a) -> p a", a=1)

            load(cw0n[:, :], ins["L0_tok_cw0"].rearrange("o i k -> o (i k)"))
            for l in range(1, CONV_LAYERS):
                load(cwn[l], ins[f"L0_tok_cw{l}"].rearrange("o i k -> o (i k)"))
            load(pwn[:, 0, :], ins["L0_tok_pw"][0:128, :])
            load(pwn[0:D1, 1, :], ins["L0_tok_pw"][128:D, :])
            for l in range(CONV_LAYERS):
                for n, name in enumerate(("cb", "gw", "gb")):
                    load(par[:, n, l:l + 1], col(ins[f"L0_tok_{name}{l}"]))
            load(pb_b[:, :], ins["L0_tok_pb"].partition_broadcast(128))
            load(bo_b[:, :], ins["L0_attn_b_O"].partition_broadcast(128))
            load(gate_b[:, :], ins["L0_ffn_gate_b"].partition_broadcast(128))
            load(gw0[:, :], ins["L0_ffn_gate_w"][0:128, :])
            load(gw1[:, :], ins["L0_ffn_gate_w"][128:D, :])
            load(wo[:, :, :], ins["L0_attn_W_O"].rearrange("(a h) m d -> (h m) a d", h=2))
            for n, name in enumerate("QKV"):
                for hh in range(2):
                    load(bqkv[DH * hh:DH * hh + DH, n, :],
                         ins[f"L0_attn_b_{name}"].rearrange("(a h) m -> h m a", h=2)[hh, :, :])

            def load_pair(pr):
                for n, name in enumerate("QKV"):
                    w = ins[f"L0_attn_W_{name}"].rearrange("(a h) d m -> a d h m", h=2)
                    for buf, rows in ((wqkv0, (0, 128)), (wqkv1[0:D1], (128, D)), (wqkv1[D1:128], (128, D))):
                        if isinstance(pr, int):
                            src = w[pr, rows[0]:rows[1], :, :]
                        else:
                            src = w[bass.ds(pr, 1), rows[0]:rows[1], :, :].rearrange("a d h m -> (a d) h m")
                        sp.dma_start(buf[:, n, :].rearrange("p (h m) -> p h m", h=2), src
                                     ).then_inc(S["w_loaded"], 16)

            def stack_heads(phase, b, pr=None):
                wait(sp, "parts_ready", phase, 1, b, pr)
                for hh in range(2):
                    if hh == 1 and phase == PAIR:
                        wait(sp, "ps_full", phase, job_index(phase, "s", (STEPS - 1,)) + 1, b, pr)
                    rows = slice(DH * hh, DH * hh + DH)
                    for part in range(2):
                        half = slice(DH * part, DH * part + DH)
                        sp.dma_start(q_stack[half, hh, :], q_parts[rows, part, :]
                                     ).then_inc(S[f"head{hh}_stacked"], 16)
                        sp.dma_start(k_stack[half, hh, :, :], k_parts[rows, :, :]
                                     ).then_inc(S[f"head{hh}_stacked"], 16)

            load_pair(0)
            sp.wait_ge(S["w_split"], 1)
            load_pair(1)
            sp.wait_ge(pads_ready, 3)
            sp.dma_start(xslot_dram.rearrange("(t p) d -> p t d", p=128),
                         zeros[:, :].unsqueeze(1).to_broadcast([128, SLOT_TILES, D])).then_inc(S["scratch_stored"], 16)
            with sp.Fori(0, BATCH) as b:
                stack_heads(TOWER, b)
                wait(sp, "w_split", TOWER, 1, b)
                load_pair(2)
                with sp.Fori(0, PAIRS - 3) as pr:
                    stack_heads(PAIR, b, pr)
                    wait(sp, "w_split", PAIR, 1, b, pr)
                    load_pair(pr + 3)
                for pr in (PAIRS - 3, PAIRS - 2):
                    stack_heads(PAIR, b, pr)
                    wait(sp, "w_split", PAIR, 1, b, pr)
                    load_pair(pr + 3 - PAIRS)
                wait(sp, "h1_ready", POST, 1, b)
                for src, dst in ((h, h1_dram), (xn, x2_dram)):
                    full = dst[bass.ds(b * TT, TT - 1), :, :].rearrange("t p d -> p t d")
                    sp.dma_start(full, src[:, 0:TT - 1, :]).then_inc(S["scratch_stored"], 16)
                    last = dst[bass.ds(b * TT + TT - 1, 1), 0:LASTM, :].rearrange("t p d -> p t d")
                    sp.dma_start(last, src[0:LASTM, TT - 1:TT, :]).then_inc(S["scratch_stored"], 16)

            wait(sp, "scratch_stored", MOE, 0)
            wait(sp, "ps_full", MOE, 0)
            for tile, dram in ((x2, x2_dram), (h1, h1_dram)):
                for b in range(BATCH):
                    sp.dma_start(tile[:, b * TT:b * TT + TT - 1, :],
                                 dram[b * TT:b * TT + TT - 1, :, :].rearrange("t p d -> p t d")
                                 ).then_inc(tokens_loaded, 16)
                    sp.dma_start(tile[0:LASTM, b * TT + TT - 1, :], dram[b * TT + TT - 1, 0:LASTM, :]
                                 ).then_inc(tokens_loaded, 16)
            for e in range(EXPERTS):
                sp.dma_start(w1a[:, e, :], ins["L0_ffn_w1"][e, 0:128, :]).then_inc(experts_loaded, 16)
                sp.dma_start(w1b[0:D1, e, :], ins["L0_ffn_w1"][e, 128:D, :]).then_inc(experts_loaded, 16)
                sp.dma_start(w2[:, e, :, :], ins["L0_ffn_w2"][e, :, :].rearrange("(c p) d -> p c d", p=128)
                             ).then_inc(experts_loaded, 16)
            sp.dma_start(w1b[D1:D1 + 1, :, :], ins["L0_ffn_b1"].unsqueeze(0)).then_inc(experts_loaded, 16)
            sp.dma_start(b2[0:1, :, :], ins["L0_ffn_b2"].unsqueeze(0)).then_inc(experts_loaded, 16)

            def xslot_tile(j):
                return xslot_dram[bass.ds(j * 128, 128), :]

            sp.wait_ge(scattered, 16 * TILES)
            sp.dma_start(xtile, xslot_dram[0:128, :]).then_inc(xtile_loaded, 16)
            sp.wait_ge(xt_full, 1)
            sp.dma_start(xtile, xslot_dram[128:256, :]).then_inc(xtile_loaded, 16)
            sp.wait_ge(xt_full, 2)
            sp.dma_start(xtile, xslot_dram[256:384, :]).then_inc(xtile_loaded, 16)
            sp.wait_ge(y_taken, 1)
            sp.dma_start(yslot_dram[0:128, :], ytile).then_inc(y_stored, 16)
            with sp.Fori(3, SLOT_TILES) as j:
                sp.wait_ge(xt_full, j)
                sp.dma_start(xtile, xslot_tile(j)).then_inc(xtile_loaded, 16)
                sp.wait_ge(y_taken, j - 1)
                sp.dma_start(yslot_dram[bass.ds(j * 128 - 256, 128), :], ytile).then_inc(y_stored, 16)
            for j in (SLOT_TILES - 2, SLOT_TILES - 1):
                sp.wait_ge(y_taken, j + 1)
                sp.dma_start(yslot_dram[j * 128:j * 128 + 128, :], ytile).then_inc(y_stored, 16)
            for b in range(BATCH):
                sp.wait_ge(out_ready, b + 1)
                n = TT - 1
                sp.dma_start(out[b, 0:128 * n, :].rearrange("(t p) d -> p t d", p=128),
                             h1[:, b * TT:b * TT + n, :]).then_inc(out_stored, 16)
                sp.dma_start(out[b, 128 * n:SEQ, :], h1[0:LASTM - 1, b * TT + n, :]).then_inc(out_stored, 16)
            sp.wait_ge(out_stored, 16 * 2 * BATCH)

        @block.gpsimd
        def _(pool):
            steps = [0]

            def const(ins_, wait_last=True):
                steps[0] += 1
                ins_.then_inc(consts_ready, 1)
                if wait_last:
                    pool.wait_ge(consts_ready, steps[0])

            g = nc.gpsimd
            for m in (ident, ident_h, ident_b):
                const(g.memset(m[:, :], 0.0))
                const(g.affine_select(out=m[:, :], in_=m[:, :], compare_op=ALU.not_equal, fill=1.0, base=0,
                                      pattern=[[-1, 128]], channel_multiplier=1))
            const(g.memset(causal_b[:, :], 0.0))
            const(g.affine_select(out=causal_b[:, :], in_=causal_b[:, :], compare_op=ALU.is_ge, fill=MASKED,
                                  base=0, pattern=[[-1, 128]], channel_multiplier=1))
            const(g.memset(group_avg[:, :], 1.0 / GROUP))
            const(g.affine_select(out=group_avg[:, :], in_=group_avg[:, :], compare_op=ALU.is_ge, fill=0.0,
                                  base=0, pattern=[[-GROUP, 128 // GROUP], [0, GROUP]], channel_multiplier=1))
            const(g.affine_select(out=group_avg[:, :], in_=group_avg[:, :], compare_op=ALU.is_ge, fill=0.0,
                                  base=GROUP - 1, pattern=[[GROUP, 128 // GROUP], [0, GROUP]],
                                  channel_multiplier=-1))
            const(g.iota(prefer[:, :], pattern=[[-1, EXPERTS]], base=EXPERTS, channel_multiplier=0,
                         allow_small_or_imprecise_dtypes=True))
            const(g.memset(neg_half[:, :], -0.5))
            const(g.memset(ones_col[:, :], 1.0))
            const(g.memset(wscale_col[:, :], WSCALE))
            assert steps[0] == N_CONSTS

            def load_samples(b):
                x = ins["x"][b:b + 1, :] if isinstance(b, int) else ins["x"][bass.ds(b, 1), :]
                rows = x.rearrange("a (p n) -> (a p) n", n=PER_COL)
                pool.dma_start(xa[0:COLS, 0:PER_COL], rows).then_inc(S["x_loaded"], 16)
                pool.dma_start(xa[0:COLS - 1, PER_COL:PER_COL + STRIDE0], rows[1:COLS, 0:STRIDE0]
                               ).then_inc(S["x_loaded"], 16)

            def split_weights(phase, b=None, pr=None):
                wait(pool, "w_loaded", phase, 144 if phase == SETUP else 0, b, pr)
                if phase != SETUP:
                    wait(pool, "ps_full", phase, job_index(phase, "v", ()) + 1, b, pr)
                times = wscale_col[:, :].unsqueeze(2).to_broadcast([128, 3, 128])
                g.tensor_tensor(w0_parts[:, 0, :, :], wqkv0[:, :, :], times, ALU.mult)
                g.tensor_tensor(w1_high[:, :, :], wqkv1[:, :, :], times, ALU.mult)
                g.tensor_tensor(wqkv0[:, :, :], wqkv0[:, :, :], times, ALU.mult)
                g.tensor_tensor(wqkv1[:, :, :], wqkv1[:, :, :], times, ALU.mult).then_inc(S["w_step"], 1)
                wait(pool, "w_step", phase, 1, b, pr)
                g.tensor_tensor(w0_parts[:, 1, :, :], wqkv0[:, :, :], w0_parts[:, 0, :, :], ALU.subtract)
                g.tensor_tensor(w1_low[:, :, :], wqkv1[0:D1, :, :], w1_high[0:D1, :, :], ALU.subtract
                                ).then_inc(S["w_split"], 1)

            def split_next(b, pr):
                wait(pool, "head1_stacked", PAIR, 0, b, pr)
                once = ones_col[:, :].to_broadcast([128, TOK])
                for kind, full, parts in (("q", q_full, q_parts), ("k", k_full, k_parts)):
                    wait(pool, "act_freed", PAIR, freed(PAIR, ACT_ENGINE, job_index(PAIR, kind, ())), b, pr)
                    g.tensor_tensor(parts[:, 0, :], full, once, ALU.mult).then_inc(S[f"{kind}_high"], 1)
                    wait(pool, f"{kind}_high", PAIR, 1, b, pr)
                    last = g.tensor_tensor(parts[:, 1, :], full, parts[:, 0, :], ALU.subtract)
                last.then_inc(S["parts_ready"], 1)

            pool.wait_ge(S["x_split"], 1)
            load_samples(0)
            split_weights(SETUP)
            with pool.Fori(0, BATCH) as b:
                def low_parts(layer):
                    for unit in SPLITS:
                        if unit[0] == layer and low_engine(*unit) == "pool":
                            wait(pool, "hi_done", TOWER, SPLITS.index(unit) + 1, b)
                            src, high, low = split_views(*unit)
                            g.tensor_tensor(low, src, high, ALU.subtract).then_inc(S["lo_pool"], 1)

                for n in range(CONV_LAYERS):
                    wait(pool, "var_ready", TOWER, n + 1, b)
                    g.tensor_tensor(tmp[:, 2:3], tmp[:, 1:2], neg_half[:, 0:1], ALU.pow
                                    ).then_inc(S["rstd_ready"], 1)
                    if n == 0:
                        wait(pool, "x_split", TOWER, 1, b)
                        wait(pool, "ps_full", TOWER, job_index(TOWER, "taps", ()) + 1, b)
                        load_samples((b + 1) & (BATCH - 1))
                    low_parts(n)
                for phase, k in ((TOWER, CONV_LAYERS + 1), (POST, 1)):
                    wait(pool, "var_ready", phase, k, b)
                    g.tensor_tensor(lnr[:, :], lnv[:, :], neg_half[:, 0:TT], ALU.pow
                                    ).then_inc(S["rstd_ready"], 1)
                    if phase == TOWER:
                        split_weights(TOWER, b)
                        with pool.Fori(0, PAIRS - 1) as pr:
                            split_next(b, pr)
                            split_weights(PAIR, b, pr)

            wait(pool, "ps_full", MOE, 0)
            wait(pool, "scratch_stored", MOE, 0)
            steps[0] = 0

            def moe_const(ins_):
                steps[0] += 1
                ins_.then_inc(moe_consts, 1)
                pool.wait_ge(moe_consts, steps[0])

            moe_const(g.memset(ones, 1.0))
            moe_const(g.memset(before, 1.0))
            moe_const(g.affine_select(out=before, in_=before, compare_op=ALU.is_gt, fill=0.0, base=0,
                                      pattern=[[1, 128]], channel_multiplier=-1))
            moe_const(g.memset(segment, 1.0))
            moe_const(g.memset(segment.rearrange("p (e t) -> p e t", t=TILES)[:, :, 0:1], 0.0))
            moe_const(g.iota(edges, pattern=[[128, TILES]], base=0, channel_multiplier=0,
                             allow_small_or_imprecise_dtypes=True))
            moe_const(g.iota(tile_ids, pattern=[[1, 32]], base=0, channel_multiplier=0,
                             allow_small_or_imprecise_dtypes=True))
            moe_const(g.memset(xe1[D1:D1 + 1, :], 1.0))
            moe_const(g.memset(counts, 0.0))
            moe_const(g.memset(tiles_end, 0.0))
            assert steps[0] == N_MOE_CONSTS
            pool.wait_ge(slots_ready, 1)
            pool.wait_ge(tokens_loaded, 16 * 4 * BATCH)
            for t in range(TILES):
                rows = SEQ - 128 * (TT - 1) if t % TT == TT - 1 else 128
                pool.indirect_dma_start(out=xslot_dram,
                                        out_offset=bass.IndirectOffsetOnAxis(ap=slots[0:rows, t:t + 1], axis=0),
                                        in_=x2[0:rows, t, :], in_offset=None).then_inc(scattered, 16)
            pool.wait_ge(y_stored, 16 * SLOT_TILES)
            for t in range(TILES):
                rows = SEQ - 128 * (TT - 1) if t % TT == TT - 1 else 128
                pool.indirect_dma_start(out=y_tok[0:rows, t, :], out_offset=None, in_=yslot_dram,
                                        in_offset=bass.IndirectOffsetOnAxis(ap=slots[0:rows, t:t + 1], axis=0)
                                        ).then_inc(gathered, 16)

        @block.scalar
        def _(act):
            a = nc.scalar

            def jobs_of(phase):
                for n in ACT_ORDER[phase]:
                    kind, args, who = JOBS[phase][n]
                    yield slot_of(phase, n), n, kind, args

            for g, n, kind, args in jobs_of(SETUP):
                wait(act, "ps_full", SETUP, n + 1)
                if kind == "cw0t":
                    src = bank(g, 0).bitcast(fp16)[0:3 * WIN, 0:SUB * CH].rearrange("p (m c) -> p m c", m=SUB)
                    a.activation(cw0f[:, :], bank(g, 1)[0:TAPS0, 0:CH], ACT.Copy)
                    a.activation(cw0t[:, :, :], src, ACT.Copy).then_inc(S["act_freed"], 1)
                elif kind == "pwt":
                    a.activation(pwt[:, :], bank(g, 0)[:, 0:D], ACT.Copy).then_inc(S["act_freed"], 1)
                else:
                    a.activation(spare[:, 0:1], bank(g, 0)[:, 0:1], ACT.Copy).then_inc(S["act_freed"], 1)

            def normalise(layer, b):
                wait(act, "affine_ready", TOWER, layer + 1, b)
                r = 0
                for rows in NORM_CHUNKS[layer]:
                    src = ys[layer][:, r * PITCH:(r + rows) * PITCH]
                    dst = src
                    if layer == 5:
                        src = src.rearrange("p (r c) -> p r c", c=PITCH)[:, :, 0:COLS]
                        dst = h5t.rearrange("p (c r) -> p r c", r=rows)
                    a.activation(dst, src, ACT.Gelu_apprx_tanh, bias=affine[:, 1:2], scale=affine[:, 0:1]
                                 ).then_inc(S["norm_done"], 1)
                    r += rows

            def attention_job(phase, g, n, kind, args, b, pr=None):
                if kind == "s":
                    (k,) = args
                    i, k_ = k % TT, k % STEPS
                    m = tile_rows(i)
                    if phase != TOWER:
                        wait(act, "ps_full", phase, transposed_before(phase, k - PROBS), b, pr)
                    wait(act, "smax_done", phase, k + 1 if phase == TOWER else k - 1, b, pr)
                    a.activation(prob[k % PROBS][0:m, 0:128 * i + m], slot(g)[0:m, 0:128 * i + m], ACT.Exp,
                                 bias=nmax[0:m, k_:k_ + 1], scale=SCALE, accum_out=rsum[0:m, k_:k_ + 1]
                                 ).then_inc(S["act_freed"], 1)
                    return
                wait(act, "ps_full", phase, n + 1, b, pr)
                if kind in ("q", "k"):
                    if phase == PAIR:
                        wait(act, "parts_ready", phase, 0, b, pr)
                    dst, w = (q_parts, 0) if kind == "q" else (k_parts, 1)
                    src = slot(g).rearrange("p (k n) -> p k n", k=2)[:, :, 0:TOK // 2]
                    bias = bqkv[:, w, 0:1] if phase == TOWER else bqkv[:, w, bass.ds(pr + 1, 1)]
                    full = q_full if kind == "q" else k_full
                    if phase == TOWER:
                        a.activation(dst[:, 0, :].rearrange("p (k n) -> p k n", k=2), src, ACT.Identity, bias=bias,
                                     scale=1.0 / WSCALE)
                    a.activation(full.rearrange("p (k n) -> p k n", k=2), src, ACT.Identity, bias=bias,
                                 scale=1.0 / WSCALE).then_inc(S["act_freed"], 1)
                elif kind == "v":
                    src = slot(g).rearrange("p (t c) -> p t c", c=128)
                    a.activation(vt[:, 0:TT, :], src[:, 0:TT, :], ACT.Copy, scale=1.0 / WSCALE
                                 ).then_inc(S["act_freed"], 1)
                elif kind == "pt":
                    (k,) = args
                    i = k % TT
                    m = tile_rows(i)
                    src = slot(g).rearrange("p (t c) -> p t c", c=128)
                    if i == 4:
                        a.activation(probt[k % 2][:, 4, 0:m], src[:, 4, 0:m], ACT.Copy
                                     ).then_inc(S["act_freed"], 1)
                    else:
                        a.activation(probt[k % 2][:, 4:6, 0:m], src[:, 4:6, 0:m], ACT.Copy
                                     ).then_inc(S["act_freed"], 1)
                else:
                    assert kind == "z"
                    (k,) = args
                    i, hh = k % TT, k // TT
                    m = tile_rows(i)
                    wait(act, "rinv_ready", phase, k + 1, b, pr)
                    a.activation(z[0:m, i, DH * hh:DH * hh + DH], slot(g)[0:m, Z_AT:Z_AT + DH], ACT.Copy,
                                 scale=rinv[0:m, k:k + 1]).then_inc(S["act_freed"], 1)

            with act.Fori(0, BATCH) as b:
                layer = 0
                for g, n, kind, args in jobs_of(TOWER):
                    if kind == "conv":
                        if args[0] > 1 and args[1] == 0:
                            normalise(args[0] - 1, b)
                        layer, r, cut = args
                        wait(act, "ps_full", TOWER, n + 1, b)
                        rows = cut[0]
                        dst = ys[layer][:, r * PITCH:(r + sum(cut)) * PITCH]
                        src = slot(g).rearrange("p (k n) -> p k n", k=2)[:, 0:len(cut), 0:rows * PITCH]
                        a.activation(dst.rearrange("p (k n) -> p k n", k=len(cut)), src, ACT.Identity,
                                     scale=1.0 / WSCALE).then_inc(S["act_freed"], 1)
                    elif kind == "conv0":
                        j, i = args
                        if args == (0, 0):
                            wait(act, "affine_ready", TOWER, 1, b)
                            wait(act, "scratch_stored", TOWER, 0, b)
                        wait(act, "ps_full", TOWER, n + 1, b)
                        piece = 3 * j + i
                        if piece >= STAGES:
                            before_ = (0, piece - STAGES)
                            wait(act, "hi_done", TOWER, SPLITS.index(before_) + 1, b)
                            if low_engine(*before_) == DVE_ENGINE:
                                wait(act, "lo_dve", TOWER, lows(DVE_ENGINE, before_), b)
                            else:
                                wait(act, "lo_pool", TOWER, lows("pool", before_), b)
                        src = slot(g).rearrange("p (m n) -> p m n", m=2)[:, :, 0:4 * PITCH]
                        a.activation(stage[:, piece % STAGES, :].rearrange("p (m n) -> p m n", m=2), src,
                                     ACT.Gelu_apprx_tanh,
                                     bias=affine[:, 1:2], scale=affine[:, 0:1]).then_inc(S["act_freed"], 1)
                    elif kind in ("q", "k", "v", "s"):
                        attention_job(TOWER, g, n, kind, args, b)
                    else:
                        assert kind == "xtr"
                        if layer == 5:
                            normalise(5, b)
                            layer = None
                        wait(act, "ps_full", TOWER, n + 1, b)
                        a.activation(xt_parts[:, args[0], :], bank(g, 0).bitcast(fp16)[:, 0:TOK], ACT.Copy
                                     ).then_inc(S["act_freed"], 1)
                with act.Fori(0, PAIRS - 1) as pr:
                    for g, n, kind, args in jobs_of(PAIR):
                        attention_job(PAIR, g, n, kind, args, b, pr)
                for g, n, kind, args in jobs_of(LAST_PAIR):
                    attention_job(LAST_PAIR, g, n, kind, args, b)
                for g, n, kind, args in jobs_of(POST):
                    wait(act, "ps_full", POST, n + 1, b)
                    a.activation(xnt1[0:D1, 0:TOK], slot(g)[0:D1, 0:TOK], ACT.Copy).then_inc(S["act_freed"], 1)

            def expert_tile(j):
                act.wait_ge(hid_full, j + 1)
                src = slot(1).rearrange("p (k n) -> p k n", k=2)[:, :, 0:FF // 2]
                a.activation(hid.rearrange("p (k n) -> p k n", k=2), src, ACT.Gelu).then_inc(hid_taken, 1)
                act.wait_ge(hidt_full, j + 1)
                a.activation(hidt[:, 4:6, :], bank(2, 1)[:, 0:256].rearrange("p (c t) -> p c t", c=2), ACT.Copy
                             ).then_inc(hidt_taken_act, 1)

            expert_tile(0)
            with act.Fori(1, SLOT_TILES) as j:
                expert_tile(j)

        @block.vector
        def _(dve):
            v = nc.vector
            state = {"phase": SETUP, "n": 0, "b": None, "pr": None}

            def enter(phase, b=None, pr=None):
                state.update(phase=phase, n=0, b=b, pr=pr)

            def step(ins_):
                state["n"] += 1
                ins_.then_inc(S["dve_step"], 1)
                dve.wait_ge(S["dve_step"], at("dve_step", state["phase"], state["n"], state["b"], state["pr"]))

            def carry_wait():
                v.memset(spare[:, 3:4], 0.0)

            def leave():
                index = PHASES.index(state["phase"])
                assert state["n"] == COUNTS["dve_step"][index], (index, state["n"])

            v.memset(xa[:, :], 0.0).then_inc(S["x_split"], 1)
            v.memset(cw0pad, 0.0).then_inc(pads_ready, 1)
            v.memset(xstack[:, :, :], 0.0).then_inc(pads_ready, 1)
            v.memset(zeros[:, :], 0.0).then_inc(pads_ready, 1)
            v.memset(onehot[:, :, :], 0.0).then_inc(pads_ready, 1)
            v.memset(logits[:, :, :], 0.0).then_inc(pads_ready, 1)
            v.memset(lnmv[:, :, :], 0.0).then_inc(pads_ready, 1)
            dve.wait_ge(pads_ready, 6)
            dve.wait_ge(weights_loaded, 16 * n_weight_dmas)
            step(v.tensor_scalar(cw0s[:, :], cw0n[:, :], WSCALE, None, ALU.mult))
            for m in range(SUB):
                o = STRIDE0 * m
                last = v.tensor_copy(cw0pad[:, m, o:o + TAPS0], cw0s[:, :])
            step(last)
            for m in range(SUB):
                o = STRIDE0 * m
                v.tensor_copy(cw0pad[:, m, WIN + o:WIN + o + TAPS0], cw0pad[:, m, o:o + TAPS0])
                last = v.tensor_tensor(cw0pad[:, m, 2 * WIN + o:2 * WIN + o + TAPS0], cw0s[:, :],
                                       cw0pad[:, m, o:o + TAPS0], ALU.subtract)
            last.then_inc(cw0_stacked, 1)
            for n, (kind, args, who) in enumerate(JOBS[SETUP]):
                if DVE_ENGINE not in who:
                    continue
                wait(dve, "ps_full", SETUP, n + 1)
                (l,) = args
                taps = 2 if l == 5 else 3
                src = bank(n, 0)[:, 0:taps * CH].rearrange("p (k c) -> p k c", k=taps)
                step(v.tensor_scalar(cwt[l][:, 0, :, :], src, WSCALE, None, ALU.mult))
                v.scalar_tensor_tensor(out=cwt[l][:, 1, :, :], in0=src, scalar=WSCALE, in1=cwt[l][:, 0, :, :],
                                       op0=ALU.mult, op1=ALU.subtract).then_inc(S["dve_freed"], 1)
            leave()

            def group_stats(layer, pieces, b):
                step(last_bn[0])
                carry_wait()
                step(v.bn_aggr(mv[:, :], bn[:, 0:pieces, :].rearrange("p n s -> p (n s)")))
                step(v.tensor_tensor(ms[:, 0:1], mv[:, 0:1], par[:, 0, layer:layer + 1], ALU.add))
                v.scalar_tensor_tensor(out=ms[:, 1:2], in0=ms[:, 0:1], scalar=ms[:, 0:1], in1=mv[:, 1:2],
                                       op0=ALU.mult, op1=ALU.add).then_inc(S["channel_stats"], 1)

            def group_affine(layer, g, n, b):
                wait(dve, "ps_full", TOWER, n + 1, b)
                ins_ = v.tensor_copy(gm[:, :], bank(g, 0)[:, 0:2])
                ins_.then_inc(S["dve_freed"], 1)
                dve.wait_ge(S["dve_freed"], at("dve_freed", TOWER, freed(TOWER, DVE_ENGINE, n), b))
                step(v.scalar_tensor_tensor(out=tmp[:, 0:1], in0=gm[:, 0:1], scalar=gm[:, 0:1], in1=gm[:, 1:2],
                                            op0=ALU.mult, op1=ALU.subtract))
                v.tensor_scalar(tmp[:, 1:2], tmp[:, 0:1], -1.0, EPS, ALU.mult, ALU.add
                                ).then_inc(S["var_ready"], 1)
                step(v.tensor_tensor(tmp[:, 3:4], par[:, 0, layer:layer + 1], gm[:, 0:1], ALU.subtract))
                wait(dve, "rstd_ready", TOWER, layer + 1, b)
                scale = affine[:, 0:1] if layer else tmp[:, 0:1]
                step(v.tensor_tensor(scale, tmp[:, 2:3], par[:, 1, layer:layer + 1], ALU.mult))
                if layer == 0:
                    v.tensor_scalar(affine[:, 0:1], scale, 1.0 / WSCALE, None, ALU.mult)
                v.scalar_tensor_tensor(out=affine[:, 1:2], in0=tmp[:, 3:4], scalar=scale,
                                       in1=par[:, 2, layer:layer + 1], op0=ALU.mult, op1=ALU.add
                                       ).then_inc(S["affine_ready"], 1)

            def layernorm():
                for i in range(TT):
                    m = tile_rows(i)
                    last = v.bn_stats(bn[0:m, i, :], h[0:m, i, :])
                step(last)
                carry_wait()
                for i in range(TT):
                    m = tile_rows(i)
                    last = v.bn_aggr(lnmv[0:m, i, :], bn[0:m, i, :])
                step(last)
                v.tensor_scalar(lnv[:, :], lnmv[:, :, 1], EPS, None, ALU.add).then_inc(S["var_ready"], 1)
                wait(dve, "rstd_ready", state["phase"], CONV_LAYERS + 1 if state["phase"] == TOWER else 1, state["b"])
                for i in range(TT):
                    m = tile_rows(i)
                    last = v.tensor_scalar(xn[0:m, i, :], h[0:m, i, :], lnmv[0:m, i, 0:1], lnr[0:m, i:i + 1],
                                           ALU.subtract, ALU.mult)
                if state["phase"] == TOWER:
                    step(last)
                    v.tensor_copy(xn_parts[:, :, 0, :], xn[:, :, 0:128])
                    v.tensor_copy(xn_parts[:, :, 2, 0:D1], xn[:, :, 128:D]).then_inc(S["xn_high"], 1)
                    wait(dve, "xn_high", TOWER, 1, state["b"])
                    v.tensor_tensor(xn_parts[:, :, 1, :], xn[:, :, 0:128], xn_parts[:, :, 0, :], ALU.subtract)
                    last = v.tensor_tensor(xn_parts[:, :, 2, D1:128], xn[:, :, 128:D], xn_parts[:, :, 2, 0:D1],
                                           ALU.subtract)
                last.then_inc(S["xn_ready"], 1)

            def take_token_rows(g, part, in1, last_inc=True):
                if part == 0:
                    for k in range(2):
                        last = v.tensor_tensor(h[:, 2 * k:2 * k + 2, :],
                                               bank(g, k)[:, 0:2 * D].rearrange("p (t d) -> p t d", t=2),
                                               in1(2 * k, 2, 128), ALU.add)
                else:
                    v.tensor_tensor(h[:, 4, :], bank(g, 0)[:, 0:D], in1(4, 1, 128), ALU.add)
                    last = v.tensor_tensor(h[0:LASTM, 5, :], bank(g, 0)[0:LASTM, D:2 * D], in1(5, 1, LASTM),
                                           ALU.add)
                last.then_inc(S["dve_freed"], 1)

            def halo(layer, b):
                r = ROWS[layer] * PITCH
                high, low = hs[layer]
                v.tensor_copy(high[:, r:r + PITCH], high[:, 1:1 + PITCH])
                v.tensor_copy(low[:, r:r + PITCH], low[:, 1:1 + PITCH]).then_inc(S["halo_done"], 1)

            def split(unit, b):
                src, high, low = split_views(*unit)
                n = SPLITS.index(unit) + 1
                v.tensor_copy(high, src).then_inc(S["hi_done"], 1)
                if low_engine(*unit) == DVE_ENGINE:
                    dve.wait_ge(S["hi_done"], at("hi_done", TOWER, n, b))
                    v.tensor_tensor(low, src, high, ALU.subtract).then_inc(S["lo_dve"], 1)

            def wait_split(unit, b):
                wait(dve, "hi_done", TOWER, SPLITS.index(unit) + 1, b)
                for engine, name in ((DVE_ENGINE, "lo_dve"), ("pool", "lo_pool")):
                    if lows(engine, unit):
                        wait(dve, name, TOWER, lows(engine, unit), b)

            def attention_job(phase, n, kind, args, b, pr=None):
                g = slot_of(phase, n)
                wait(dve, "ps_full", phase, n + 1, b, pr)
                if kind in ("q", "k"):
                    wait(dve, "act_freed", phase, freed(phase, ACT_ENGINE, n), b, pr)
                    full, dst = (q_full, q_parts) if kind == "q" else (k_full, k_parts)
                    last = v.tensor_tensor(dst[:, 1, :], full, dst[:, 0, :], ALU.subtract)
                    if kind == "k":
                        last.then_inc(S["parts_ready"], 1)
                elif kind == "s":
                    (k,) = args
                    i, k_ = k % TT, k % STEPS
                    m = tile_rows(i)
                    step(v.reduce_max(smax[0:m, k_:k_ + 1], slot(g)[0:m, 0:128 * i + m], AX.X))
                    v.tensor_scalar(nmax[0:m, k_:k_ + 1], smax[0:m, k_:k_ + 1], -SCALE, None, ALU.mult
                                    ).then_inc(S["smax_done"], 1)
                elif kind == "pt":
                    (k,) = args
                    i = k % TT
                    m = tile_rows(i)
                    src = slot(g).rearrange("p (t c) -> p t c", c=128)
                    w = min(i + 1, 4)
                    v.tensor_copy(probt[k % 2][:, 0:w, 0:m], src[:, 0:w, 0:m]).then_inc(S["dve_freed"], 1)
                    wait(dve, "act_freed", phase, exp_done(phase, k), b, pr)
                    v.reciprocal(rinv[0:m, k:k + 1], rsum[0:m, k:k + 1]).then_inc(S["rinv_ready"], 1)
                else:
                    assert kind == "zt"
                    a = PAIRS - 1 if pr is None else pr
                    dst = zt[:, a, 0:TOK] if pr is None else zt[:, bass.ds(a, 1), 0:TOK].rearrange("p a t -> p (a t)")
                    bias = bqkv[:, 2, a:a + 1] if pr is None else bqkv[:, 2, bass.ds(a, 1)]
                    v.tensor_scalar(dst, slot(g)[:, 0:TOK], bias, None, ALU.add).then_inc(S["dve_freed"], 1)

            last_bn = [None]
            with dve.Fori(0, BATCH) as b:
                enter(TOWER, b)
                wait(dve, "x_loaded", TOWER, 0, b)
                main = xa[:, 0:PER_COL].rearrange("p (n k) -> p n k", k=BLK_STEP)
                tail = xa[:, BLK_STEP:BLK_STEP + PER_COL].rearrange("p (n k) -> p n k", k=BLK_STEP)[:, :, 0:WIN - BLK_STEP]
                v.tensor_copy(xstack[:, :, 0:BLK_STEP], main)
                step(v.tensor_copy(xstack[:, :, BLK_STEP:WIN], tail))
                v.tensor_tensor(xstack[:, :, WIN:WIN + BLK_STEP], main, xstack[:, :, 0:BLK_STEP], ALU.subtract)
                v.tensor_tensor(xstack[:, :, WIN + BLK_STEP:2 * WIN], tail, xstack[:, :, BLK_STEP:WIN], ALU.subtract)
                v.tensor_copy(xstack[:, :, 2 * WIN:3 * WIN], xstack[:, :, 0:WIN]).then_inc(S["x_split"], 1)
                pieces = 0
                for n, (kind, args, who) in enumerate(JOBS[TOWER]):
                    g = n
                    if kind == "xt":
                        (i,) = args
                        wait(dve, "ps_full", TOWER, n + 1, b)
                        half = NBLK // 2
                        src = slot(g).bitcast(fp16)[0:3 * WIN, :].rearrange("p (k n) -> p k n", k=2)[:, :, 0:8 * PITCH]
                        dst = xt[:, half * i:half * i + half, :].rearrange("p (k n) c -> p k (n c)", k=2)
                        v.tensor_copy(dst, src).then_inc(S["dve_freed"], 1)
                    elif kind in ("gram", "taps"):
                        wait(dve, "ps_full", TOWER, n + 1, b)
                        dst, m = (gram, WIN) if kind == "gram" else (tap_sums, TAPS0)
                        v.tensor_copy(dst[:, 0:m], bank(g, 0)[0:m, 0:m])
                        v.tensor_copy(dst[:, m:m + 1], bank(g, 1)[0:m, 0:1]).then_inc(S["dve_freed"], 1)
                    elif kind == "chan":
                        wait(dve, "ps_full", TOWER, n + 1, b)
                        count = float(COLS * ROWS[0] - 1)
                        bias = par[:, 0, 0:1]
                        v.tensor_scalar(ms[:, 0:1], bank(g, 0)[:, TAPS0:TAPS0 + 1], 1.0 / count, bias, ALU.mult,
                                        ALU.add)
                        v.tensor_tensor(quad[:, :], bank(g, 0)[:, 0:TAPS0], cw0n[:, :], ALU.mult
                                        ).then_inc(S["dve_freed"], 1)
                        dve.wait_ge(S["dve_freed"], at("dve_freed", TOWER, freed(TOWER, DVE_ENGINE, n), b))
                        step(v.reduce_sum(mv[:, 0:1], quad[:, :], AX.X))
                        step(v.scalar_tensor_tensor(out=tmp[:, 0:1], in0=ms[:, 0:1], scalar=2.0, in1=bias,
                                                    op0=ALU.mult, op1=ALU.subtract))
                        step(v.tensor_tensor(tmp[:, 1:2], tmp[:, 0:1], bias, ALU.mult))
                        v.scalar_tensor_tensor(out=ms[:, 1:2], in0=mv[:, 0:1], scalar=1.0 / count,
                                               in1=tmp[:, 1:2], op0=ALU.mult, op1=ALU.add
                                               ).then_inc(S["channel_stats"], 1)
                    elif kind == "conv0":
                        wait(dve, "act_freed", TOWER, freed(TOWER, ACT_ENGINE, n), b)
                        split((0, 3 * args[0] + args[1]), b)
                    elif kind == "group":
                        (layer,) = args
                        if layer:
                            group_stats(layer, pieces, b)
                            pieces = 0
                        group_affine(layer, g, n, b)
                        if 1 <= layer <= 4:
                            r = 0
                            for c, rows in enumerate(NORM_CHUNKS[layer]):
                                wait(dve, "norm_done", TOWER, norm_chunk_of(layer, r), b)
                                split((layer, c), b)
                                r += rows
                            if layer < 4:
                                wait_split((layer, 0), b)
                                halo(layer, b)
                    elif kind == "conv":
                        layer, r, cut = args
                        if layer == 1 and r == 0:
                            wait_split((0, 0), b)
                            halo(0, b)
                        wait(dve, "act_freed", TOWER, freed(TOWER, ACT_ENGINE, n), b)
                        rows = ys[layer].rearrange("p (r c) -> p r c", c=PITCH)
                        for c in cut:
                            if r + c == ROWS[layer]:
                                v.bn_stats(bn[:, pieces, :], rows[:, r:r + c - 1, 0:COLS])
                                last_bn[0] = v.bn_stats(bn[:, pieces + 1, :], rows[:, r + c - 1, 0:COLS - 1])
                                pieces += 2
                            else:
                                last_bn[0] = v.bn_stats(bn[:, pieces, :], rows[:, r:r + c, 0:COLS])
                                pieces += 1
                            r += c
                    elif kind == "embed":
                        wait(dve, "ps_full", TOWER, n + 1, b)
                        take_token_rows(g, args[0], lambda i, k, m: pb_b[0:m, :] if k == 1 else
                                        pb_b[:, :].unsqueeze(1).to_broadcast([128, 2, D]))
                        if args[0] == 1:
                            dve.wait_ge(S["dve_freed"], at("dve_freed", TOWER, freed(TOWER, DVE_ENGINE, n), b))
                            layernorm()
                    elif kind == "xtr" and DVE_ENGINE in who:
                        wait(dve, "ps_full", TOWER, n + 1, b)
                        v.tensor_copy(xt_parts[:, args[0], :], bank(g, 0).bitcast(fp16)[:, 0:TOK]
                                      ).then_inc(S["dve_freed"], 1)
                    elif kind in ("q", "k", "s"):
                        attention_job(TOWER, n, kind, args, b)
                leave()

                with dve.Fori(0, PAIRS - 1) as pr:
                    enter(PAIR, b, pr)
                    for n, (kind, args, who) in enumerate(JOBS[PAIR]):
                        if DVE_ENGINE in who or kind == "s":
                            attention_job(PAIR, n, kind, args, b, pr)
                    leave()
                enter(LAST_PAIR, b)
                for n, (kind, args, who) in enumerate(JOBS[LAST_PAIR]):
                    if DVE_ENGINE in who or kind == "s":
                        attention_job(LAST_PAIR, n, kind, args, b)
                leave()

                enter(POST, b)
                for n, (kind, args, who) in enumerate(JOBS[POST]):
                    g = slot_of(POST, n)
                    if DVE_ENGINE not in who:
                        continue
                    wait(dve, "ps_full", POST, n + 1, b)
                    if kind == "wo":
                        if args[0] == 0:
                            for i in range(TT):
                                m = tile_rows(i)
                                last = v.tensor_tensor(h[0:m, i, :], h[0:m, i, :], bo_b[0:m, :], ALU.add)
                            step(last)
                        take_token_rows(g, args[0], lambda i, k, m: h[0:m, i, :] if k == 1 else h[:, i:i + 2, :])
                        if args[0] == 1:
                            dve.wait_ge(S["dve_freed"], at("dve_freed", POST, freed(POST, DVE_ENGINE, n), b))
                            layernorm()
                            wait(dve, "xn_ready", POST, 1, b)
                            v.memset(spare[:, 2:3], 0.0).then_inc(S["h1_ready"], 1)
                    elif kind == "tr":
                        v.tensor_copy(xnt0[:, 0:TOK], slot(g)[:, 0:TOK]).then_inc(S["dve_freed"], 1)
                    elif kind == "gate":
                        src = bank(g, 0)[:, 0:TT * EXPERTS].rearrange("p (t e) -> p t e", e=EXPERTS)
                        v.tensor_tensor(logits[:, 0:TT - 1, :], src[:, 0:TT - 1, :],
                                        gate_b[:, :].unsqueeze(1).to_broadcast([128, TT - 1, EXPERTS]), ALU.add)
                        v.tensor_tensor(logits[0:LASTM, TT - 1, :], src[0:LASTM, TT - 1, :], gate_b[0:LASTM, :],
                                        ALU.add).then_inc(S["dve_freed"], 1)
                        dve.wait_ge(S["dve_freed"], at("dve_freed", POST, freed(POST, DVE_ENGINE, n), b))
                        step(v.reduce_max(best[:, :], logits[:, :, :], AX.X))
                        step(v.tensor_tensor(pick[:, :, :], logits[:, :, :],
                                             best[:, :].unsqueeze(2).to_broadcast([128, TT, EXPERTS]), ALU.is_ge))
                        step(v.tensor_tensor(pick[:, :, :], pick[:, :, :],
                                             prefer[:, :].unsqueeze(1).to_broadcast([128, TT, EXPERTS]), ALU.mult))
                        step(v.reduce_max(best[:, :], pick[:, :, :], AX.X))
                        step(v.tensor_tensor(pick[:, :, :], pick[:, :, :],
                                             best[:, :].unsqueeze(2).to_broadcast([128, TT, EXPERTS]), ALU.is_ge))
                        v.tensor_copy(onehot[:, bass.ds(b * TT, TT - 1), :], pick[:, 0:TT - 1, :])
                        step(v.tensor_copy(onehot[0:LASTM - 1, bass.ds(b * TT + TT - 1, 1), :],
                                           pick[0:LASTM - 1, TT - 1:TT, :]))
                    else:
                        v.tensor_copy(spare[:, 4 + n:5 + n], bank(g, 0)[:, 0:1]).then_inc(S["dve_freed"], 1)
                leave()

            total = [0]

            def chain(ins_):
                total[0] += 1
                ins_.then_inc(S["dve_step"], 1)
                dve.wait_ge(S["dve_step"], at("dve_step", MOE, total[0]))

            dve.wait_ge(rank_full, 1)
            dve.wait_ge(moe_consts, N_MOE_CONSTS)
            v.tensor_copy(rank, bank(0, 0)[:, 0:TILES * EXPERTS].rearrange("p (t e) -> p t e", e=EXPERTS))
            chain(v.tensor_copy(per_tile.rearrange("p (e t) -> p e t", t=TILES),
                                bank(0, 1)[:, 0:TILES * EXPERTS].rearrange("p (t e) -> p e t", e=EXPERTS)))
            chain(v.tensor_tensor_scan(running, segment, per_tile, 0.0, ALU.mult, ALU.add))
            run_et = running.rearrange("p (e t) -> p e t", t=TILES)
            chain(v.tensor_copy(counts, run_et[:, :, TILES - 1]))
            chain(v.tensor_tensor(over[:, 0:TILES, :].rearrange("p t e -> p e t"),
                                  counts.unsqueeze(2).to_broadcast([128, EXPERTS, TILES]),
                                  edges.unsqueeze(1).to_broadcast([128, EXPERTS, TILES]), ALU.is_gt))
            chain(v.reduce_sum(ntiles, over[:, 0:TILES, :].rearrange("p t e -> p e t"), AX.X))
            chain(v.tensor_tensor_scan(tiles_end, ones[:, 0:EXPERTS], ntiles, 0.0, ALU.mult, ALU.add))
            chain(v.tensor_tensor(base, tiles_end, ntiles, ALU.subtract))
            chain(v.tensor_scalar(base, base, 128.0, None, ALU.mult))
            chain(v.tensor_tensor(running, running, per_tile, ALU.subtract))
            chain(v.tensor_tensor(rank, rank, run_et.rearrange("p e t -> p t e"), ALU.add))
            chain(v.tensor_tensor(rank, rank, base.unsqueeze(1).to_broadcast([128, TILES, EXPERTS]), ALU.add))
            chain(v.tensor_tensor(rank, rank, onehot[:, :, :], ALU.mult))
            chain(v.reduce_sum(slots_f, rank, AX.X))
            v.tensor_copy(slots, slots_f).then_inc(slots_ready, 1)
            chain(v.tensor_tensor(over, tiles_end.unsqueeze(1).to_broadcast([128, 32, EXPERTS]),
                                  tile_ids.unsqueeze(2).to_broadcast([128, 32, EXPERTS]), ALU.is_le))
            chain(v.reduce_sum(tile_expert_f, over, AX.X))
            chain(v.tensor_scalar(tile_expert_f, tile_expert_f, float(EXPERTS - 1), None, ALU.min))
            v.tensor_copy(tile_expert, tile_expert_f).then_inc(slots_ready, 1)

            def take_xt(j):
                dve.wait_ge(xt_full, j + 1)
                v.tensor_copy(xe0, bank(0, 0)[:, 0:128])
                v.tensor_copy(xe1[0:D1, :], bank(0, 1)[0:D1, 0:128]).then_inc(xt_taken, 1)

            def take_hidt(j):
                dve.wait_ge(hidt_full, j + 1)
                v.tensor_copy(hidt[:, 0:4, :], bank(2, 0).rearrange("p (c t) -> p c t", c=4)
                              ).then_inc(hidt_taken_dve, 1)

            def take_y(j, first=False):
                dve.wait_ge(y_full, j + 1)
                if not first:
                    dve.wait_ge(y_stored, 16 * j)
                v.tensor_copy(ytile, bank(3, 0)[:, 0:D]).then_inc(y_taken, 1)

            take_xt(0)
            take_xt(1)
            take_hidt(0)
            take_xt(2)
            take_y(0, first=True)
            take_hidt(1)
            with dve.Fori(2, SLOT_TILES - 1) as j:
                take_xt(j + 1)
                take_y(j - 1)
                take_hidt(j)
            take_y(SLOT_TILES - 2)
            take_hidt(SLOT_TILES - 1)
            take_y(SLOT_TILES - 1)

            dve.wait_ge(gathered, 16 * TILES)
            for b in range(BATCH):
                t = b * TT
                v.tensor_tensor(h1[:, t:t + TT - 1, :], h1[:, t:t + TT - 1, :], y_tok[:, t:t + TT - 1, :], ALU.add)
                m = LASTM - 1
                v.tensor_tensor(h1[0:m, t + TT - 1, :], h1[0:m, t + TT - 1, :], y_tok[0:m, t + TT - 1, :], ALU.add
                                ).then_inc(out_ready, 1)

        @block.tensor
        def _(pe):
            t = nc.tensor

            def slot_free(phase, n, b=None, pr=None):
                if phase in (PAIR, LAST_PAIR):
                    r = RING[phase][n] - 4
                    of = phase if r >= 0 else PAIR
                    r %= ring_length(of)
                    jobs = [m for m, position in enumerate(RING[of]) if position == r]
                    for engine, name in ((ACT_ENGINE, "act_freed"), (DVE_ENGINE, "dve_freed")):
                        read = [m for m in jobs if engine in JOBS[of][m][2]]
                        if read:
                            count = freed(of, engine, read[-1])
                            wait(pe, name, phase, count if RING[phase][n] >= 4 else count - readers(PAIR, engine), b, pr)
                    return
                if phase == SETUP and n < 4:
                    return
                if phase != SETUP and n == 0:
                    wait(pe, "act_freed", phase, 0, b, pr)
                    wait(pe, "dve_freed", phase, 0, b, pr)
                if n >= 4:
                    for engine, name in ((ACT_ENGINE, "act_freed"), (DVE_ENGINE, "dve_freed")):
                        if engine in JOBS[phase][n - 4][2]:
                            wait(pe, name, phase, freed(phase, engine, n - 4), b, pr)

            pe.wait_ge(consts_ready, N_CONSTS)
            pe.wait_ge(weights_loaded, 16 * n_weight_dmas)
            for n, (kind, args, who) in enumerate(JOBS[SETUP]):
                slot_free(SETUP, n)
                if kind == "cwt":
                    (l,) = args
                    taps = 2 if l == 5 else 3
                    w = cwn[l].rearrange("p (i k) -> p k i", k=taps)
                    for k in range(taps):
                        last = t.transpose(bank(n, 0)[:, k * CH:(k + 1) * CH], w[:, k, :], ident[:, :])
                elif kind == "cw0t":
                    pe.wait_ge(cw0_stacked, 1)
                    dst = bank(n, 0).bitcast(fp16)
                    t.transpose(bank(n, 1)[0:TAPS0, 0:CH], cw0n[:, :], ident[:, :])
                    for m in range(SUB):
                        last = t.transpose(dst[0:3 * WIN, m * CH:(m + 1) * CH], cw0pad[:, m, :], ident_h[:, :])
                elif kind == "pwt":
                    t.transpose(bank(n, 0)[:, 0:128], pwn[:, 0, :], ident[:, :])
                    last = t.transpose(bank(n, 0)[:, 128:D], pwn[0:D1, 1, :], ident[0:D1, 0:D1])
                else:
                    last = t.transpose(bank(n, 0)[:, 0:128], ident[:, :], ident[:, :])
                last.then_inc(S["ps_full"], 1)

            def carry_wait(g):
                t.transpose(bank(g, 0)[:, 384:512], ident[:, :], ident[:, :])

            def token_transposes(g, part):
                for i in range(TT):
                    m = tile_rows(i)
                    if part == 0:
                        last = t.transpose(slot(g)[:, 128 * i:128 * i + m], xn[0:m, i, 0:128], ident[0:m, 0:m])
                    else:
                        last = t.transpose(slot(g)[0:D1, 128 * i:128 * i + m], xn[0:m, i, 128:D], ident[0:m, 0:m])
                return last

            def projection_terms(w, cols):
                x_high, x_low, x_rest = (xt_parts[:, a, cols] for a in range(3))
                return [(w0_parts[:, 0, w, :], x_high), (w0_parts[:, 0, w, :], x_low),
                        (w0_parts[:, 1, w, :], x_high), (w1_high[:, w, :], x_rest),
                        (w1_low[:, w, :], xt_parts[0:D1, 2, cols])]

            def attention_job(phase, n, kind, args, b, pr=None):
                g = slot_of(phase, n)
                if kind != "z":
                    slot_free(phase, n, b, pr)
                if kind in ("q", "k"):
                    if kind == "q":
                        wait(pe, "w_split", phase, 0, b, pr)
                    if kind == "q" and phase == TOWER:
                        wait(pe, "dve_freed", TOWER, freed(TOWER, DVE_ENGINE, n - 1), b)
                        wait(pe, "act_freed", TOWER, freed(TOWER, ACT_ENGINE, n - 1), b)
                    w = 0 if kind == "q" else 1
                    for k in range(2):
                        cols = slice(k * TOK // 2, (k + 1) * TOK // 2)
                        terms = projection_terms(w, cols)
                        for m, (weights, x) in enumerate(terms):
                            last = t.matmul(bank(g, k)[:, 0:TOK // 2], weights, x, start=m == 0,
                                            stop=m == len(terms) - 1)
                elif kind == "v":
                    for i in range(TT):
                        m = tile_rows(i)
                        terms = projection_terms(2, slice(128 * i, 128 * i + m))
                        for k, (weights, x) in enumerate(terms):
                            last = t.matmul(slot(g)[0:m, 128 * i:128 * i + 128], x, weights, start=k == 0,
                                            stop=k == len(terms) - 1)
                elif kind == "s":
                    (k,) = args
                    i, hh = k % TT, k % STEPS // TT
                    m = tile_rows(i)
                    if k in (0, STEPS):
                        wait(pe, "head0_stacked", phase, 64, b, pr)
                    if k == TT:
                        wait(pe, "head1_stacked", phase, 0, b, pr)
                    q = q_stack[:, hh, 128 * i:128 * i + m]
                    end = 128 * i + m
                    for lo in range(0, end, 512):
                        hi = min(lo + 512, end)
                        diagonal = lo <= 128 * i < hi
                        t.matmul(slot(g)[0:m, lo:hi], q, k_stack[:, hh, 0, lo:hi], start=True, stop=False)
                        last = t.matmul(slot(g)[0:m, lo:hi], q, k_stack[:, hh, 1, lo:hi], start=False,
                                        stop=not diagonal)
                        if diagonal:
                            last = t.matmul(slot(g)[0:m, 128 * i:end], ident_b[0:m, 0:m], causal_b[0:m, 0:m],
                                            start=False, stop=True)
                elif kind == "pt":
                    (k,) = args
                    i = k % TT
                    m = tile_rows(i)
                    wait(pe, "act_freed", phase, exp_done(phase, k), b, pr)
                    for c in range(i + 1):
                        kk = tile_rows(c)
                        last = t.transpose(slot(g)[0:kk, 128 * c:128 * c + m],
                                           prob[k % PROBS][0:m, 128 * c:128 * c + kk], ident[0:m, 0:m])
                elif kind == "z":
                    (k,) = args
                    i, hh = k % TT, k // TT
                    m = tile_rows(i)
                    if k == 0:
                        wait(pe, "act_freed", phase, 0, b, pr)
                    done = job_index(phase, "pt", (k,))
                    wait(pe, "dve_freed", phase, freed(phase, DVE_ENGINE, done), b, pr)
                    if i >= 4:
                        wait(pe, "act_freed", phase, freed(phase, ACT_ENGINE, done), b, pr)
                    for c in range(i + 1):
                        kk = tile_rows(c)
                        last = t.matmul(slot(g)[0:m, Z_AT:Z_AT + DH], probt[k % 2][0:kk, c, 0:m],
                                        vt[0:kk, c, DH * hh:DH * hh + DH], start=c == 0, stop=c == i)
                else:
                    assert kind == "zt"
                    done = job_index(phase, "z", (STEPS - 1,))
                    wait(pe, "act_freed", phase, freed(phase, ACT_ENGINE, done), b, pr)
                    for i in range(TT):
                        m = tile_rows(i)
                        last = t.transpose(slot(g)[:, 128 * i:128 * i + m], z[0:m, i, :], ident[0:m, 0:m])
                last.then_inc(S["ps_full"], 1)

            with pe.Fori(0, BATCH) as b:
                for n, (kind, args, who) in enumerate(JOBS[TOWER]):
                    g = n
                    if kind in ("q", "k", "v", "s"):
                        attention_job(TOWER, n, kind, args, b)
                        continue
                    slot_free(TOWER, n, b)
                    if kind == "xt":
                        if args[0] == 0:
                            wait(pe, "x_split", TOWER, 1, b)
                        half = NBLK // 2
                        for i in range(half):
                            dst = bank(g, i // 8).bitcast(fp16)[0:3 * WIN, (i % 8) * PITCH:(i % 8 + 1) * PITCH]
                            last = t.transpose(dst, xstack[:, half * args[0] + i, :], ident_h[0:PITCH, 0:PITCH])
                    elif kind == "gram":
                        for k in range(NBLK - 1):
                            x = xa[0:COLS, BLK_STEP * k:BLK_STEP * k + WIN]
                            flags = dict(start=k == 0, stop=k == NBLK - 2)
                            t.matmul(bank(g, 0)[0:WIN, 0:WIN], x, x, **flags)
                            last = t.matmul(bank(g, 1)[0:WIN, 0:1], x, ones_col[0:COLS, :], **flags)
                    elif kind == "taps":
                        wait(pe, "dve_freed", TOWER, freed(TOWER, DVE_ENGINE, n - 1), b)
                        carry_wait(g)
                        for m in range(SUB):
                            o = STRIDE0 * m
                            flags = dict(start=m == 0, stop=False)
                            pick_ = ident[0:WIN, o:o + TAPS0]
                            t.matmul(bank(g, 0)[0:TAPS0, 0:TAPS0], pick_, gram[:, o:o + TAPS0], **flags)
                            t.matmul(bank(g, 1)[0:TAPS0, 0:1], pick_, gram[:, WIN:WIN + 1], **flags)
                        for m in range(SUB):
                            o = BLK_STEP * (NBLK - 1) + STRIDE0 * m
                            cols = COLS - 1 if m == SUB - 1 else COLS
                            flags = dict(start=False, stop=m == SUB - 1)
                            x = xa[0:cols, o:o + TAPS0]
                            t.matmul(bank(g, 0)[0:TAPS0, 0:TAPS0], x, x, **flags)
                            last = t.matmul(bank(g, 1)[0:TAPS0, 0:1], x, ones_col[0:cols, :], **flags)
                    elif kind == "chan":
                        wait(pe, "dve_freed", TOWER, freed(TOWER, DVE_ENGINE, n - 1), b)
                        last = t.matmul(bank(g, 0)[:, 0:TAPS0 + 1], cw0f[:, :], tap_sums[:, :], start=True, stop=True)
                    elif kind == "conv0":
                        j, i = args
                        if args == (0, 0):
                            wait(pe, "dve_freed", TOWER, freed(TOWER, DVE_ENGINE, 1), b)
                        for k in range(2):
                            last = t.matmul(bank(g, k)[:, 0:4 * PITCH], cw0t[:, 2 * i + k, :],
                                            xt[:, 4 * j:4 * j + 4, :].rearrange("p k c -> p (k c)"),
                                            start=True, stop=True)
                    elif kind == "group":
                        wait(pe, "channel_stats", TOWER, args[0] + 1, b)
                        last = t.matmul(bank(g, 0)[:, 0:2], group_avg[:, :], ms[:, :], start=True, stop=True)
                    elif kind == "conv":
                        layer, r, cut = args
                        taps = 2 if layer == 5 else 3
                        parts = [a.rearrange("p (r c) -> p r c", c=PITCH) for a in hs[layer - 1]]
                        terms = [(tap, w, 0) for tap in range(taps) for w in (0, 1)]
                        terms += [(tap, 0, 1) for tap in range(taps)]
                        for k, c in enumerate(cut):
                            need = 2 * (r + c) - 2 + taps - 1
                            if need >= ROWS[layer - 1]:
                                wait(pe, "halo_done", TOWER, layer, b)
                                need = ROWS[layer - 1] - 1
                            unit = split_unit_of(layer - 1, need)
                            wait(pe, "hi_done", TOWER, SPLITS.index(unit) + 1, b)
                            for tap, w, x in terms:
                                if (tap, w, x) == (0, 0, 1):
                                    for engine, name in ((DVE_ENGINE, "lo_dve"), ("pool", "lo_pool")):
                                        wait(pe, name, TOWER, lows(engine, unit), b)
                                f = 2 * r + tap
                                last = t.matmul(bank(g, k)[:, 0:c * PITCH].rearrange("p (r c) -> p r c", c=PITCH),
                                                cwt[layer][:, w, tap, :], parts[x][:, f:f + 2 * c - 1:2, :],
                                                start=(tap, w, x) == terms[0], stop=(tap, w, x) == terms[-1])
                            r += c
                    elif kind == "embed":
                        if args[0] == 0:
                            wait(pe, "norm_done", TOWER, 24, b)
                        tiles = range(4) if args[0] == 0 else range(4, TT)
                        for q, i in enumerate(tiles):
                            m = tile_rows(i)
                            last = t.matmul(bank(g, q // 2)[0:m, (q % 2) * D:(q % 2 + 1) * D],
                                            h5t[:, 128 * i:128 * i + m], pwt[:, :], start=True, stop=True)
                    else:
                        assert kind == "xtr"
                        if args[0] == 0:
                            wait(pe, "xn_ready", TOWER, 1, b)
                        for i in range(TT):
                            m = tile_rows(i)
                            last = t.transpose(bank(g, 0).bitcast(fp16)[:, 128 * i:128 * i + m],
                                               xn_parts[0:m, i, args[0], :], ident_h[0:m, 0:m])
                    last.then_inc(S["ps_full"], 1)

                with pe.Fori(0, PAIRS - 1) as pr:
                    for n, (kind, args, who) in enumerate(JOBS[PAIR]):
                        attention_job(PAIR, n, kind, args, b, pr)
                for n, (kind, args, who) in enumerate(JOBS[LAST_PAIR]):
                    attention_job(LAST_PAIR, n, kind, args, b)

                for n, (kind, args, who) in enumerate(JOBS[POST]):
                    g = slot_of(POST, n)
                    if (kind, args) != ("tr", (1,)):
                        slot_free(POST, n, b)
                    if (kind, args) == ("tr", (0,)):
                        slot_free(POST, n + 1, b)
                    if kind == "wo":
                        tiles = range(4) if args[0] == 0 else range(4, TT)
                        for q, i in enumerate(tiles):
                            m = tile_rows(i)
                            for a in range(PAIRS):
                                last = t.matmul(bank(g, q // 2)[0:m, (q % 2) * D:(q % 2 + 1) * D],
                                                zt[:, a, 128 * i:128 * i + m], wo[:, a, :], start=a == 0,
                                                stop=a == PAIRS - 1)
                    elif kind == "tr":
                        if args[0] == 0:
                            wait(pe, "xn_ready", POST, 1, b)
                        last = token_transposes(g, args[0])
                    elif kind == "gate":
                        wait(pe, "dve_freed", POST, freed(POST, DVE_ENGINE, n - 1), b)
                        wait(pe, "act_freed", POST, freed(POST, ACT_ENGINE, n - 1), b)
                        for i in range(TT):
                            m = tile_rows(i)
                            dst = bank(g, 0)[0:m, EXPERTS * i:EXPERTS * (i + 1)]
                            t.matmul(dst, xnt0[:, 128 * i:128 * i + m], gw0[:, :], start=True, stop=False)
                            last = t.matmul(dst, xnt1[0:D1, 128 * i:128 * i + m], gw1[:, :], start=False, stop=True)
                    else:
                        last = t.transpose(bank(g, 0)[:, 0:128], ident[:, :], ident[:, :])
                    last.then_inc(S["ps_full"], 1)

            wait(pe, "dve_step", MOE, 0)
            wait(pe, "act_freed", MOE, 0)
            wait(pe, "dve_freed", MOE, 0)
            pe.wait_ge(moe_consts, 3)
            choice = onehot[:, :, :].rearrange("p t e -> p (t e)")
            t.matmul(bank(0, 0)[:, 0:TILES * EXPERTS], before, choice, start=True, stop=True)
            t.matmul(bank(0, 1)[:, 0:TILES * EXPERTS], ones, choice, start=True, stop=True).then_inc(rank_full, 1)
            pe.wait_ge(slots_ready, 2)

            def make_xt(j):
                pe.wait_ge(xtile_loaded, 16 * j + 16)
                t.transpose(bank(0, 0)[:, 0:128], xtile[:, 0:128], ident[:, :])
                t.transpose(bank(0, 1)[0:D1, 0:128], xtile[:, 128:D], ident[:, :]).then_inc(xt_full, 1)

            def make_hidden(e, j):
                pe.wait_ge(xt_taken, j + 1)
                for k in range(2):
                    f = slice(k * FF // 2, (k + 1) * FF // 2)
                    wa = w1a[:, bass.ds(e, 1), f].rearrange("p a f -> p (a f)")
                    wb = w1b[0:D1 + 1, bass.ds(e, 1), f].rearrange("p a f -> p (a f)")
                    t.matmul(bank(1, k)[:, 0:FF // 2], xe0, wa, start=True, stop=False)
                    last = t.matmul(bank(1, k)[:, 0:FF // 2], xe1[0:D1 + 1, :], wb, start=False, stop=True)
                last.then_inc(hid_full, 1)

            def make_hidt(j):
                pe.wait_ge(hid_taken, j + 1)
                for c in range(FF // 128):
                    last = t.transpose(slot(2)[:, 128 * c:128 * c + 128], hid[:, 128 * c:128 * c + 128], ident[:, :])
                last.then_inc(hidt_full, 1)

            def make_y(e, j, first=False):
                pe.wait_ge(hidt_taken_dve, j + 1)
                pe.wait_ge(hidt_taken_act, j + 1)
                if not first:
                    pe.wait_ge(y_taken, j)
                dst = bank(3, 0)[:, 0:D]
                for c in range(FF // 128):
                    w = w2[:, bass.ds(e, 1), c, :].rearrange("p a d -> p (a d)")
                    t.matmul(dst, hidt[:, c, :], w, start=c == 0, stop=False)
                t.matmul(dst, ones[0:1, :], b2[0:1, bass.ds(e, 1), :].rearrange("p a d -> p (a d)"), start=False,
                         stop=True).then_inc(y_full, 1)

            def expert_of(j):
                return pe.value_load(tile_expert[0:1, bass.ds(j, 1)] if not isinstance(j, int)
                                     else tile_expert[0:1, j:j + 1], min_val=0, max_val=EXPERTS - 1)

            pe.wait_ge(moe_consts, N_MOE_CONSTS)
            make_xt(0)
            pe.wait_ge(experts_loaded, 16 * (3 * EXPERTS + 2))
            make_hidden(expert_of(0), 0)
            make_xt(1)
            make_hidt(0)
            make_hidden(expert_of(1), 1)
            make_xt(2)
            make_y(expert_of(0), 0, first=True)
            make_hidt(1)
            with pe.Fori(2, SLOT_TILES - 1) as j:
                make_hidden(expert_of(j), j)
                make_xt(j + 1)
                make_y(expert_of(j - 1), j - 1)
                make_hidt(j)
            last_tile = SLOT_TILES - 1
            make_hidden(expert_of(last_tile), last_tile)
            make_y(expert_of(last_tile - 1), last_tile - 1)
            make_hidt(last_tile)
            make_y(expert_of(last_tile), last_tile)


_INS = (["x"] + [f"L0_tok_{p}{l}" for l in range(CONV_LAYERS) for p in ("cw", "cb", "gw", "gb")]
        + ["L0_tok_pw", "L0_tok_pb"] + [f"L0_attn_{p}_{q}" for q in "QKVO" for p in ("W", "b")]
        + ["L0_ffn_gate_w", "L0_ffn_gate_b", "L0_ffn_w1", "L0_ffn_b1", "L0_ffn_w2", "L0_ffn_b2"])


def kernel(**inputs):
    import concourse.bacc as bacc
    from concourse.bass_utils import run_bass_kernel_spmd

    nc = bacc.Bacc("TRN2", target_bir_lowering=False, num_devices=1)
    arrays, args = {}, {}
    for name in _INS:
        a = np.ascontiguousarray(inputs[name])
        arrays[f"in_{name}"] = a
        args[name] = nc.dram_tensor(f"in_{name}", a.shape, mybir.dt.from_np(a.dtype), kind="ExternalInput").ap()
    out = nc.dram_tensor("out", (BATCH, SEQ, D), mybir.dt.float32, kind="ExternalOutput").ap()
    audio_tower(nc, args, out)
    r = run_bass_kernel_spmd(nc, [arrays], core_ids=[0])
    return r.results[0]["out"]
```

```python
from contextlib import ExitStack

import numpy as np
import concourse.bass as bass
from concourse import mybir

BATCH, SAMPLES = 4, 120000
COLS, PITCH = 125, 126
ROWS = [192, 96, 48, 24, 12, 6]
CONV_LAYERS, CH, GROUP = 6, 128, 4
TAPS0, STRIDE0 = 10, 5
PER_COL = SAMPLES // COLS
SUB, NBLK = 6, 32
WIN = STRIDE0 * (SUB - 1) + TAPS0
WSCALE = 64.0
BLK_STEP = SUB * STRIDE0
D, HEADS, DH, EXPERTS, FF = 192, 12, 64, 8, 768
D1 = D - 128
PAIRS = HEADS // 2
TOK = ROWS[5] * COLS
SEQ = TOK - 1
TT = -(-TOK // 128)
LASTM = TOK - 128 * (TT - 1)
TILES = BATCH * TT
SLOT_TILES = (BATCH * SEQ + EXPERTS * 127) // 128
ROW = 2 * D + 1
NO_TOKEN = 1 << 20
EPS = 1e-5
SCALE = DH ** -0.5
MASKED = -8.0e5
ACT_ENGINE, DVE_ENGINE = "act", "dve"


def tile_rows(i):
    return LASTM if i == TT - 1 else 128


def tower_jobs():
    jobs = []
    t = 0
    for j in range(8):
        jobs += [("conv0", (j, i), (ACT_ENGINE,)) for i in range(3)]
        while t < ROWS[1] // 8 and min(16 * t + 16, ROWS[0] - 1) // 24 <= j - 1:
            jobs.append(("conv", (1, 8 * t, (4, 4)), (ACT_ENGINE,)))
            t += 1
    while t < ROWS[1] // 8 - 1:
        jobs.append(("conv", (1, 8 * t, (4, 4)), (ACT_ENGINE,)))
        t += 1
    jobs += [("conv", (1, r, (4,)), (ACT_ENGINE,)) for r in (ROWS[1] - 8, ROWS[1] - 4)]
    jobs.append(("group", (1,), (DVE_ENGINE,)))
    for layer in range(2, CONV_LAYERS):
        r = 0
        while r < ROWS[layer]:
            cut = (3, 3) if layer == 5 else (2, 2) if r == 0 else (4, 4) if ROWS[layer] - r > 8 else (4,)
            jobs.append(("conv", (layer, r, cut), (ACT_ENGINE,)))
            r += sum(cut)
        jobs.append(("group", (layer,), (DVE_ENGINE,)))
    jobs += [("embed", (0,), (DVE_ENGINE,)), ("embed", (1,), (DVE_ENGINE,))]
    jobs += [("xtr", (0,), (DVE_ENGINE,)), ("xtr", (1,), (ACT_ENGINE,)), ("xtr", (2,), (DVE_ENGINE,))]
    jobs += [("q", (), (ACT_ENGINE,)), ("k", (), (ACT_ENGINE,)), ("v", (), (ACT_ENGINE,))]
    jobs += [("s", (k,), (ACT_ENGINE,)) for k in range(2)]
    return jobs


PROBS = 3
Z_AT = TT * 128
TILE_ORDER = (0, 4, 1, 5, 2, 3)
STEPS = 2 * TT


def pair_jobs(last):
    jobs = []
    for k in range(STEPS):
        ahead = k + 2
        if ahead < STEPS:
            jobs.append(("s", (ahead,), (ACT_ENGINE,)))
        elif ahead == STEPS + 1 and not last:
            jobs.append(("s", (STEPS,), (ACT_ENGINE,)))
        if k in (TT - 1, TT) and not last:
            jobs.append(("q" if k == TT - 1 else "k", (), (ACT_ENGINE,)))
        jobs.append(("pt", (k,), (DVE_ENGINE, ACT_ENGINE) if TILE_ORDER[k % TT] >= 4 else (DVE_ENGINE,)))
        if k:
            jobs.append(("z", (k - 1,), (ACT_ENGINE,)))
    if not last:
        jobs.append(("s", (STEPS + 1,), (ACT_ENGINE,)))
    jobs.append(("z", (STEPS - 1,), (ACT_ENGINE,)))
    if not last:
        jobs.append(("v", (), (ACT_ENGINE,)))
    jobs.append(("zt", (), (DVE_ENGINE,)))
    return jobs


def samples_jobs():
    return [("xt", (0,), (DVE_ENGINE,)), ("xt", (1,), (DVE_ENGINE,)), ("gram", (), (DVE_ENGINE,)),
            ("taps", (), (DVE_ENGINE,)), ("chan", (), (DVE_ENGINE,)), ("group", (0,), (DVE_ENGINE,))]


def post_jobs():
    jobs = [("wo", (0,), (DVE_ENGINE,)), ("wo", (1,), (DVE_ENGINE,))]
    xt0, xt1, gram, taps, chan, group = samples_jobs()
    jobs += [xt0, xt1, gram, ("tr", (0,), (DVE_ENGINE,)), ("tr", (1,), (ACT_ENGINE,)), taps,
             chan, ("gate", (), (DVE_ENGINE,)), group]
    return jobs


def setup_jobs():
    jobs = [("cwt", (l,), (DVE_ENGINE,)) for l in range(1, CONV_LAYERS)]
    jobs += [("cw0t", (), (ACT_ENGINE,)), ("pwt", (), (ACT_ENGINE,))] + samples_jobs()
    return jobs + [("pad", (), (ACT_ENGINE,))] * (-len(jobs) % 4)


SETUP, TOWER, PAIR, LAST_PAIR, POST, MOE = range(6)
JOBS = {SETUP: setup_jobs(), TOWER: tower_jobs(), PAIR: pair_jobs(False), LAST_PAIR: pair_jobs(True),
        POST: post_jobs()}


def ring_length(phase):
    return sum(job[0] != "z" for job in JOBS[phase])


while (ring_length(TOWER) + ring_length(LAST_PAIR) + ring_length(POST)) % 4:
    JOBS[POST].append(("pad", (), (DVE_ENGINE,)))
assert ring_length(SETUP) % 4 == 0 and ring_length(PAIR) % 4 == 0
PHASES = (SETUP, TOWER, PAIR, LAST_PAIR, POST)


def ring_positions(phase):
    positions, r, of_pt = [], 0, {}
    for kind, args, _ in JOBS[phase]:
        if kind == "z":
            positions.append(of_pt[args])
            continue
        if kind == "pt":
            of_pt[args] = r
        positions.append(r)
        r += 1
    return positions


RING = {f: ring_positions(f) for f in PHASES}
RING0 = {SETUP: 0, TOWER: 0, PAIR: ring_length(TOWER), LAST_PAIR: ring_length(TOWER),
         POST: ring_length(TOWER) + ring_length(LAST_PAIR)}


def slot_of(phase, n):
    return RING0[phase] + RING[phase][n]


def readers(phase, engine):
    return sum(engine in job[2] for job in JOBS[phase])


NORM_CHUNKS = {1: [5, 4] + [8] * 10 + [7], 2: [5, 4] + [8] * 4 + [7], 3: [5, 4, 8, 7], 4: [6, 6], 5: [6]}
SPLITS = [(0, d) for d in range(24)] + [(l, c) for l in range(1, 5) for c in range(len(NORM_CHUNKS[l]))]
STAGES = 4


def low_engine(layer, piece):
    if layer == 0:
        return DVE_ENGINE if piece % 3 == 2 else "pool"
    return "pool" if piece % 2 else DVE_ENGINE


COUNTS = {
    "ps_full": tuple(len(JOBS[f]) for f in PHASES),
    "act_freed": tuple(readers(f, ACT_ENGINE) for f in PHASES),
    "dve_freed": tuple(readers(f, DVE_ENGINE) for f in PHASES),
    "x_loaded": (32, 32, 0, 0, 0),
    "var_ready": (1, CONV_LAYERS, 0, 0, 2),
    "rstd_ready": (1, CONV_LAYERS, 0, 0, 2),
    "x_split": (2, 0, 0, 0, 1),
    "channel_stats": (1, CONV_LAYERS - 1, 0, 0, 1),
    "affine_ready": (1, CONV_LAYERS - 1, 0, 0, 1),
    "norm_done": (0, sum(len(c) for c in NORM_CHUNKS.values()), 0, 0, 0),
    "hi_done": (0, len(SPLITS), 0, 0, 0),
    "lo_dve": (0, sum(low_engine(*u) == DVE_ENGINE for u in SPLITS), 0, 0, 0),
    "lo_pool": (0, sum(low_engine(*u) == "pool" for u in SPLITS), 0, 0, 0),
    "halo_done": (0, 4, 0, 0, 0),
    "xn_ready": (0, 1, 0, 0, 1),
    "w_loaded": (288, 144, 144, 0, 0),
    "w_split": (1, 1, 1, 0, 0),
    "w_step": (1, 1, 1, 0, 0),
    "xn_high": (0, 1, 0, 0, 0),
    "q_high": (0, 0, 1, 0, 0),
    "k_high": (0, 0, 1, 0, 0),
    "parts_ready": (0, 1, 1, 0, 0),
    "head0_stacked": (0, 64, 64, 0, 0),
    "head1_stacked": (0, 64, 64, 0, 0),
    "smax_done": (0, 2, STEPS, STEPS - 2, 0),
    "rinv_ready": (0, 0, STEPS, STEPS, 0),
    "h1_ready": (0, 0, 0, 0, 1),
    "scratch_stored": (16, 0, 0, 0, 64),
    "dve_step": (14, 35, STEPS, STEPS - 2, 16),
}
def lows(engine, unit):
    return sum(low_engine(*u) == engine for u in SPLITS[:SPLITS.index(unit) + 1])


def split_unit_of(layer, row):
    if layer == 0:
        return (0, 3 * (row // 24) + 2)
    return (layer, next(c for c in range(len(NORM_CHUNKS[layer])) if row < sum(NORM_CHUNKS[layer][:c + 1])))


def at(sem, phase, k, b=None, pr=None):
    setup, *each = COUNTS[sem]
    tower, pair, last_pair, post = each
    before_last = tower + (PAIRS - 1) * pair
    if phase == SETUP:
        return k
    period = before_last + last_pair + post
    if phase == MOE:
        return setup + BATCH * period + k
    base = b * period + setup
    if phase == PAIR:
        return base + pr * pair + (tower + k) if pair else base + (tower + k)
    return base + ({TOWER: 0, LAST_PAIR: before_last, POST: before_last + last_pair}[phase] + k)


def act_order(phase):
    order, held = [], None
    for n, (kind, args, who) in enumerate(JOBS[phase]):
        if ACT_ENGINE not in who:
            continue
        if kind == "s" and phase in (PAIR, LAST_PAIR):
            if held is not None:
                order.append(held)
            held = n
            continue
        order.append(n)
        if kind == "z" and held is not None:
            order.append(held)
            held = None
    assert held is None
    return order


ACT_ORDER = {f: act_order(f) for f in PHASES}


def freed(phase, engine, n):
    if engine == ACT_ENGINE and phase in (PAIR, LAST_PAIR):
        return ACT_ORDER[phase].index(n) + 1
    return sum(engine in job[2] for job in JOBS[phase][:n + 1])


def norm_chunk_of(layer, row):
    before = sum(len(NORM_CHUNKS[i]) for i in range(1, layer))
    edge = 0
    for n, rows in enumerate(NORM_CHUNKS[layer]):
        edge += rows
        if row < edge:
            return before + n + 1


def job_index(phase, kind, args):
    return next(n for n, job in enumerate(JOBS[phase]) if job[0] == kind and job[1] == args)


def exp_done(phase, k):
    if k < 2 and phase != TOWER:
        return k - 1
    return freed(phase, ACT_ENGINE, job_index(phase, "s", (k,)))


def transposed_before(phase, k):
    if k < 0:
        return job_index(PAIR, "pt", (k + STEPS,)) + 1 - len(JOBS[PAIR])
    return job_index(phase, "pt", (k,)) + 1


def audio_tower(nc, ins, out):
    fp32, fp16, bf16, i32 = mybir.dt.float32, mybir.dt.float16, mybir.dt.bfloat16, mybir.dt.int32
    ALU, ACT, AX = mybir.AluOpType, mybir.ActivationFunctionType, mybir.AxisListType

    h1_dram = nc.dram_tensor("h1_scratch", (TILES, 128, D), fp32, kind="Internal").ap()
    x2_dram = nc.dram_tensor("x2_scratch", (TILES, 128, D), fp32, kind="Internal").ap()
    slot_dram = nc.dram_tensor("slot_scratch", (SLOT_TILES * 128, ROW), fp32, kind="Internal").ap()

    ctx = ExitStack()
    with ctx:
        def sb(name, shape, dt=fp32):
            return ctx.enter_context(nc.sbuf_tensor(name, shape, dt))

        def sem(name):
            return ctx.enter_context(nc.semaphore(name))

        ident = sb("ident", [128, 128])
        ident_h = sb("ident_h", [128, 128], fp16)
        ident_b = sb("ident_b", [128, 128], bf16)
        causal_b = sb("causal_b", [128, 128], bf16)
        group_avg = sb("group_avg", [128, 128])
        cwt = [None] + [sb(f"cwt{l}", [CH, 2, 2 if l == 5 else 3, CH], fp16) for l in range(1, CONV_LAYERS)]
        cw0t = sb("cw0t", [3 * WIN, SUB, CH], fp16)
        cw0n = sb("cw0n", [CH, TAPS0])
        cw0s = sb("cw0s", [CH, TAPS0])
        cw0f = sb("cw0f", [TAPS0, CH])
        gram = sb("gram", [WIN, WIN + 1])
        tap_sums = sb("tap_sums", [TAPS0, TAPS0 + 1])
        quad = sb("quad", [CH, TAPS0])
        ones_col = sb("ones_col", [128, 1])
        wscale_col = sb("wscale_col", [128, 1])
        carry = sb("carry", [128, 2])
        pwt = sb("pwt", [CH, D])
        channel_par = sb("channel_par", [CH, 3, CONV_LAYERS])
        pb_b = sb("pb_b", [128, D])
        bo_b = sb("bo_b", [128, D])
        gate_b = sb("gate_b", [128, EXPERTS])
        gw0 = sb("gw0", [128, EXPERTS])
        gw1 = sb("gw1", [D1, EXPERTS])
        wo = sb("wo", [128, PAIRS, D])
        bqkv = sb("bqkv", [128, 3, PAIRS])
        wqkv0 = sb("wqkv0", [128, 3, 128])
        wqkv1 = sb("wqkv1", [128, 3, 128])
        w0_parts = sb("w0_parts", [128, 2, 3, 128], fp16)
        w1_high = sb("w1_high", [128, 3, 128], fp16)
        w1_low = sb("w1_low", [D1, 3, 128], fp16)
        onehot = sb("onehot", [128, TILES, EXPERTS])
        prefer = sb("prefer", [128, EXPERTS])
        bn = sb("bn", [128, 49, 6])
        mv = sb("mv", [128, 2])
        ms = sb("ms", [128, 2])
        gm = sb("gm", [128, 2])
        tmp = sb("tmp", [128, 4])
        spare = sb("spare", [128, 32])
        affine = sb("affine", [128, 2])
        lnmv = sb("lnmv", [128, TT, 2])
        lnr = sb("lnr", [128, TT])
        lnv = sb("lnv", [128, TT])
        neg_half = sb("neg_half", [128, TT])
        smax = sb("smax", [128, STEPS])
        nmax = sb("nmax", [128, STEPS])
        rsum = sb("rsum", [128, STEPS])
        rinv = sb("rinv", [128, STEPS])
        logits = sb("logits", [128, TT, EXPERTS])
        pick = sb("pick", [128, TT, EXPERTS])
        best = sb("best", [128, TT])
        empty_slot = sb("empty_slot", [128, ROW])
        xa = sb("xa", [PITCH, PER_COL + BLK_STEP + 2])
        xstack = sb("xstack", [PITCH, NBLK, 3 * WIN], fp16)
        xt = sb("xt", [3 * WIN, NBLK, PITCH], fp16)

        H0, Y1 = (ROWS[0] + 1) * PITCH, (ROWS[1] + 1) * PITCH
        STAGE = 8 * PITCH
        ARENA = H0 + Y1 + STAGES * STAGE
        arena = sb("arena", [128, ARENA])
        stage = arena[:, H0 + Y1:ARENA].rearrange("p (s n) -> p s n", s=STAGES)

        def rows_at(first, layer):
            return arena[:, first:first + (ROWS[layer] + 1) * PITCH]

        Y2, Y3, Y4, Y5 = Y1, H0 + 49 * PITCH, 30 * PITCH, H0 + 80 * PITCH
        ys = [None, rows_at(H0, 1), rows_at(Y2, 2), rows_at(Y3, 3), rows_at(Y4, 4), rows_at(Y5, 5)]
        hs = []
        for l, first in enumerate((0, 0, H0, 0, H0)):
            both = rows_at(first, l).bitcast(fp16)
            n = (ROWS[l] + 1) * PITCH
            hs.append((both[:, 0:n], both[:, n:2 * n]))
        cursor = [0]

        def take(n):
            a = arena[:, cursor[0]:cursor[0] + n]
            cursor[0] += n
            return a

        h5t = take(TOK)
        h = take(TT * D).rearrange("p (t d) -> p t d", d=D)
        xn = take(TT * D).rearrange("p (t d) -> p t d", d=D)
        xn_parts = take(TT * D).bitcast(fp16).rearrange("p (t a d) -> p t a d", t=TT, a=3)
        xt_parts = take(3 * TOK // 2).bitcast(fp16).rearrange("p (a t) -> p a t", a=3)
        xnt0 = take(TT * 128)
        xnt1 = take(TT * 128)
        zt = take(PAIRS * TT * 128).rearrange("p (a t) -> p a t", a=PAIRS)
        heads_first = cursor[0]
        q_full, k_full = take(TOK), take(TOK)
        q_parts = take(TOK).bitcast(fp16).rearrange("p (a t) -> p a t", a=2)
        k_parts = take(TOK).bitcast(fp16).rearrange("p (a t) -> p a t", a=2)
        q_stack = take(TOK).bitcast(fp16).rearrange("p (h t) -> p h t", h=2)
        k_stack = take(2 * TOK).bitcast(fp16).rearrange("p (h a t) -> p h a t", h=2, a=2)
        vt = take(TT * 128).rearrange("p (t c) -> p t c", c=128)
        prob = [take(TT * 128) for _ in range(PROBS)]
        probt = [take(TT * 128).rearrange("p (t c) -> p t c", c=128) for _ in range(2)]
        z = take(TT * 128).rearrange("p (t c) -> p t c", c=128)
        attention_end = cursor[0]

        cursor[0] = 0
        cwn = [None] + [take((2 if l == 5 else 3) * CH) for l in range(1, CONV_LAYERS)]
        cw0pad = take(SUB * 3 * WIN // 2).bitcast(fp16).rearrange("p (m k) -> p m k", m=SUB)
        pwn = take(2 * CH).rearrange("p (a c) -> p a c", a=2)

        cursor[0] = ARENA - EXPERTS * (FF + PAIRS * D + D)
        assert cursor[0] >= attention_end
        w1b = take(EXPERTS * FF).rearrange("p (e f) -> p e f", e=EXPERTS)
        w2 = take(EXPERTS * PAIRS * D).rearrange("p (e c d) -> p e c d", e=EXPERTS, c=FF // 128)
        b2 = take(EXPERTS * D).rearrange("p (e d) -> p e d", e=EXPERTS)
        cursor[0] = 0
        rows_of_tokens = take(TILES * ROW).rearrange("p (t r) -> p t r", r=ROW)
        before = take(128)
        ones = take(128)
        rank = take(TILES * EXPERTS).rearrange("p (t e) -> p t e", e=EXPERTS)
        per_tile = take(TILES * EXPERTS)
        running = take(TILES * EXPERTS)
        segment = take(TILES * EXPERTS)
        edges = take(TILES)
        counts = take(EXPERTS)
        ntiles = take(EXPERTS)
        tiles_end = take(EXPERTS)
        base = take(EXPERTS)
        slots_f = take(TILES)
        slots = take(TILES).bitcast(i32)
        tile_ids = take(32)
        tile_expert_f = take(32)
        tile_expert = take(32).bitcast(i32)
        over = take(32 * EXPERTS).rearrange("p (j e) -> p j e", e=EXPERTS)
        assert cursor[0] <= heads_first
        cursor[0] = heads_first
        w1a = take(EXPERTS * FF).rearrange("p (e f) -> p e f", e=EXPERTS)
        xtile, rest, out_tile, hid = [], [], [], []
        xe0, xe1, hidt = [], [], []
        for _ in range(2):
            xtile.append(take(D))
            rest.append(take(D + 1))
            xe0.append(take(128))
            xe1.append(take(128))
            hid.append(take(FF))
            hidt.append(take(FF).rearrange("p (c t) -> p c t", c=FF // 128))
            out_tile.append(take(D))
        assert cursor[0] <= ARENA - EXPERTS * (FF + PAIRS * D + D), cursor[0]

        ps = ctx.enter_context(nc.psum_tensor("ps", [128, 8 * 512], fp32))

        def slot(n):
            return ps[:, (n % 4) * 1024:(n % 4 + 1) * 1024]

        def bank(n, i):
            return ps[:, (n % 4) * 1024 + 512 * i:(n % 4) * 1024 + 512 * i + 512]

        S = {name: sem(name) for name in COUNTS}
        consts_ready = sem("consts_ready")
        weights_loaded = sem("weights_loaded")
        params_loaded = sem("params_loaded")
        slots_cleared = sem("slots_cleared")
        pads_ready = sem("pads_ready")
        cw0_stacked = sem("cw0_stacked")
        experts_loaded = sem("experts_loaded")
        tokens_loaded = [sem(f"tokens_loaded_{b}") for b in range(BATCH)]
        moe_consts = sem("moe_consts")
        slots_ready = sem("slots_ready")
        scattered = sem("scattered")
        xtile_loaded = [sem(f"xtile_loaded_{par}") for par in range(2)]
        rest_loaded = [sem(f"rest_loaded_{par}") for par in range(2)]
        scatter_begun = [sem(f"scatter_begun_{par}") for par in range(2)]
        out_scattered = [sem(f"out_scattered_{par}") for par in range(2)]
        rank_full = sem("rank_full")
        xt_full, hid_full, hidt_full, y_full = sem("xt_full"), sem("hid_full"), sem("hidt_full"), sem("y_full")
        xt_taken, hid_taken, y_taken = sem("xt_taken"), sem("hid_taken"), sem("y_taken")
        hidt_taken_dve, hidt_taken_act = sem("hidt_taken_dve"), sem("hidt_taken_act")
        N_CONSTS = 15
        N_MOE_CONSTS = 12
        block = ctx.enter_context(nc.Block())

        def wait(eng, name, phase, k, b=None, pr=None):
            assert at(name, phase, k, 0, 0) > 0, (name, phase, k)
            eng.wait_ge(S[name], at(name, phase, k, b, pr))

        def first_layer_rows(a, piece):
            j, i = piece // 3, piece % 3
            rows = a[:, 24 * j * PITCH:24 * (j + 1) * PITCH].rearrange("p (k m c) -> p m k c", m=SUB, c=PITCH)
            return rows[:, 2 * i:2 * i + 2, :, :]

        def split_views(layer, piece):
            if layer == 0:
                src = stage[:, piece % STAGES, :].rearrange("p (m k c) -> p m k c", m=2, c=PITCH)
                return src, first_layer_rows(hs[0][0], piece), first_layer_rows(hs[0][1], piece)
            r = sum(NORM_CHUNKS[layer][:piece])
            cut = slice(r * PITCH, (r + NORM_CHUNKS[layer][piece]) * PITCH)
            return ys[layer][:, cut], hs[layer][0][:, cut], hs[layer][1][:, cut]

        n_dmas = {weights_loaded: 0, params_loaded: 0}

        @block.sync
        def _(sp):
            def load(dst, src, loaded=params_loaded):
                sp.dma_start(dst, src, allow_slow_non_contiguous=True).then_inc(loaded, 16)
                n_dmas[loaded] += 1

            def col(a):
                return a.rearrange("(p a) -> p a", a=1)

            load(cw0n[:, :], ins["L0_tok_cw0"].rearrange("o i k -> o (i k)"), weights_loaded)
            for l in range(1, CONV_LAYERS):
                load(cwn[l], ins[f"L0_tok_cw{l}"].rearrange("o i k -> o (i k)"), weights_loaded)
            load(pwn[:, 0, :], ins["L0_tok_pw"][0:128, :], weights_loaded)
            load(pwn[0:D1, 1, :], ins["L0_tok_pw"][128:D, :], weights_loaded)
            for l in range(CONV_LAYERS):
                for n, name in enumerate(("cb", "gw", "gb")):
                    load(channel_par[:, n, l:l + 1], col(ins[f"L0_tok_{name}{l}"]))
            load(pb_b[:, :], ins["L0_tok_pb"].partition_broadcast(128))
            load(bo_b[:, :], ins["L0_attn_b_O"].partition_broadcast(128))
            load(gate_b[:, :], ins["L0_ffn_gate_b"].partition_broadcast(128))
            load(gw0[:, :], ins["L0_ffn_gate_w"][0:128, :])
            load(gw1[:, :], ins["L0_ffn_gate_w"][128:D, :])
            load(wo[:, :, :], ins["L0_attn_W_O"].rearrange("(a h) m d -> (h m) a d", h=2))
            for n, name in enumerate("QKV"):
                for hh in range(2):
                    load(bqkv[DH * hh:DH * hh + DH, n, :],
                         ins[f"L0_attn_b_{name}"].rearrange("(a h) m -> h m a", h=2)[hh, :, :])

            def load_pair(pr):
                for n, name in enumerate("QKV"):
                    w = ins[f"L0_attn_W_{name}"].rearrange("(a h) d m -> a d h m", h=2)
                    for buf, rows in ((wqkv0, (0, 128)), (wqkv1[0:D1], (128, D)), (wqkv1[D1:128], (128, D))):
                        if isinstance(pr, int):
                            src = w[pr, rows[0]:rows[1], :, :]
                        else:
                            src = w[bass.ds(pr, 1), rows[0]:rows[1], :, :].rearrange("a d h m -> (a d) h m")
                        sp.dma_start(buf[:, n, :].rearrange("p (h m) -> p h m", h=2), src
                                     ).then_inc(S["w_loaded"], 16)

            def stack_heads(phase, b, pr=None):
                wait(sp, "parts_ready", phase, 1, b, pr)
                for hh in range(2):
                    if hh == 1 and phase == PAIR:
                        wait(sp, "ps_full", phase, job_index(phase, "s", (STEPS - 1,)) + 1, b, pr)
                    rows = slice(DH * hh, DH * hh + DH)
                    for part in range(2):
                        half = slice(DH * part, DH * part + DH)
                        sp.dma_start(q_stack[half, hh, :], q_parts[rows, part, :]
                                     ).then_inc(S[f"head{hh}_stacked"], 16)
                        sp.dma_start(k_stack[half, hh, :, :], k_parts[rows, :, :]
                                     ).then_inc(S[f"head{hh}_stacked"], 16)

            load_pair(0)
            sp.wait_ge(pads_ready, 3)
            sp.dma_start(slot_dram[0:128, :], empty_slot[:, :]).then_inc(S["scratch_stored"], 16)
            sp.wait_ge(S["w_split"], 1)
            load_pair(1)
            sp.dma_start(slot_dram[128:SLOT_TILES * 128, :].rearrange("(t p) d -> p t d", p=128),
                         empty_slot[:, :].unsqueeze(1).to_broadcast([128, SLOT_TILES - 1, ROW])
                         ).then_inc(slots_cleared, 16)

            def store_tokens(b):
                wait(sp, "h1_ready", POST, 1, b)
                for src, dst in ((h, h1_dram), (xn, x2_dram)):
                    full = dst[bass.ds(b * TT, TT - 1), :, :].rearrange("t p d -> p t d")
                    sp.dma_start(full, src[:, 0:TT - 1, :]).then_inc(S["scratch_stored"], 16)
                    last = dst[bass.ds(b * TT + TT - 1, 1), 0:LASTM, :].rearrange("t p d -> p t d")
                    sp.dma_start(last, src[0:LASTM, TT - 1:TT, :]).then_inc(S["scratch_stored"], 16)

            with sp.Fori(0, BATCH - 1) as b:
                stack_heads(TOWER, b)
                wait(sp, "w_split", TOWER, 1, b)
                load_pair(2)
                with sp.Fori(0, PAIRS - 3) as pr:
                    stack_heads(PAIR, b, pr)
                    wait(sp, "w_split", PAIR, 1, b, pr)
                    load_pair(pr + 3)
                for pr in (PAIRS - 3, PAIRS - 2):
                    stack_heads(PAIR, b, pr)
                    wait(sp, "w_split", PAIR, 1, b, pr)
                    load_pair(pr + 3 - PAIRS)
                store_tokens(b)

            b = BATCH - 1

            def load_experts(some):
                for e in some:
                    sp.dma_start(w1b[0:D1, e, :], ins["L0_ffn_w1"][e, 128:D, :]).then_inc(experts_loaded, 16)
                    sp.dma_start(w2[:, e, :, :], ins["L0_ffn_w2"][e, :, :].rearrange("(c p) d -> p c d", p=128)
                                 ).then_inc(experts_loaded, 16)

            stack_heads(TOWER, b)
            wait(sp, "w_split", TOWER, 1, b)
            load_pair(2)
            load_experts(range(0, 2))
            sp.dma_start(w1b[D1:D1 + 1, :, :], ins["L0_ffn_b1"].unsqueeze(0)).then_inc(experts_loaded, 16)
            sp.dma_start(b2[0:1, :, :], ins["L0_ffn_b2"].unsqueeze(0)).then_inc(experts_loaded, 16)
            for pr in range(PAIRS - 1):
                stack_heads(PAIR, b, pr)
                wait(sp, "w_split", PAIR, 1, b, pr)
                load_pair((pr + 3) % PAIRS)
                load_experts(range(2 + 2 * pr, min(4 + 2 * pr, EXPERTS)))
            wait(sp, "ps_full", LAST_PAIR, len(JOBS[LAST_PAIR]), b)
            for e in range(EXPERTS):
                if e == EXPERTS // 2:
                    store_tokens(b)
                sp.dma_start(w1a[:, e, :], ins["L0_ffn_w1"][e, 0:128, :]).then_inc(experts_loaded, 16)

            wait(sp, "scratch_stored", MOE, 0)
            wait(sp, "ps_full", MOE, 0)
            for b in range(BATCH):
                for first, dram in ((0, x2_dram), (D, h1_dram)):
                    tile = rows_of_tokens[:, :, first:first + D]
                    sp.dma_start(tile[:, b * TT:b * TT + TT - 1, :],
                                 dram[b * TT:b * TT + TT - 1, :, :].rearrange("t p d -> p t d")
                                 ).then_inc(tokens_loaded[b], 16)
                    sp.dma_start(tile[0:LASTM, b * TT + TT - 1, :], dram[b * TT + TT - 1, 0:LASTM, :]
                                 ).then_inc(tokens_loaded[b], 16)

            def load_x(i, par, first=False):
                j = i * 2 + par
                if not first:
                    sp.wait_ge(xt_full, j - 1)
                sp.dma_start(xtile[par], slot_dram[bass.ds(j * 128, 128), 0:D]).then_inc(xtile_loaded[par], 16)

            def load_rest(i, par, first=False):
                j = i * 2 + par
                if not first:
                    sp.wait_ge(out_scattered[par], i * 16)
                    sp.wait_ge(scatter_begun[par], i)
                sp.dma_start(rest[par], slot_dram[bass.ds(j * 128, 128), D:ROW]).then_inc(rest_loaded[par], 16)

            sp.wait_ge(scattered, 16 * TILES)
            for par in range(2):
                load_x(0, par, first=True)
            for par in range(2):
                load_rest(0, par, first=True)
            for par in range(2):
                load_x(1, par)
            with sp.Fori(1, SLOT_TILES // 2 - 1) as i:
                for par in range(2):
                    load_x(i + 1, par)
                for par in range(2):
                    load_rest(i, par)
            load_x(SLOT_TILES // 2, 0)
            for par in range(2):
                load_rest(SLOT_TILES // 2 - 1, par)
            load_rest(SLOT_TILES // 2, 0)
            sp.wait_ge(out_scattered[0], 16 * (SLOT_TILES // 2 + 1))
            sp.wait_ge(out_scattered[1], 16 * (SLOT_TILES // 2))

        @block.gpsimd
        def _(pool):
            steps = [0]

            def const(ins_, wait_last=True):
                steps[0] += 1
                ins_.then_inc(consts_ready, 1)
                if wait_last:
                    pool.wait_ge(consts_ready, steps[0])

            g = nc.gpsimd
            for m in (ident, ident_h, ident_b):
                const(g.memset(m[:, :], 0.0))
                const(g.affine_select(out=m[:, :], in_=m[:, :], compare_op=ALU.not_equal, fill=1.0, base=0,
                                      pattern=[[-1, 128]], channel_multiplier=1))
            const(g.memset(causal_b[:, :], 0.0))
            const(g.affine_select(out=causal_b[:, :], in_=causal_b[:, :], compare_op=ALU.is_ge, fill=MASKED,
                                  base=0, pattern=[[-1, 128]], channel_multiplier=1))
            const(g.memset(group_avg[:, :], 1.0 / GROUP))
            const(g.affine_select(out=group_avg[:, :], in_=group_avg[:, :], compare_op=ALU.is_ge, fill=0.0,
                                  base=0, pattern=[[-GROUP, 128 // GROUP], [0, GROUP]], channel_multiplier=1))
            const(g.affine_select(out=group_avg[:, :], in_=group_avg[:, :], compare_op=ALU.is_ge, fill=0.0,
                                  base=GROUP - 1, pattern=[[GROUP, 128 // GROUP], [0, GROUP]],
                                  channel_multiplier=-1))
            const(g.iota(prefer[:, :], pattern=[[-1, EXPERTS]], base=EXPERTS, channel_multiplier=0,
                         allow_small_or_imprecise_dtypes=True))
            const(g.memset(neg_half[:, :], -0.5))
            const(g.memset(ones_col[:, :], 1.0))
            const(g.memset(wscale_col[:, :], WSCALE))
            assert steps[0] == N_CONSTS

            def load_samples(b):
                x = ins["x"][b:b + 1, :] if isinstance(b, int) else ins["x"][bass.ds(b, 1), :]
                rows = x.rearrange("a (p n) -> (a p) n", n=PER_COL)
                pool.dma_start(xa[0:COLS, 0:PER_COL], rows).then_inc(S["x_loaded"], 16)
                pool.dma_start(xa[0:COLS - 1, PER_COL:PER_COL + STRIDE0], rows[1:COLS, 0:STRIDE0]
                               ).then_inc(S["x_loaded"], 16)

            def split_weights(phase, b=None, pr=None):
                wait(pool, "w_loaded", phase, 144 if phase == SETUP else 0, b, pr)
                if phase != SETUP:
                    wait(pool, "ps_full", phase, job_index(phase, "v", ()) + 1, b, pr)
                times = wscale_col[:, :].unsqueeze(2).to_broadcast([128, 3, 128])
                g.tensor_tensor(w0_parts[:, 0, :, :], wqkv0[:, :, :], times, ALU.mult)
                g.tensor_tensor(w1_high[:, :, :], wqkv1[:, :, :], times, ALU.mult)
                g.tensor_tensor(wqkv0[:, :, :], wqkv0[:, :, :], times, ALU.mult)
                g.tensor_tensor(wqkv1[:, :, :], wqkv1[:, :, :], times, ALU.mult).then_inc(S["w_step"], 1)
                wait(pool, "w_step", phase, 1, b, pr)
                g.tensor_tensor(w0_parts[:, 1, :, :], wqkv0[:, :, :], w0_parts[:, 0, :, :], ALU.subtract)
                g.tensor_tensor(w1_low[:, :, :], wqkv1[0:D1, :, :], w1_high[0:D1, :, :], ALU.subtract
                                ).then_inc(S["w_split"], 1)

            def group_rstd(phase, k, b=None):
                wait(pool, "var_ready", phase, k, b)
                g.tensor_tensor(tmp[:, 2:3], tmp[:, 1:2], neg_half[:, 0:1], ALU.pow).then_inc(S["rstd_ready"], 1)

            def split_next(b, pr):
                wait(pool, "head1_stacked", PAIR, 0, b, pr)
                once = ones_col[:, :].to_broadcast([128, TOK])
                for kind, full, parts in (("q", q_full, q_parts), ("k", k_full, k_parts)):
                    wait(pool, "act_freed", PAIR, freed(PAIR, ACT_ENGINE, job_index(PAIR, kind, ())), b, pr)
                    g.tensor_tensor(parts[:, 0, :], full, once, ALU.mult).then_inc(S[f"{kind}_high"], 1)
                    wait(pool, f"{kind}_high", PAIR, 1, b, pr)
                    last = g.tensor_tensor(parts[:, 1, :], full, parts[:, 0, :], ALU.subtract)
                last.then_inc(S["parts_ready"], 1)

            pool.wait_ge(S["x_split"], 1)
            load_samples(0)
            split_weights(SETUP)
            group_rstd(SETUP, 1)
            with pool.Fori(0, BATCH) as b:
                def low_parts(layer):
                    for unit in SPLITS:
                        if unit[0] == layer and low_engine(*unit) == "pool":
                            wait(pool, "hi_done", TOWER, SPLITS.index(unit) + 1, b)
                            src, high, low = split_views(*unit)
                            g.tensor_tensor(low, src, high, ALU.subtract).then_inc(S["lo_pool"], 1)

                wait(pool, "x_split", TOWER, 0, b)
                wait(pool, "ps_full", TOWER, 0, b)
                load_samples((b + 1) & (BATCH - 1))
                low_parts(0)
                for n in range(1, CONV_LAYERS):
                    group_rstd(TOWER, n, b)
                    low_parts(n)
                for phase, k in ((TOWER, CONV_LAYERS), (POST, 1)):
                    wait(pool, "var_ready", phase, k, b)
                    g.tensor_tensor(lnr[:, :], lnv[:, :], neg_half[:, 0:TT], ALU.pow
                                    ).then_inc(S["rstd_ready"], 1)
                    if phase == TOWER:
                        split_weights(TOWER, b)
                        with pool.Fori(0, PAIRS - 1) as pr:
                            split_next(b, pr)
                            split_weights(PAIR, b, pr)
                group_rstd(POST, 2, b)

            wait(pool, "ps_full", MOE, 0)
            wait(pool, "scratch_stored", MOE, 0)
            pool.wait_ge(slots_cleared, 16)
            steps[0] = 0

            def moe_const(ins_):
                steps[0] += 1
                ins_.then_inc(moe_consts, 1)
                pool.wait_ge(moe_consts, steps[0])

            moe_const(g.memset(ones, 1.0))
            moe_const(g.memset(before, 1.0))
            moe_const(g.affine_select(out=before, in_=before, compare_op=ALU.is_gt, fill=0.0, base=0,
                                      pattern=[[1, 128]], channel_multiplier=-1))
            moe_const(g.memset(segment, 1.0))
            moe_const(g.memset(segment.rearrange("p (e t) -> p e t", t=TILES)[:, :, 0:1], 0.0))
            moe_const(g.iota(edges, pattern=[[128, TILES]], base=0, channel_multiplier=0,
                             allow_small_or_imprecise_dtypes=True))
            moe_const(g.iota(tile_ids, pattern=[[1, 32]], base=0, channel_multiplier=0,
                             allow_small_or_imprecise_dtypes=True))
            for par in range(2):
                moe_const(g.memset(xe1[par][D1:D1 + 1, :], 1.0))
            moe_const(g.iota(rows_of_tokens[:, :, 2 * D:ROW].bitcast(i32), pattern=[[SEQ, BATCH], [128, TT]],
                             base=0, channel_multiplier=1))
            moe_const(g.memset(counts, 0.0))
            moe_const(g.memset(tiles_end, 0.0))
            assert steps[0] == N_MOE_CONSTS
            pool.wait_ge(slots_ready, 1)
            for t in range(TILES):
                if t % TT == 0:
                    pool.wait_ge(tokens_loaded[t // TT], 16 * 4)
                rows = SEQ - 128 * (TT - 1) if t % TT == TT - 1 else 128
                pool.indirect_dma_start(out=slot_dram,
                                        out_offset=bass.IndirectOffsetOnAxis(ap=slots[0:rows, t:t + 1], axis=0),
                                        in_=rows_of_tokens[0:rows, t, :], in_offset=None).then_inc(scattered, 16)

            def scatter_out(i, par):
                j = i * 2 + par
                pool.wait_ge(rest_loaded[par], i * 16 + 16)
                pool.wait_ge(y_taken, j + 1)
                g.tensor_tensor(carry[:, par:par + 1], ones_col[:, :], ones_col[:, :], ALU.mult
                                ).then_inc(scatter_begun[par], 1)
                pool.indirect_dma_start(out=out.rearrange("b s d -> (b s) d"),
                                        out_offset=bass.IndirectOffsetOnAxis(
                                            ap=rest[par][:, D:D + 1].bitcast(mybir.dt.uint32), axis=0),
                                        in_=out_tile[par], in_offset=None, bounds_check=BATCH * SEQ - 1,
                                        oob_is_err=False).then_inc(out_scattered[par], 16)

            with pool.Fori(0, SLOT_TILES // 2) as i:
                scatter_out(i, 0)
                scatter_out(i, 1)
            scatter_out(SLOT_TILES // 2, 0)

        @block.scalar
        def _(act):
            a = nc.scalar

            def jobs_of(phase):
                for n in ACT_ORDER[phase]:
                    kind, args, who = JOBS[phase][n]
                    yield slot_of(phase, n), n, kind, args

            for g, n, kind, args in jobs_of(SETUP):
                wait(act, "ps_full", SETUP, n + 1)
                if kind == "cw0t":
                    src = bank(g, 0).bitcast(fp16)[0:3 * WIN, 0:SUB * CH].rearrange("p (m c) -> p m c", m=SUB)
                    a.activation(cw0f[:, :], bank(g, 1)[0:TAPS0, 0:CH], ACT.Copy)
                    a.activation(cw0t[:, :, :], src, ACT.Copy).then_inc(S["act_freed"], 1)
                elif kind == "pwt":
                    a.activation(pwt[:, :], bank(g, 0)[:, 0:D], ACT.Copy).then_inc(S["act_freed"], 1)
                else:
                    a.activation(spare[:, n + 10:n + 11], bank(g, 0)[:, 0:1], ACT.Copy).then_inc(S["act_freed"], 1)

            def normalise(layer, b):
                wait(act, "affine_ready", TOWER, layer, b)
                r = 0
                for rows in NORM_CHUNKS[layer]:
                    src = ys[layer][:, r * PITCH:(r + rows) * PITCH]
                    dst = src
                    if layer == 5:
                        src = src.rearrange("p (r c) -> p r c", c=PITCH)[:, :, 0:COLS]
                        dst = h5t.rearrange("p (c r) -> p r c", r=rows)
                    a.activation(dst, src, ACT.Gelu_apprx_tanh, bias=affine[:, 1:2], scale=affine[:, 0:1]
                                 ).then_inc(S["norm_done"], 1)
                    r += rows

            def attention_job(phase, g, n, kind, args, b, pr=None):
                if kind == "s":
                    (k,) = args
                    i, k_ = TILE_ORDER[k % TT], k % STEPS
                    m = tile_rows(i)
                    if phase != TOWER:
                        wait(act, "ps_full", phase, transposed_before(phase, k - PROBS), b, pr)
                    wait(act, "smax_done", phase, k + 1 if phase == TOWER else k - 1, b, pr)
                    a.activation(prob[k % PROBS][0:m, 0:128 * i + m], slot(g)[0:m, 0:128 * i + m], ACT.Exp,
                                 bias=nmax[0:m, k_:k_ + 1], scale=SCALE, accum_out=rsum[0:m, k_:k_ + 1]
                                 ).then_inc(S["act_freed"], 1)
                    return
                wait(act, "ps_full", phase, n + 1, b, pr)
                if kind in ("q", "k"):
                    if phase == PAIR:
                        wait(act, "parts_ready", phase, 0, b, pr)
                    dst, w = (q_parts, 0) if kind == "q" else (k_parts, 1)
                    src = slot(g).rearrange("p (k n) -> p k n", k=2)[:, :, 0:TOK // 2]
                    bias = bqkv[:, w, 0:1] if phase == TOWER else bqkv[:, w, bass.ds(pr + 1, 1)]
                    full = q_full if kind == "q" else k_full
                    if phase == TOWER:
                        a.activation(dst[:, 0, :].rearrange("p (k n) -> p k n", k=2), src, ACT.Identity, bias=bias,
                                     scale=1.0 / WSCALE)
                    a.activation(full.rearrange("p (k n) -> p k n", k=2), src, ACT.Identity, bias=bias,
                                 scale=1.0 / WSCALE).then_inc(S["act_freed"], 1)
                elif kind == "v":
                    src = slot(g).rearrange("p (t c) -> p t c", c=128)
                    a.activation(vt[:, 0:TT, :], src[:, 0:TT, :], ACT.Copy, scale=1.0 / WSCALE
                                 ).then_inc(S["act_freed"], 1)
                elif kind == "pt":
                    (k,) = args
                    i = TILE_ORDER[k % TT]
                    m = tile_rows(i)
                    src = slot(g).rearrange("p (t c) -> p t c", c=128)
                    if i == 4:
                        a.activation(probt[k % 2][:, 4, 0:m], src[:, 4, 0:m], ACT.Copy
                                     ).then_inc(S["act_freed"], 1)
                    else:
                        a.activation(probt[k % 2][:, 4:6, 0:m], src[:, 4:6, 0:m], ACT.Copy
                                     ).then_inc(S["act_freed"], 1)
                else:
                    assert kind == "z"
                    (k,) = args
                    i, hh = TILE_ORDER[k % TT], k // TT
                    m = tile_rows(i)
                    wait(act, "rinv_ready", phase, k + 1, b, pr)
                    a.activation(z[0:m, i, DH * hh:DH * hh + DH], slot(g)[0:m, Z_AT:Z_AT + DH], ACT.Copy,
                                 scale=rinv[0:m, k:k + 1]).then_inc(S["act_freed"], 1)

            act.wait_ge(params_loaded, 16 * n_dmas[params_loaded])
            with act.Fori(0, BATCH) as b:
                layer = 0
                for g, n, kind, args in jobs_of(TOWER):
                    if kind == "conv":
                        if args[0] > 1 and args[1] == 0:
                            normalise(args[0] - 1, b)
                        layer, r, cut = args
                        wait(act, "ps_full", TOWER, n + 1, b)
                        rows = cut[0]
                        dst = ys[layer][:, r * PITCH:(r + sum(cut)) * PITCH]
                        src = slot(g).rearrange("p (k n) -> p k n", k=2)[:, 0:len(cut), 0:rows * PITCH]
                        a.activation(dst.rearrange("p (k n) -> p k n", k=len(cut)), src, ACT.Identity,
                                     scale=1.0 / WSCALE).then_inc(S["act_freed"], 1)
                    elif kind == "conv0":
                        j, i = args
                        if args == (0, 0):
                            wait(act, "affine_ready", TOWER, 0, b)
                            wait(act, "scratch_stored", TOWER, 0, b)
                        wait(act, "ps_full", TOWER, n + 1, b)
                        piece = 3 * j + i
                        if piece >= STAGES:
                            had_it = (0, piece - STAGES)
                            wait(act, "hi_done", TOWER, SPLITS.index(had_it) + 1, b)
                            if low_engine(*had_it) == DVE_ENGINE:
                                wait(act, "lo_dve", TOWER, lows(DVE_ENGINE, had_it), b)
                            else:
                                wait(act, "lo_pool", TOWER, lows("pool", had_it), b)
                        src = slot(g).rearrange("p (m n) -> p m n", m=2)[:, :, 0:4 * PITCH]
                        a.activation(stage[:, piece % STAGES, :].rearrange("p (m n) -> p m n", m=2), src,
                                     ACT.Gelu_apprx_tanh,
                                     bias=affine[:, 1:2], scale=affine[:, 0:1]).then_inc(S["act_freed"], 1)
                    elif kind in ("q", "k", "v", "s"):
                        attention_job(TOWER, g, n, kind, args, b)
                    else:
                        assert kind == "xtr"
                        if layer == 5:
                            normalise(5, b)
                            layer = None
                        wait(act, "ps_full", TOWER, n + 1, b)
                        a.activation(xt_parts[:, args[0], :], bank(g, 0).bitcast(fp16)[:, 0:TOK], ACT.Copy
                                     ).then_inc(S["act_freed"], 1)
                with act.Fori(0, PAIRS - 1) as pr:
                    for g, n, kind, args in jobs_of(PAIR):
                        attention_job(PAIR, g, n, kind, args, b, pr)
                for g, n, kind, args in jobs_of(LAST_PAIR):
                    attention_job(LAST_PAIR, g, n, kind, args, b)
                for g, n, kind, args in jobs_of(POST):
                    wait(act, "ps_full", POST, n + 1, b)
                    a.activation(xnt1[0:D1, 0:TOK], slot(g)[0:D1, 0:TOK], ACT.Copy).then_inc(S["act_freed"], 1)

            def take_hidden(j, par):
                act.wait_ge(hid_full, j + 1)
                src = slot(1 + par).rearrange("p (k n) -> p k n", k=2)[:, :, 0:FF // 2]
                a.activation(hid[par].rearrange("p (k n) -> p k n", k=2), src, ACT.Gelu).then_inc(hid_taken, 1)

            def take_hidt_end(j, par):
                act.wait_ge(hidt_full, j + 1)
                a.activation(hidt[par][:, 4:6, :], bank(1 + par, 1)[:, 0:256].rearrange("p (c t) -> p c t", c=2),
                             ACT.Copy).then_inc(hidt_taken_act, 1)

            with act.Fori(0, SLOT_TILES // 2) as i:
                take_hidden(i * 2, 0)
                take_hidden(i * 2 + 1, 1)
                take_hidt_end(i * 2, 0)
                take_hidt_end(i * 2 + 1, 1)
            take_hidden(SLOT_TILES - 1, 0)
            take_hidt_end(SLOT_TILES - 1, 0)

        @block.vector
        def _(dve):
            v = nc.vector
            state = {"phase": SETUP, "n": 0, "b": None, "pr": None}

            def enter(phase, b=None, pr=None):
                state.update(phase=phase, n=0, b=b, pr=pr)

            def step(ins_):
                state["n"] += 1
                ins_.then_inc(S["dve_step"], 1)
                dve.wait_ge(S["dve_step"], at("dve_step", state["phase"], state["n"], state["b"], state["pr"]))

            def carry_wait():
                v.memset(spare[:, 3:4], 0.0)

            def leave():
                index = PHASES.index(state["phase"])
                assert state["n"] == COUNTS["dve_step"][index], (index, state["n"])

            v.memset(xa[:, :], 0.0).then_inc(S["x_split"], 1)
            v.memset(cw0pad, 0.0).then_inc(pads_ready, 1)
            v.memset(xstack[:, :, :], 0.0).then_inc(pads_ready, 1)
            v.memset(empty_slot[:, 0:2 * D], 0.0)
            v.memset(empty_slot[:, 2 * D:ROW].bitcast(i32), NO_TOKEN).then_inc(pads_ready, 1)
            v.memset(onehot[:, :, :], 0.0).then_inc(pads_ready, 1)
            v.memset(logits[:, :, :], 0.0).then_inc(pads_ready, 1)
            v.memset(lnmv[:, :, :], 0.0).then_inc(pads_ready, 1)
            dve.wait_ge(pads_ready, 6)
            dve.wait_ge(weights_loaded, 16 * n_dmas[weights_loaded])
            step(v.tensor_scalar(cw0s[:, :], cw0n[:, :], WSCALE, None, ALU.mult))
            for m in range(SUB):
                o = STRIDE0 * m
                last = v.tensor_copy(cw0pad[:, m, o:o + TAPS0], cw0s[:, :])
            step(last)
            for m in range(SUB):
                o = STRIDE0 * m
                v.tensor_copy(cw0pad[:, m, WIN + o:WIN + o + TAPS0], cw0pad[:, m, o:o + TAPS0])
                last = v.tensor_tensor(cw0pad[:, m, 2 * WIN + o:2 * WIN + o + TAPS0], cw0s[:, :],
                                       cw0pad[:, m, o:o + TAPS0], ALU.subtract)
            last.then_inc(cw0_stacked, 1)
            for n, (kind, args, who) in enumerate(JOBS[SETUP]):
                if kind != "cwt":
                    continue
                wait(dve, "ps_full", SETUP, n + 1)
                (l,) = args
                taps = 2 if l == 5 else 3
                src = bank(n, 0)[:, 0:taps * CH].rearrange("p (k c) -> p k c", k=taps)
                step(v.tensor_scalar(cwt[l][:, 0, :, :], src, WSCALE, None, ALU.mult))
                v.scalar_tensor_tensor(out=cwt[l][:, 1, :, :], in0=src, scalar=WSCALE, in1=cwt[l][:, 0, :, :],
                                       op0=ALU.mult, op1=ALU.subtract).then_inc(S["dve_freed"], 1)

            def group_stats(layer, pieces, b):
                step(last_bn[0])
                carry_wait()
                step(v.bn_aggr(mv[:, :], bn[:, 0:pieces, :].rearrange("p n s -> p (n s)")))
                step(v.tensor_tensor(ms[:, 0:1], mv[:, 0:1], channel_par[:, 0, layer:layer + 1], ALU.add))
                v.scalar_tensor_tensor(out=ms[:, 1:2], in0=ms[:, 0:1], scalar=ms[:, 0:1], in1=mv[:, 1:2],
                                       op0=ALU.mult, op1=ALU.add).then_inc(S["channel_stats"], 1)

            def group_affine(phase, layer, g, n, b=None):
                wait(dve, "ps_full", phase, n + 1, b)
                ins_ = v.tensor_copy(gm[:, :], bank(g, 0)[:, 0:2])
                ins_.then_inc(S["dve_freed"], 1)
                dve.wait_ge(S["dve_freed"], at("dve_freed", phase, freed(phase, DVE_ENGINE, n), b))
                step(v.scalar_tensor_tensor(out=tmp[:, 0:1], in0=gm[:, 0:1], scalar=gm[:, 0:1], in1=gm[:, 1:2],
                                            op0=ALU.mult, op1=ALU.subtract))
                v.tensor_scalar(tmp[:, 1:2], tmp[:, 0:1], -1.0, EPS, ALU.mult, ALU.add
                                ).then_inc(S["var_ready"], 1)
                step(v.tensor_tensor(tmp[:, 3:4], channel_par[:, 0, layer:layer + 1], gm[:, 0:1], ALU.subtract))
                wait(dve, "rstd_ready", phase, {SETUP: 1, TOWER: layer, POST: 2}[phase], b)
                scale = affine[:, 0:1] if layer else tmp[:, 0:1]
                step(v.tensor_tensor(scale, tmp[:, 2:3], channel_par[:, 1, layer:layer + 1], ALU.mult))
                if layer == 0:
                    v.tensor_scalar(affine[:, 0:1], scale, 1.0 / WSCALE, None, ALU.mult)
                v.scalar_tensor_tensor(out=affine[:, 1:2], in0=tmp[:, 3:4], scalar=scale,
                                       in1=channel_par[:, 2, layer:layer + 1], op0=ALU.mult, op1=ALU.add
                                       ).then_inc(S["affine_ready"], 1)

            def token_stats(tiles):
                for i in tiles:
                    m = tile_rows(i)
                    last = v.bn_stats(bn[0:m, i, :], h[0:m, i, :])
                return last

            def layernorm(meanwhile=None):
                step(token_stats(range(4, TT)))
                carry_wait()
                for i in range(TT):
                    m = tile_rows(i)
                    last = v.bn_aggr(lnmv[0:m, i, :], bn[0:m, i, :])
                step(last)
                v.tensor_scalar(lnv[:, :], lnmv[:, :, 1], EPS, None, ALU.add).then_inc(S["var_ready"], 1)
                if meanwhile is not None:
                    meanwhile()
                wait(dve, "rstd_ready", state["phase"], CONV_LAYERS if state["phase"] == TOWER else 1, state["b"])
                for i in range(TT):
                    m = tile_rows(i)
                    last = v.tensor_scalar(xn[0:m, i, :], h[0:m, i, :], lnmv[0:m, i, 0:1], lnr[0:m, i:i + 1],
                                           ALU.subtract, ALU.mult)
                if state["phase"] == TOWER:
                    step(last)
                    v.tensor_copy(xn_parts[:, :, 0, :], xn[:, :, 0:128])
                    v.tensor_copy(xn_parts[:, :, 2, 0:D1], xn[:, :, 128:D]).then_inc(S["xn_high"], 1)
                    wait(dve, "xn_high", TOWER, 1, state["b"])
                    v.tensor_tensor(xn_parts[:, :, 1, :], xn[:, :, 0:128], xn_parts[:, :, 0, :], ALU.subtract)
                    last = v.tensor_tensor(xn_parts[:, :, 2, D1:128], xn[:, :, 128:D], xn_parts[:, :, 2, 0:D1],
                                           ALU.subtract)
                last.then_inc(S["xn_ready"], 1)

            def take_token_rows(g, part, in1, last_inc=True):
                if part == 0:
                    for k in range(2):
                        last = v.tensor_tensor(h[:, 2 * k:2 * k + 2, :],
                                               bank(g, k)[:, 0:2 * D].rearrange("p (t d) -> p t d", t=2),
                                               in1(2 * k, 2, 128), ALU.add)
                else:
                    v.tensor_tensor(h[:, 4, :], bank(g, 0)[:, 0:D], in1(4, 1, 128), ALU.add)
                    last = v.tensor_tensor(h[0:LASTM, 5, :], bank(g, 0)[0:LASTM, D:2 * D], in1(5, 1, LASTM),
                                           ALU.add)
                last.then_inc(S["dve_freed"], 1)

            def halo(layer, b):
                r = ROWS[layer] * PITCH
                high, low = hs[layer]
                v.tensor_copy(high[:, r:r + PITCH], high[:, 1:1 + PITCH])
                v.tensor_copy(low[:, r:r + PITCH], low[:, 1:1 + PITCH]).then_inc(S["halo_done"], 1)

            def split(unit, b):
                src, high, low = split_views(*unit)
                n = SPLITS.index(unit) + 1
                v.tensor_copy(high, src).then_inc(S["hi_done"], 1)
                if low_engine(*unit) == DVE_ENGINE:
                    dve.wait_ge(S["hi_done"], at("hi_done", TOWER, n, b))
                    v.tensor_tensor(low, src, high, ALU.subtract).then_inc(S["lo_dve"], 1)

            def wait_split(unit, b):
                wait(dve, "hi_done", TOWER, SPLITS.index(unit) + 1, b)
                for engine, name in ((DVE_ENGINE, "lo_dve"), ("pool", "lo_pool")):
                    if lows(engine, unit):
                        wait(dve, name, TOWER, lows(engine, unit), b)

            def attention_job(phase, n, kind, args, b, pr=None):
                g = slot_of(phase, n)
                wait(dve, "ps_full", phase, n + 1, b, pr)
                if kind in ("q", "k"):
                    wait(dve, "act_freed", phase, freed(phase, ACT_ENGINE, n), b, pr)
                    full, dst = (q_full, q_parts) if kind == "q" else (k_full, k_parts)
                    last = v.tensor_tensor(dst[:, 1, :], full, dst[:, 0, :], ALU.subtract)
                    if kind == "k":
                        last.then_inc(S["parts_ready"], 1)
                elif kind == "s":
                    (k,) = args
                    i, k_ = TILE_ORDER[k % TT], k % STEPS
                    m = tile_rows(i)
                    step(v.reduce_max(smax[0:m, k_:k_ + 1], slot(g)[0:m, 0:128 * i + m], AX.X))
                    v.tensor_scalar(nmax[0:m, k_:k_ + 1], smax[0:m, k_:k_ + 1], -SCALE, None, ALU.mult
                                    ).then_inc(S["smax_done"], 1)
                elif kind == "pt":
                    (k,) = args
                    i = TILE_ORDER[k % TT]
                    m = tile_rows(i)
                    src = slot(g).rearrange("p (t c) -> p t c", c=128)
                    w = min(i + 1, 4)
                    v.tensor_copy(probt[k % 2][:, 0:w, 0:m], src[:, 0:w, 0:m]).then_inc(S["dve_freed"], 1)
                    wait(dve, "act_freed", phase, exp_done(phase, k), b, pr)
                    v.reciprocal(rinv[0:m, k:k + 1], rsum[0:m, k:k + 1]).then_inc(S["rinv_ready"], 1)
                else:
                    assert kind == "zt"
                    a = PAIRS - 1 if pr is None else pr
                    dst = zt[:, a, 0:TOK] if pr is None else zt[:, bass.ds(a, 1), 0:TOK].rearrange("p a t -> p (a t)")
                    bias = bqkv[:, 2, a:a + 1] if pr is None else bqkv[:, 2, bass.ds(a, 1)]
                    v.tensor_scalar(dst, slot(g)[:, 0:TOK], bias, None, ALU.add).then_inc(S["dve_freed"], 1)

            last_bn = [None]
            def split_samples(phase, b=None):
                wait(dve, "x_loaded", phase, 32 if phase == SETUP else 0, b)
                main = xa[:, 0:PER_COL].rearrange("p (n k) -> p n k", k=BLK_STEP)
                tail = xa[:, BLK_STEP:BLK_STEP + PER_COL].rearrange("p (n k) -> p n k", k=BLK_STEP)[:, :, 0:WIN - BLK_STEP]
                v.tensor_copy(xstack[:, :, 0:BLK_STEP], main)
                step(v.tensor_copy(xstack[:, :, BLK_STEP:WIN], tail))
                v.tensor_tensor(xstack[:, :, WIN:WIN + BLK_STEP], main, xstack[:, :, 0:BLK_STEP], ALU.subtract)
                v.tensor_tensor(xstack[:, :, WIN + BLK_STEP:2 * WIN], tail, xstack[:, :, BLK_STEP:WIN], ALU.subtract)
                v.tensor_copy(xstack[:, :, 2 * WIN:3 * WIN], xstack[:, :, 0:WIN]).then_inc(S["x_split"], 1)

            def samples_job(phase, n, b=None):
                kind, args, _ = JOBS[phase][n]
                g = slot_of(phase, n)
                if kind == "xt":
                    (i,) = args
                    wait(dve, "ps_full", phase, n + 1, b)
                    half = NBLK // 2
                    src = slot(g).bitcast(fp16)[0:3 * WIN, :].rearrange("p (k n) -> p k n", k=2)[:, :, 0:8 * PITCH]
                    dst = xt[:, half * i:half * i + half, :].rearrange("p (k n) c -> p k (n c)", k=2)
                    v.tensor_copy(dst, src).then_inc(S["dve_freed"], 1)
                elif kind in ("gram", "taps"):
                    wait(dve, "ps_full", phase, n + 1, b)
                    dst, m = (gram, WIN) if kind == "gram" else (tap_sums, TAPS0)
                    v.tensor_copy(dst[:, 0:m], bank(g, 0)[0:m, 0:m])
                    v.tensor_copy(dst[:, m:m + 1], bank(g, 1)[0:m, 0:1]).then_inc(S["dve_freed"], 1)
                elif kind == "chan":
                    wait(dve, "ps_full", phase, n + 1, b)
                    count = float(COLS * ROWS[0] - 1)
                    bias = channel_par[:, 0, 0:1]
                    v.tensor_scalar(ms[:, 0:1], bank(g, 0)[:, TAPS0:TAPS0 + 1], 1.0 / count, bias, ALU.mult,
                                    ALU.add)
                    v.tensor_tensor(quad[:, :], bank(g, 0)[:, 0:TAPS0], cw0n[:, :], ALU.mult
                                    ).then_inc(S["dve_freed"], 1)
                    dve.wait_ge(S["dve_freed"], at("dve_freed", phase, freed(phase, DVE_ENGINE, n), b))
                    step(v.reduce_sum(mv[:, 0:1], quad[:, :], AX.X))
                    step(v.scalar_tensor_tensor(out=tmp[:, 0:1], in0=ms[:, 0:1], scalar=2.0, in1=bias,
                                                op0=ALU.mult, op1=ALU.subtract))
                    step(v.tensor_tensor(tmp[:, 1:2], tmp[:, 0:1], bias, ALU.mult))
                    v.scalar_tensor_tensor(out=ms[:, 1:2], in0=mv[:, 0:1], scalar=1.0 / count,
                                           in1=tmp[:, 1:2], op0=ALU.mult, op1=ALU.add
                                           ).then_inc(S["channel_stats"], 1)
                else:
                    assert (kind, args) == ("group", (0,))
                    group_affine(phase, 0, g, n, b)

            split_samples(SETUP)
            dve.wait_ge(params_loaded, 16 * n_dmas[params_loaded])
            for n, (kind, args, who) in enumerate(JOBS[SETUP]):
                if kind in ("xt", "gram", "taps", "chan", "group"):
                    samples_job(SETUP, n)
            leave()

            with dve.Fori(0, BATCH) as b:
                enter(TOWER, b)
                pieces = 0
                for n, (kind, args, who) in enumerate(JOBS[TOWER]):
                    g = n
                    if kind == "conv0":
                        wait(dve, "act_freed", TOWER, freed(TOWER, ACT_ENGINE, n), b)
                        split((0, 3 * args[0] + args[1]), b)
                    elif kind == "group":
                        (layer,) = args
                        group_stats(layer, pieces, b)
                        pieces = 0
                        group_affine(TOWER, layer, g, n, b)
                        if 1 <= layer <= 4:
                            r = 0
                            for c, rows in enumerate(NORM_CHUNKS[layer]):
                                wait(dve, "norm_done", TOWER, norm_chunk_of(layer, r), b)
                                split((layer, c), b)
                                r += rows
                            if layer < 4:
                                wait_split((layer, 0), b)
                                halo(layer, b)
                    elif kind == "conv":
                        layer, r, cut = args
                        if layer == 1 and r == 0:
                            wait_split((0, 0), b)
                            halo(0, b)
                        wait(dve, "act_freed", TOWER, freed(TOWER, ACT_ENGINE, n), b)
                        rows = ys[layer].rearrange("p (r c) -> p r c", c=PITCH)
                        for c in cut:
                            if r + c == ROWS[layer]:
                                v.bn_stats(bn[:, pieces, :], rows[:, r:r + c - 1, 0:COLS])
                                last_bn[0] = v.bn_stats(bn[:, pieces + 1, :], rows[:, r + c - 1, 0:COLS - 1])
                                pieces += 2
                            else:
                                last_bn[0] = v.bn_stats(bn[:, pieces, :], rows[:, r:r + c, 0:COLS])
                                pieces += 1
                            r += c
                    elif kind == "embed":
                        wait(dve, "ps_full", TOWER, n + 1, b)
                        take_token_rows(g, args[0], lambda i, k, m: pb_b[0:m, :] if k == 1 else
                                        pb_b[:, :].unsqueeze(1).to_broadcast([128, 2, D]))
                        dve.wait_ge(S["dve_freed"], at("dve_freed", TOWER, freed(TOWER, DVE_ENGINE, n), b))
                        if args[0] == 0:
                            token_stats(range(4))
                        else:
                            layernorm()
                    elif kind == "xtr" and DVE_ENGINE in who:
                        wait(dve, "ps_full", TOWER, n + 1, b)
                        v.tensor_copy(xt_parts[:, args[0], :], bank(g, 0).bitcast(fp16)[:, 0:TOK]
                                      ).then_inc(S["dve_freed"], 1)
                    elif kind in ("q", "k", "s"):
                        attention_job(TOWER, n, kind, args, b)
                leave()

                with dve.Fori(0, PAIRS - 1) as pr:
                    enter(PAIR, b, pr)
                    for n, (kind, args, who) in enumerate(JOBS[PAIR]):
                        if DVE_ENGINE in who or kind == "s":
                            attention_job(PAIR, n, kind, args, b, pr)
                    leave()
                enter(LAST_PAIR, b)
                for n, (kind, args, who) in enumerate(JOBS[LAST_PAIR]):
                    if DVE_ENGINE in who or kind == "s":
                        attention_job(LAST_PAIR, n, kind, args, b)
                leave()

                enter(POST, b)
                split_samples(POST, b)
                for i in range(TT):
                    m = tile_rows(i)
                    last = v.tensor_tensor(h[0:m, i, :], h[0:m, i, :], bo_b[0:m, :], ALU.add)
                step(last)
                for n, (kind, args, who) in enumerate(JOBS[POST]):
                    g = slot_of(POST, n)
                    if DVE_ENGINE not in who or (kind, args) == ("xt", (0,)):
                        continue
                    if kind in ("xt", "gram", "taps", "chan", "group"):
                        samples_job(POST, n, b)
                        continue
                    wait(dve, "ps_full", POST, n + 1, b)
                    if kind == "wo":
                        take_token_rows(g, args[0], lambda i, k, m: h[0:m, i, :] if k == 1 else h[:, i:i + 2, :])
                        dve.wait_ge(S["dve_freed"], at("dve_freed", POST, freed(POST, DVE_ENGINE, n), b))
                        if args[0] == 0:
                            token_stats(range(4))
                        else:
                            layernorm(meanwhile=lambda: samples_job(POST, job_index(POST, "xt", (0,)), b))
                            wait(dve, "xn_ready", POST, 1, b)
                            v.memset(spare[:, 2:3], 0.0).then_inc(S["h1_ready"], 1)
                    elif kind == "tr":
                        v.tensor_copy(xnt0[:, 0:TOK], slot(g)[:, 0:TOK]).then_inc(S["dve_freed"], 1)
                    elif kind == "gate":
                        src = bank(g, 0)[:, 0:TT * EXPERTS].rearrange("p (t e) -> p t e", e=EXPERTS)
                        v.tensor_tensor(logits[:, 0:TT - 1, :], src[:, 0:TT - 1, :],
                                        gate_b[:, :].unsqueeze(1).to_broadcast([128, TT - 1, EXPERTS]), ALU.add)
                        v.tensor_tensor(logits[0:LASTM, TT - 1, :], src[0:LASTM, TT - 1, :], gate_b[0:LASTM, :],
                                        ALU.add).then_inc(S["dve_freed"], 1)
                        dve.wait_ge(S["dve_freed"], at("dve_freed", POST, freed(POST, DVE_ENGINE, n), b))
                        step(v.reduce_max(best[:, :], logits[:, :, :], AX.X))
                        step(v.tensor_tensor(pick[:, :, :], logits[:, :, :],
                                             best[:, :].unsqueeze(2).to_broadcast([128, TT, EXPERTS]), ALU.is_ge))
                        step(v.tensor_tensor(pick[:, :, :], pick[:, :, :],
                                             prefer[:, :].unsqueeze(1).to_broadcast([128, TT, EXPERTS]), ALU.mult))
                        step(v.reduce_max(best[:, :], pick[:, :, :], AX.X))
                        step(v.tensor_tensor(pick[:, :, :], pick[:, :, :],
                                             best[:, :].unsqueeze(2).to_broadcast([128, TT, EXPERTS]), ALU.is_ge))
                        v.tensor_copy(onehot[:, bass.ds(b * TT, TT - 1), :], pick[:, 0:TT - 1, :])
                        step(v.tensor_copy(onehot[0:LASTM - 1, bass.ds(b * TT + TT - 1, 1), :],
                                           pick[0:LASTM - 1, TT - 1:TT, :]))
                    else:
                        v.tensor_copy(spare[:, 4 + n:5 + n], bank(g, 0)[:, 0:1]).then_inc(S["dve_freed"], 1)
                leave()

            total = [0]

            def chain(ins_):
                total[0] += 1
                ins_.then_inc(S["dve_step"], 1)
                dve.wait_ge(S["dve_step"], at("dve_step", MOE, total[0]))

            dve.wait_ge(rank_full, 1)
            dve.wait_ge(moe_consts, N_MOE_CONSTS)
            v.tensor_copy(rank, bank(0, 0)[:, 0:TILES * EXPERTS].rearrange("p (t e) -> p t e", e=EXPERTS))
            chain(v.tensor_copy(per_tile.rearrange("p (e t) -> p e t", t=TILES),
                                bank(0, 1)[:, 0:TILES * EXPERTS].rearrange("p (t e) -> p e t", e=EXPERTS)))
            chain(v.tensor_tensor_scan(running, segment, per_tile, 0.0, ALU.mult, ALU.add))
            run_et = running.rearrange("p (e t) -> p e t", t=TILES)
            chain(v.tensor_copy(counts, run_et[:, :, TILES - 1]))
            chain(v.tensor_tensor(over[:, 0:TILES, :].rearrange("p t e -> p e t"),
                                  counts.unsqueeze(2).to_broadcast([128, EXPERTS, TILES]),
                                  edges.unsqueeze(1).to_broadcast([128, EXPERTS, TILES]), ALU.is_gt))
            chain(v.reduce_sum(ntiles, over[:, 0:TILES, :].rearrange("p t e -> p e t"), AX.X))
            chain(v.tensor_tensor_scan(tiles_end, ones[:, 0:EXPERTS], ntiles, 0.0, ALU.mult, ALU.add))
            chain(v.tensor_tensor(base, tiles_end, ntiles, ALU.subtract))
            chain(v.tensor_scalar(base, base, 128.0, None, ALU.mult))
            chain(v.tensor_tensor(running, running, per_tile, ALU.subtract))
            chain(v.tensor_tensor(rank, rank, run_et.rearrange("p e t -> p t e"), ALU.add))
            chain(v.tensor_tensor(rank, rank, base.unsqueeze(1).to_broadcast([128, TILES, EXPERTS]), ALU.add))
            chain(v.tensor_tensor(rank, rank, onehot[:, :, :], ALU.mult))
            chain(v.reduce_sum(slots_f, rank, AX.X))
            v.tensor_copy(slots, slots_f).then_inc(slots_ready, 1)
            chain(v.tensor_tensor(over, tiles_end.unsqueeze(1).to_broadcast([128, 32, EXPERTS]),
                                  tile_ids.unsqueeze(2).to_broadcast([128, 32, EXPERTS]), ALU.is_le))
            chain(v.reduce_sum(tile_expert_f, over, AX.X))
            chain(v.tensor_scalar(tile_expert_f, tile_expert_f, float(EXPERTS - 1), None, ALU.min))
            v.tensor_copy(tile_expert, tile_expert_f).then_inc(slots_ready, 1)

            def take_xt(j, par):
                dve.wait_ge(xt_full, j + 1)
                v.tensor_copy(xe0[par], bank(0, par)[:, 0:128])
                v.tensor_copy(xe1[par][0:D1, :], bank(0, par)[0:D1, 128:256]).then_inc(xt_taken, 1)

            def take_hidt(j, par):
                dve.wait_ge(hidt_full, j + 1)
                v.tensor_copy(hidt[par][:, 0:4, :], bank(1 + par, 0).rearrange("p (c t) -> p c t", c=4)
                              ).then_inc(hidt_taken_dve, 1)

            def take_y(i, par, first=False):
                j = i * 2 + par
                dve.wait_ge(y_full, j + 1)
                dve.wait_ge(rest_loaded[par], i * 16 + 16)
                if not first:
                    dve.wait_ge(out_scattered[par], i * 16)
                v.tensor_tensor(out_tile[par], bank(3, par)[:, 0:D], rest[par][:, 0:D], ALU.add
                                ).then_inc(y_taken, 1)

            def two_tiles(i, first=False, last=False):
                j = i * 2
                take_hidt(j, 0)
                take_xt(j + 2, 0)
                if not last:
                    take_xt(j + 3, 1)
                take_hidt(j + 1, 1)
                take_y(i, 0, first)
                take_y(i, 1, first)

            take_xt(0, 0)
            take_xt(1, 1)
            two_tiles(0, first=True)
            with dve.Fori(1, SLOT_TILES // 2 - 1) as i:
                two_tiles(i)
            two_tiles(SLOT_TILES // 2 - 1, last=True)
            take_hidt(SLOT_TILES - 1, 0)
            take_y(SLOT_TILES // 2, 0)

        @block.tensor
        def _(pe):
            t = nc.tensor

            def slot_free(phase, n, b=None, pr=None):
                if phase in (PAIR, LAST_PAIR):
                    r = RING[phase][n] - 4
                    of = phase if r >= 0 else PAIR
                    r %= ring_length(of)
                    jobs = [m for m, position in enumerate(RING[of]) if position == r]
                    for engine, name in ((ACT_ENGINE, "act_freed"), (DVE_ENGINE, "dve_freed")):
                        read = [m for m in jobs if engine in JOBS[of][m][2]]
                        if read:
                            count = freed(of, engine, read[-1])
                            wait(pe, name, phase, count if RING[phase][n] >= 4 else count - readers(PAIR, engine), b, pr)
                    return
                if phase == SETUP and n < 4:
                    return
                if phase != SETUP and n == 0:
                    wait(pe, "act_freed", phase, 0, b, pr)
                    wait(pe, "dve_freed", phase, 0, b, pr)
                if n >= 4:
                    for engine, name in ((ACT_ENGINE, "act_freed"), (DVE_ENGINE, "dve_freed")):
                        if engine in JOBS[phase][n - 4][2]:
                            wait(pe, name, phase, freed(phase, engine, n - 4), b, pr)

            def carry_wait(g):
                t.transpose(bank(g, 0)[:, 384:512], ident[:, :], ident[:, :])

            def samples_job(phase, n, b=None):
                kind, args, _ = JOBS[phase][n]
                g = slot_of(phase, n)

                def before(n):
                    kinds = ["xt", "gram", "taps", "chan", "group"]
                    return job_index(phase, kinds[kinds.index(kind) - 1], ())

                if kind == "xt":
                    if args[0] == 0:
                        wait(pe, "x_split", phase, 2 if phase == SETUP else 1, b)
                    half = NBLK // 2
                    for i in range(half):
                        dst = bank(g, i // 8).bitcast(fp16)[0:3 * WIN, (i % 8) * PITCH:(i % 8 + 1) * PITCH]
                        last = t.transpose(dst, xstack[:, half * args[0] + i, :], ident_h[0:PITCH, 0:PITCH])
                elif kind == "gram":
                    for k in range(NBLK - 1):
                        x = xa[0:COLS, BLK_STEP * k:BLK_STEP * k + WIN]
                        flags = dict(start=k == 0, stop=k == NBLK - 2)
                        t.matmul(bank(g, 0)[0:WIN, 0:WIN], x, x, **flags)
                        last = t.matmul(bank(g, 1)[0:WIN, 0:1], x, ones_col[0:COLS, :], **flags)
                elif kind == "taps":
                    wait(pe, "dve_freed", phase, freed(phase, DVE_ENGINE, before(n)), b)
                    carry_wait(g)
                    for m in range(SUB):
                        o = STRIDE0 * m
                        flags = dict(start=m == 0, stop=False)
                        pick_ = ident[0:WIN, o:o + TAPS0]
                        t.matmul(bank(g, 0)[0:TAPS0, 0:TAPS0], pick_, gram[:, o:o + TAPS0], **flags)
                        t.matmul(bank(g, 1)[0:TAPS0, 0:1], pick_, gram[:, WIN:WIN + 1], **flags)
                    for m in range(SUB):
                        o = BLK_STEP * (NBLK - 1) + STRIDE0 * m
                        cols = COLS - 1 if m == SUB - 1 else COLS
                        flags = dict(start=False, stop=m == SUB - 1)
                        x = xa[0:cols, o:o + TAPS0]
                        t.matmul(bank(g, 0)[0:TAPS0, 0:TAPS0], x, x, **flags)
                        last = t.matmul(bank(g, 1)[0:TAPS0, 0:1], x, ones_col[0:cols, :], **flags)
                elif kind == "chan":
                    wait(pe, "dve_freed", phase, freed(phase, DVE_ENGINE, before(n)), b)
                    last = t.matmul(bank(g, 0)[:, 0:TAPS0 + 1], cw0f[:, :], tap_sums[:, :], start=True, stop=True)
                else:
                    assert kind == "group"
                    wait(pe, "channel_stats", phase, 1, b)
                    last = t.matmul(bank(g, 0)[:, 0:2], group_avg[:, :], ms[:, :], start=True, stop=True)
                last.then_inc(S["ps_full"], 1)

            pe.wait_ge(consts_ready, N_CONSTS)
            pe.wait_ge(weights_loaded, 16 * n_dmas[weights_loaded])
            for n, (kind, args, who) in enumerate(JOBS[SETUP]):
                slot_free(SETUP, n)
                if kind in ("xt", "gram", "taps", "chan", "group"):
                    if kind == "chan":
                        wait(pe, "act_freed", SETUP, freed(SETUP, ACT_ENGINE, job_index(SETUP, "cw0t", ())))
                    samples_job(SETUP, n)
                    continue
                if kind == "cwt":
                    (l,) = args
                    taps = 2 if l == 5 else 3
                    w = cwn[l].rearrange("p (i k) -> p k i", k=taps)
                    for k in range(taps):
                        last = t.transpose(bank(n, 0)[:, k * CH:(k + 1) * CH], w[:, k, :], ident[:, :])
                elif kind == "cw0t":
                    pe.wait_ge(cw0_stacked, 1)
                    dst = bank(n, 0).bitcast(fp16)
                    t.transpose(bank(n, 1)[0:TAPS0, 0:CH], cw0n[:, :], ident[:, :])
                    for m in range(SUB):
                        last = t.transpose(dst[0:3 * WIN, m * CH:(m + 1) * CH], cw0pad[:, m, :], ident_h[:, :])
                elif kind == "pwt":
                    t.transpose(bank(n, 0)[:, 0:128], pwn[:, 0, :], ident[:, :])
                    last = t.transpose(bank(n, 0)[:, 128:D], pwn[0:D1, 1, :], ident[0:D1, 0:D1])
                else:
                    last = t.transpose(bank(n, 0)[:, 0:128], ident[:, :], ident[:, :])
                last.then_inc(S["ps_full"], 1)

            def token_transposes(g, part):
                for i in range(TT):
                    m = tile_rows(i)
                    if part == 0:
                        last = t.transpose(slot(g)[:, 128 * i:128 * i + m], xn[0:m, i, 0:128], ident[0:m, 0:m])
                    else:
                        last = t.transpose(slot(g)[0:D1, 128 * i:128 * i + m], xn[0:m, i, 128:D], ident[0:m, 0:m])
                return last

            def projection_terms(w, cols):
                x_high, x_low, x_rest = (xt_parts[:, a, cols] for a in range(3))
                return [(w0_parts[:, 0, w, :], x_high), (w0_parts[:, 0, w, :], x_low),
                        (w0_parts[:, 1, w, :], x_high), (w1_high[:, w, :], x_rest),
                        (w1_low[:, w, :], xt_parts[0:D1, 2, cols])]

            def attention_job(phase, n, kind, args, b, pr=None):
                g = slot_of(phase, n)
                if kind != "z":
                    slot_free(phase, n, b, pr)
                if kind in ("q", "k"):
                    if kind == "q":
                        wait(pe, "w_split", phase, 0, b, pr)
                    if kind == "q" and phase == TOWER:
                        wait(pe, "dve_freed", TOWER, freed(TOWER, DVE_ENGINE, n - 1), b)
                        wait(pe, "act_freed", TOWER, freed(TOWER, ACT_ENGINE, n - 1), b)
                    w = 0 if kind == "q" else 1
                    for k in range(2):
                        cols = slice(k * TOK // 2, (k + 1) * TOK // 2)
                        terms = projection_terms(w, cols)
                        for m, (weights, x) in enumerate(terms):
                            last = t.matmul(bank(g, k)[:, 0:TOK // 2], weights, x, start=m == 0,
                                            stop=m == len(terms) - 1)
                elif kind == "v":
                    for i in range(TT):
                        m = tile_rows(i)
                        terms = projection_terms(2, slice(128 * i, 128 * i + m))
                        for k, (weights, x) in enumerate(terms):
                            last = t.matmul(slot(g)[0:m, 128 * i:128 * i + 128], x, weights, start=k == 0,
                                            stop=k == len(terms) - 1)
                elif kind == "s":
                    (k,) = args
                    i, hh = TILE_ORDER[k % TT], k % STEPS // TT
                    m = tile_rows(i)
                    if phase == TOWER:
                        if k == 0:
                            wait(pe, "parts_ready", TOWER, 1, b)
                        q_cols = slice(128 * i, 128 * i + m)
                        terms = [(q_parts[0:DH, a, q_cols], k_parts[0:DH, c, :]) for a, c in ((0, 0), (0, 1), (1, 0))]
                    else:
                        if k in (2, STEPS):
                            wait(pe, "head0_stacked", phase, 64 if k == STEPS else 0, b, pr)
                        if k == TT:
                            wait(pe, "head1_stacked", phase, 0, b, pr)
                        q = q_stack[:, hh, 128 * i:128 * i + m]
                        terms = [(q, k_stack[:, hh, a, :]) for a in range(2)]
                    end = 128 * i + m
                    for lo in range(0, end, 512):
                        hi = min(lo + 512, end)
                        diagonal = lo <= 128 * i < hi
                        for a, (q, keys) in enumerate(terms):
                            last = t.matmul(slot(g)[0:m, lo:hi], q, keys[:, lo:hi], start=a == 0,
                                            stop=a == len(terms) - 1 and not diagonal)
                        if diagonal:
                            last = t.matmul(slot(g)[0:m, 128 * i:end], ident_b[0:m, 0:m], causal_b[0:m, 0:m],
                                            start=False, stop=True)
                elif kind == "pt":
                    (k,) = args
                    i = TILE_ORDER[k % TT]
                    m = tile_rows(i)
                    wait(pe, "act_freed", phase, exp_done(phase, k), b, pr)
                    for c in range(i + 1):
                        kk = tile_rows(c)
                        last = t.transpose(slot(g)[0:kk, 128 * c:128 * c + m],
                                           prob[k % PROBS][0:m, 128 * c:128 * c + kk], ident[0:m, 0:m])
                elif kind == "z":
                    (k,) = args
                    i, hh = TILE_ORDER[k % TT], k // TT
                    m = tile_rows(i)
                    if k == 0:
                        wait(pe, "act_freed", phase, 0, b, pr)
                    done = job_index(phase, "pt", (k,))
                    wait(pe, "dve_freed", phase, freed(phase, DVE_ENGINE, done), b, pr)
                    if i >= 4:
                        wait(pe, "act_freed", phase, freed(phase, ACT_ENGINE, done), b, pr)
                    for c in range(i + 1):
                        kk = tile_rows(c)
                        last = t.matmul(slot(g)[0:m, Z_AT:Z_AT + DH], probt[k % 2][0:kk, c, 0:m],
                                        vt[0:kk, c, DH * hh:DH * hh + DH], start=c == 0, stop=c == i)
                else:
                    assert kind == "zt"
                    done = job_index(phase, "z", (STEPS - 1,))
                    wait(pe, "act_freed", phase, freed(phase, ACT_ENGINE, done), b, pr)
                    for i in range(TT):
                        m = tile_rows(i)
                        last = t.transpose(slot(g)[:, 128 * i:128 * i + m], z[0:m, i, :], ident[0:m, 0:m])
                last.then_inc(S["ps_full"], 1)

            pe.wait_ge(params_loaded, 16 * n_dmas[params_loaded])
            with pe.Fori(0, BATCH) as b:
                for n, (kind, args, who) in enumerate(JOBS[TOWER]):
                    g = n
                    if kind in ("q", "k", "v", "s"):
                        attention_job(TOWER, n, kind, args, b)
                        continue
                    slot_free(TOWER, n, b)
                    if kind == "conv0":
                        j, i = args
                        for k in range(2):
                            last = t.matmul(bank(g, k)[:, 0:4 * PITCH], cw0t[:, 2 * i + k, :],
                                            xt[:, 4 * j:4 * j + 4, :].rearrange("p k c -> p (k c)"),
                                            start=True, stop=True)
                    elif kind == "group":
                        wait(pe, "channel_stats", TOWER, args[0], b)
                        last = t.matmul(bank(g, 0)[:, 0:2], group_avg[:, :], ms[:, :], start=True, stop=True)
                    elif kind == "conv":
                        layer, r, cut = args
                        taps = 2 if layer == 5 else 3
                        parts = [a.rearrange("p (r c) -> p r c", c=PITCH) for a in hs[layer - 1]]
                        terms = [(tap, w, 0) for tap in range(taps) for w in (0, 1)]
                        terms += [(tap, 0, 1) for tap in range(taps)]
                        for k, c in enumerate(cut):
                            need = 2 * (r + c) - 2 + taps - 1
                            if need >= ROWS[layer - 1]:
                                wait(pe, "halo_done", TOWER, layer, b)
                                need = ROWS[layer - 1] - 1
                            unit = split_unit_of(layer - 1, need)
                            wait(pe, "hi_done", TOWER, SPLITS.index(unit) + 1, b)
                            for tap, w, x in terms:
                                if (tap, w, x) == (0, 0, 1):
                                    for engine, name in ((DVE_ENGINE, "lo_dve"), ("pool", "lo_pool")):
                                        wait(pe, name, TOWER, lows(engine, unit), b)
                                f = 2 * r + tap
                                last = t.matmul(bank(g, k)[:, 0:c * PITCH].rearrange("p (r c) -> p r c", c=PITCH),
                                                cwt[layer][:, w, tap, :], parts[x][:, f:f + 2 * c - 1:2, :],
                                                start=(tap, w, x) == terms[0], stop=(tap, w, x) == terms[-1])
                            r += c
                    elif kind == "embed":
                        if args[0] == 0:
                            wait(pe, "norm_done", TOWER, COUNTS["norm_done"][1], b)
                        tiles = range(4) if args[0] == 0 else range(4, TT)
                        for q, i in enumerate(tiles):
                            m = tile_rows(i)
                            last = t.matmul(bank(g, q // 2)[0:m, (q % 2) * D:(q % 2 + 1) * D],
                                            h5t[:, 128 * i:128 * i + m], pwt[:, :], start=True, stop=True)
                    else:
                        assert kind == "xtr"
                        if args[0] == 0:
                            wait(pe, "xn_ready", TOWER, 1, b)
                        for i in range(TT):
                            m = tile_rows(i)
                            last = t.transpose(bank(g, 0).bitcast(fp16)[:, 128 * i:128 * i + m],
                                               xn_parts[0:m, i, args[0], :], ident_h[0:m, 0:m])
                    last.then_inc(S["ps_full"], 1)

                with pe.Fori(0, PAIRS - 1) as pr:
                    for n, (kind, args, who) in enumerate(JOBS[PAIR]):
                        attention_job(PAIR, n, kind, args, b, pr)
                for n, (kind, args, who) in enumerate(JOBS[LAST_PAIR]):
                    attention_job(LAST_PAIR, n, kind, args, b)

                for n, (kind, args, who) in enumerate(JOBS[POST]):
                    g = slot_of(POST, n)
                    if (kind, args) != ("tr", (1,)):
                        slot_free(POST, n, b)
                    if (kind, args) == ("tr", (0,)):
                        slot_free(POST, n + 1, b)
                    if kind in ("xt", "gram", "taps", "chan", "group"):
                        samples_job(POST, n, b)
                        continue
                    if kind == "wo":
                        tiles = range(4) if args[0] == 0 else range(4, TT)
                        for q, i in enumerate(tiles):
                            m = tile_rows(i)
                            for a in range(PAIRS):
                                last = t.matmul(bank(g, q // 2)[0:m, (q % 2) * D:(q % 2 + 1) * D],
                                                zt[:, a, 128 * i:128 * i + m], wo[:, a, :], start=a == 0,
                                                stop=a == PAIRS - 1)
                    elif kind == "tr":
                        if args[0] == 0:
                            wait(pe, "xn_ready", POST, 1, b)
                        last = token_transposes(g, args[0])
                    elif kind == "gate":
                        wait(pe, "dve_freed", POST, freed(POST, DVE_ENGINE, job_index(POST, "tr", (0,))), b)
                        wait(pe, "act_freed", POST, freed(POST, ACT_ENGINE, job_index(POST, "tr", (1,))), b)
                        for i in range(TT):
                            m = tile_rows(i)
                            dst = bank(g, 0)[0:m, EXPERTS * i:EXPERTS * (i + 1)]
                            t.matmul(dst, xnt0[:, 128 * i:128 * i + m], gw0[:, :], start=True, stop=False)
                            last = t.matmul(dst, xnt1[0:D1, 128 * i:128 * i + m], gw1[:, :], start=False, stop=True)
                    else:
                        last = t.transpose(bank(g, 0)[:, 0:128], ident[:, :], ident[:, :])
                    last.then_inc(S["ps_full"], 1)

            wait(pe, "dve_step", MOE, 0)
            wait(pe, "act_freed", MOE, 0)
            wait(pe, "dve_freed", MOE, 0)
            pe.wait_ge(moe_consts, 3)
            choice = onehot[:, :, :].rearrange("p t e -> p (t e)")
            t.matmul(bank(0, 0)[:, 0:TILES * EXPERTS], before, choice, start=True, stop=True)
            t.matmul(bank(0, 1)[:, 0:TILES * EXPERTS], ones, choice, start=True, stop=True).then_inc(rank_full, 1)
            pe.wait_ge(slots_ready, 2)

            def make_xt(i, par):
                pe.wait_ge(xtile_loaded[par], i * 16 + 16)
                t.transpose(bank(0, par)[:, 0:128], xtile[par][:, 0:128], ident[:, :])
                t.transpose(bank(0, par)[0:D1, 128:256], xtile[par][:, 128:D], ident[:, :]).then_inc(xt_full, 1)

            def make_hidden(e, j, par, first=False):
                pe.wait_ge(xt_taken, j + 1)
                if not first:
                    pe.wait_ge(hidt_taken_dve, j - 1)
                    pe.wait_ge(hidt_taken_act, j - 1)
                for k in range(2):
                    f = slice(k * FF // 2, (k + 1) * FF // 2)
                    wa = w1a[:, bass.ds(e, 1), f].rearrange("p a f -> p (a f)")
                    wb = w1b[0:D1 + 1, bass.ds(e, 1), f].rearrange("p a f -> p (a f)")
                    t.matmul(bank(1 + par, k)[:, 0:FF // 2], xe0[par], wa, start=True, stop=False)
                    last = t.matmul(bank(1 + par, k)[:, 0:FF // 2], xe1[par][0:D1 + 1, :], wb, start=False,
                                    stop=True)
                last.then_inc(hid_full, 1)

            def make_hidt(j, par):
                pe.wait_ge(hid_taken, j + 1)
                for c in range(FF // 128):
                    last = t.transpose(slot(1 + par)[:, 128 * c:128 * c + 128], hid[par][:, 128 * c:128 * c + 128],
                                       ident[:, :])
                last.then_inc(hidt_full, 1)

            def make_y(e, j, par, first=False):
                pe.wait_ge(hidt_taken_dve, j + 1)
                pe.wait_ge(hidt_taken_act, j + 1)
                if not first:
                    pe.wait_ge(y_taken, j - 1)
                dst = bank(3, par)[:, 0:D]
                for c in range(FF // 128):
                    w = w2[:, bass.ds(e, 1), c, :].rearrange("p a d -> p (a d)")
                    t.matmul(dst, hidt[par][:, c, :], w, start=c == 0, stop=False)
                t.matmul(dst, ones[0:1, :], b2[0:1, bass.ds(e, 1), :].rearrange("p a d -> p (a d)"), start=False,
                         stop=True).then_inc(y_full, 1)

            def expert_of(j):
                return pe.value_load(tile_expert[0:1, bass.ds(j, 1)] if not isinstance(j, int)
                                     else tile_expert[0:1, j:j + 1], min_val=0, max_val=EXPERTS - 1)

            def two_tiles(i, first=False, last=False):
                j = i * 2
                experts = [expert_of(j), expert_of(j + 1)]
                make_hidden(experts[0], j, 0, first)
                make_hidden(experts[1], j + 1, 1, first)
                make_hidt(j, 0)
                make_xt(i + 1, 0)
                if not last:
                    make_xt(i + 1, 1)
                make_hidt(j + 1, 1)
                make_y(experts[0], j, 0, first)
                make_y(experts[1], j + 1, 1, first)

            pe.wait_ge(moe_consts, N_MOE_CONSTS)
            make_xt(0, 0)
            make_xt(0, 1)
            pe.wait_ge(experts_loaded, 16 * (3 * EXPERTS + 2))
            two_tiles(0, first=True)
            with pe.Fori(1, SLOT_TILES // 2 - 1) as i:
                two_tiles(i)
            two_tiles(SLOT_TILES // 2 - 1, last=True)
            last_tile = SLOT_TILES - 1
            e = expert_of(last_tile)
            make_hidden(e, last_tile, 0)
            make_hidt(last_tile, 0)
            make_y(e, last_tile, 0)


_INS = (["x"] + [f"L0_tok_{p}{l}" for l in range(CONV_LAYERS) for p in ("cw", "cb", "gw", "gb")]
        + ["L0_tok_pw", "L0_tok_pb"] + [f"L0_attn_{p}_{q}" for q in "QKVO" for p in ("W", "b")]
        + ["L0_ffn_gate_w", "L0_ffn_gate_b", "L0_ffn_w1", "L0_ffn_b1", "L0_ffn_w2", "L0_ffn_b2"])


def kernel(**inputs):
    import concourse.bacc as bacc
    from concourse.bass_utils import run_bass_kernel_spmd

    nc = bacc.Bacc("TRN2", target_bir_lowering=False, num_devices=1)
    arrays, args = {}, {}
    for name in _INS:
        a = np.ascontiguousarray(inputs[name])
        arrays[f"in_{name}"] = a
        args[name] = nc.dram_tensor(f"in_{name}", a.shape, mybir.dt.from_np(a.dtype), kind="ExternalInput").ap()
    out = nc.dram_tensor("out", (BATCH, SEQ, D), mybir.dt.float32, kind="ExternalOutput").ap()
    audio_tower(nc, args, out)
    r = run_bass_kernel_spmd(nc, [arrays], core_ids=[0])
    return r.results[0]["out"]
```
